# Optimizing a Trainium2 kernel written in Bass

```python
import numpy as np
import jax
import jax.numpy as jnp

def _softmax(x, axis=-1):
    return jax.nn.softmax(x, axis=axis)

def _gelu(x):
    return jax.nn.gelu(x, approximate=True)

def _silu(x):
    return jax.nn.silu(x)

def _sigmoid(x):
    return jax.nn.sigmoid(x)

def _layernorm(x, axis=-1, eps=1e-05):
    m = jnp.mean(x, axis=axis, keepdims=True)
    v = jnp.var(x, axis=axis, keepdims=True)
    return (x - m) / jnp.sqrt(v + eps)

def _scatter_add(tgt, idx, src, axis=0):
    return tgt.at[idx].add(src)

def _segment_sum(src, seg, n):
    return jax.ops.segment_sum(src, seg, n)
kernel_name = 'mk_flamingo_gated_d1_seqx_r4_717db2'

def setup_inputs(seed: int=0):
    np.random.seed(seed)
    _w = jnp.asarray

    def _rec_inputs():
        import jax
        import jax.numpy as jnp
        _rk = jax.random.key(seed)
        x = -0.0002928 + 1 * jax.random.normal(jax.random.fold_in(_rk, 1), (4, 1024, 256), jnp.float32)
        _lenS = 1024 - jax.random.randint(jax.random.fold_in(_rk, 7), (4,), 0, max(1, 1024 // 4) + 1, jnp.int32)
        _lenS2 = 64 - jax.random.randint(jax.random.fold_in(_rk, 8), (4,), 0, max(1, 64 // 4) + 1, jnp.int32)
        _ctx_1024P = jax.random.normal(jax.random.fold_in(_rk, 11), (4, 16, 256), jnp.float32)
        _ctx_1024c = jax.random.dirichlet(jax.random.fold_in(_rk, 511), 0.3 * jnp.ones((16,), jnp.float32), (4, 64))
        _ctx_1024t = jnp.einsum('bsk,bkd->bsd', _ctx_1024c, _ctx_1024P)
        _ctx_1024t = _ctx_1024t * jax.lax.rsqrt(jnp.mean(jnp.square(_ctx_1024t)) + 1e-12) * 0.953939
        ctx_1024 = -1.39393e-06 + 0.999914 * (_ctx_1024t + 0.3 * jax.random.normal(jax.random.fold_in(_rk, 611), (4, 64, 256), jnp.float32))
        _g = jax.random.normal(jax.random.fold_in(_rk, 9001), (2, 1), jnp.float32)
        _g = jnp.sign(_g) * jnp.maximum(jnp.abs(_g), 1.0) + (_g == 0) * 1.0
        g_xattn = _g[0]
        g_ffn = _g[1]
        return (x, ctx_1024, g_xattn, g_ffn)
    x, ctx_1024, g_xattn, g_ffn = _rec_inputs()

    def _L0_xattn_setup():
        import jax, jax.numpy as jnp
        import numpy as np
        B, L, D_MODEL = (2, 512, 256)
        N_HEADS, D_K = (16, 64)
        key = jax.random.key(seed)
        ks = jax.random.split(key, 8)
        std = float(np.sqrt(2.0 / (D_MODEL + D_K)))
        std_p = float(np.sqrt(1.0 / (N_HEADS * D_K)))
        return {'q': jax.random.normal(ks[0], (B, L, D_MODEL), jnp.float32), 'k': jax.random.normal(ks[1], (B, L, D_MODEL), jnp.float32), 'v': jax.random.normal(ks[2], (B, L, D_MODEL), jnp.float32), 'w_qs': jax.random.normal(ks[3], (N_HEADS, D_MODEL, D_K), jnp.float32) * std, 'w_ks': jax.random.normal(ks[4], (N_HEADS, D_MODEL, D_K), jnp.float32) * std, 'w_vs': jax.random.normal(ks[5], (N_HEADS, D_MODEL, D_K), jnp.float32) * std, 'w_proj': jax.random.normal(ks[6], (D_MODEL, N_HEADS * D_K), jnp.float32) * std_p, 'b_proj': jnp.zeros((D_MODEL,), jnp.float32)}
    _L0_xattn_all = _L0_xattn_setup()
    _L0_xattn_in = {k: v for k, v in _L0_xattn_all.items() if k in ('w_qs', 'w_ks', 'w_vs', 'w_proj', 'b_proj')}
    del _L0_xattn_all

    def _L0_ffn_setup():
        import jax, jax.numpy as jnp
        import numpy as np
        K = 2
        key = jax.random.key(seed)
        k1, k2, k3, k4 = jax.random.split(key, 4)
        B, S, D, E, F = (2, 256, 256, 8, 1024)
        x = jax.random.normal(k1, (B, S, D), dtype=jnp.float32)
        gate_w = jax.random.normal(k2, (E, D), dtype=jnp.float32) * (1.0 / np.sqrt(D))
        w1 = jax.random.normal(k3, (E, D, F), dtype=jnp.float32) * (1.0 / np.sqrt(D))
        w2 = jax.random.normal(k4, (E, F, D), dtype=jnp.float32) * (1.0 / np.sqrt(F))
        return {'x': x, 'gate_w': gate_w, 'w1': w1, 'w2': w2}
    _L0_ffn_all = _L0_ffn_setup()
    _L0_ffn_in = {k: v for k, v in _L0_ffn_all.items() if k in ('gate_w', 'w1', 'w2')}
    del _L0_ffn_all
    return {'x': x, 'ctx_1024': ctx_1024, 'g_xattn': g_xattn, 'g_ffn': g_ffn, 'L0_xattn_w_qs': _L0_xattn_in['w_qs'], 'L0_xattn_w_ks': _L0_xattn_in['w_ks'], 'L0_xattn_w_vs': _L0_xattn_in['w_vs'], 'L0_xattn_w_proj': _L0_xattn_in['w_proj'], 'L0_xattn_b_proj': _L0_xattn_in['b_proj'], 'L0_ffn_gate_w': _L0_ffn_in['gate_w'], 'L0_ffn_w1': _L0_ffn_in['w1'], 'L0_ffn_w2': _L0_ffn_in['w2']}

def reference(x, ctx_1024, g_xattn, g_ffn, L0_xattn_w_qs, L0_xattn_w_ks, L0_xattn_w_vs, L0_xattn_w_proj, L0_xattn_b_proj, L0_ffn_gate_w, L0_ffn_w1, L0_ffn_w2):
    import jax
    import jax.numpy as jnp

    def _L0_xattn_ref(q, k, v, w_qs, w_ks, w_vs, w_proj, b_proj):
        import jax, jax.numpy as jnp
        import numpy as np
        B, L, D_MODEL = (2, 512, 256)
        N_HEADS, D_K = (16, 64)
        qh = jnp.einsum('bld,hdk->hblk', q, w_qs)
        kh = jnp.einsum('bld,hdk->hblk', k, w_ks)
        vh = jnp.einsum('bld,hdk->hblk', v, w_vs)
        attn = jax.nn.softmax(jnp.einsum('hblk,hbmk->hblm', qh, kh), axis=-1)
        out = jnp.einsum('hblm,hbmk->hblk', attn, vh) * qh
        out = out.transpose(1, 2, 0, 3).reshape(q.shape[0], q.shape[1], -1)
        return out @ w_proj.T + b_proj

    def _L0_ffn_ref(x, gate_w, w1, w2):
        import jax, jax.numpy as jnp
        import numpy as np
        K = 2
        D = x.shape[-1]
        xt = x.reshape(-1, D)
        T = xt.shape[0]
        E = gate_w.shape[0]
        logits = jnp.einsum('td,ed->te', xt, gate_w)
        w_topk, sel = jax.lax.top_k(logits, K)
        w_topk = jax.nn.softmax(w_topk.astype(jnp.float32), axis=-1).astype(x.dtype)
        combine = jnp.zeros((T, E), dtype=x.dtype)
        combine = combine.at[jnp.arange(T)[:, None], sel].add(w_topk)
        h = jax.nn.silu(jnp.einsum('td,edf->tef', xt, w1))
        y = jnp.einsum('tef,efd->ted', h, w2)
        out = jnp.einsum('ted,te->td', y, combine)
        return out.reshape(x.shape)
    x = x + jnp.tanh(g_xattn[0]) * _L0_xattn_ref(_layernorm(x, axis=-1), ctx_1024, ctx_1024, L0_xattn_w_qs, L0_xattn_w_ks, L0_xattn_w_vs, L0_xattn_w_proj, L0_xattn_b_proj)
    x = x + jnp.tanh(g_ffn[0]) * _L0_ffn_ref(_layernorm(x, axis=-1), L0_ffn_gate_w, L0_ffn_w1, L0_ffn_w2)
    return x

_drawn_inputs = setup_inputs


def setup_inputs(seed=0):
    import zlib

    import numpy as np

    out = dict(_drawn_inputs(seed))
    spreads = {'L0_xattn_b_proj': (0.0, 0.1)}
    factors = {}
    for name, (base, spread) in spreads.items():
        noise = np.random.default_rng([zlib.crc32(name.encode()), seed]).standard_normal(out[name].shape)
        drawn = base * np.exp(spread * noise) if base else spread * noise
        out[name] = jnp.asarray(drawn.astype(out[name].dtype))
    for name, factor in factors.items():
        out[name] = (out[name] * factor).astype(out[name].dtype)
    return out
```

```python
from contextlib import ExitStack

import numpy as np
import concourse.bass as bass
from concourse import mybir

F32 = mybir.dt.float32
F16 = mybir.dt.float16
U32 = mybir.dt.uint32
I32 = mybir.dt.int32
ACT = mybir.ActivationFunctionType
ALU = mybir.AluOpType
AX = mybir.AxisListType

P = 128
B, L, D = 4, 1024, 256
M, H, DK = 64, 16, 64
E, F = 8, 1024
T = B * L
KD = D // P
NP = H // 2
TG = 4
G = TG * P
NG = T // G
GB = L // G
NS = NG * NP
FC = F // P
VW = DK + 1
EPS = 1e-5
WS = 64.0
REGION = T + P
ROW = D + 2
NB = (2 * T + E * (P - 1)) // P
HELD = 1
BIG = 3.0e38
WN = 2 * KD * F
LAST = 5


def after(eng, sem, count):
    if isinstance(count, int) and count <= 0:
        return
    eng.wait_ge(sem, count)


def build(nc, x, ctxt, g_xattn, g_ffn, wq, wk, wv, wproj, bproj, gate, w1, w2, out):
    dram = dict(
        x=x, ctxt=ctxt, g_xattn=g_xattn, g_ffn=g_ffn, wq=wq, wk=wk, wv=wv, wproj=wproj, bproj=bproj, gate=gate, w1=w1, w2=w2,
        out=out,
        records=nc.dram_tensor("records", (E * REGION + P, ROW), F32, kind="Internal").ap(),
        w_split=nc.dram_tensor("w_split", (E, P, 2, WN), F16, kind="Internal").ap(),
    )
    with ExitStack() as keep:
        def sb(name, shape, dt):
            return keep.enter_context(nc.sbuf_tensor(name, shape, dt))

        ident = sb("ident", [P, P], F32)
        table = sb("table", [1, 2 * NB], I32)
        loads_base = sb("loads_base", [1, 8], F32)
        weights = nc.alloc_sbuf_tensor_at("weights", [P, E, 2, WN], F16, offset=nc.sbuf_base)
        sb("weights_held", [P, HELD, 2, WN], F16)
        with ExitStack() as stage_ctx:
            attention(nc, stage_ctx, dram, ident, table, weights)
        with ExitStack() as stage_ctx:
            experts(nc, stage_ctx, dram, ident, table, loads_base, weights)


def attention(nc, ctx, dram, ident, table, weights):
    x_groups = dram["x"].rearrange("b l d -> (b l) d").rearrange("(g p t) d -> g p t d", p=P, t=TG)
    out_groups = dram["out"][0:T, :].rearrange("(g p t) d -> g p t d", p=P, t=TG)
    records, w_split = dram["records"], dram["w_split"]

    def sb(name, shape, dt):
        return ctx.enter_context(nc.sbuf_tensor(name, shape, dt))

    def psum(name, shape):
        return ctx.enter_context(nc.psum_tensor(name, shape, F32))

    def sem(name):
        return ctx.enter_context(nc.semaphore(name))

    wq_h, wq_l = (sb(f"wq_{s}", [P, KD, H * DK], F16) for s in "hl")
    wp_h, wp_l = (sb(f"wp_{s}", [P, NP, D], F16) for s in "hl")
    kb_h, kb_l = (sb(f"kb_{s}", [P, B, NP, 2 * M], F16) for s in "hl")
    vb_h, vb_l = (sb(f"vb_{s}", [P, B, NP, 2, VW], F16) for s in "hl")
    gate_t = sb("gate_t", [P, KD, E], F32)
    bias_rows = sb("bias_rows", [1, 2, D], F16)
    ones = sb("ones", [P, P], F16)
    before = sb("before", [P, P], F16)
    iota_e = sb("iota_e", [P, TG, E], F32)
    e_off = sb("e_off", [P, TG, E], F32)
    pad_off = sb("pad_off", [P, E], F32)
    tok_ids = sb("tok_ids", [P, TG], F32)
    minus_half = sb("minus_half", [P, TG], F32)
    pad_rec = sb("pad_rec", [P, ROW], F32)
    tanhs = sb("tanhs", [P, 2], F32)
    gains = sb("gains", [P, 2], F32)
    seen = sb("seen", [P, E], F32)
    seen_h = sb("seen_h", [P, E], F16)

    stage = sb("stage", [P, WN], F32)
    split = sb("split", [P, 2, WN], F16)
    ctx_sb = sb("ctx_sb", [P, 2, D], F32)
    gate_sb = sb("gate_sb", [E, D], F32)
    bias_sb = sb("bias_sb", [1, D], F32)

    xin = sb("xin", [P, 2, TG, D], F32)
    xres = sb("xres", [P, 2, TG, D], F32)
    stats = sb("stats", [P, 2, TG, 6], F32)
    mv = sb("mv", [P, 2, TG, 2], F32)
    vare = sb("vare", [P, 2, TG], F32)
    rstd = sb("rstd", [P, 2, TG], F32)
    xn = sb("xn", [P, TG, D], F32)
    xt_h, xt_l = (sb(f"xt_{s}", [P, 2, KD, G], F16) for s in "hl")
    q32 = sb("q32", [P, NP, G], F32)
    q_h, q_l = (sb(f"q_{s}", [P, 2, G], F16) for s in "hl")
    smax = sb("smax", [P, 2, TG, 2], F32)
    ssub = sb("ssub", [P, 2, TG, 2, M], F32)
    ex = sb("ex", [P, 2, TG, 2 * M], F32)
    e_h, e_l = (sb(f"e_{s}", [P, 2, G], F16) for s in "hl")
    rinv = sb("rinv", [P, 2, 2, TG], F32)
    on = sb("on", [P, 2, TG, 2 * DK], F32)
    r32 = sb("r32", [P, 2, G], F32)
    r_h, r_l = (sb(f"r_{s}", [P, 2, G], F16) for s in "hl")
    rec = sb("rec", [P, 2, 2, TG, ROW], F32)
    x2t = sb("x2t", [P, KD, G], F32)
    lg, lg2, cand, pos = (sb(n, [P, TG, E], F32) for n in ("lg", "lg2", "cand", "pos"))
    mask = sb("mask", [P, 2, TG, E], F32)
    mboth = sb("mboth", [P, TG, E], F16)
    mtiles = sb("mtiles", [P, E], F32)
    top = sb("top", [P, 2, TG], F32)
    choice = sb("choice", [P, 2, TG], F32)
    delta, edelta, wsum, wfirst = (sb(n, [P, TG], F32) for n in ("delta", "edelta", "wsum", "wfirst"))
    slot = sb("slot", [P, 2, 2, TG], U32)
    spare_slot = sb("spare_slot", [P, 1], U32)
    pad_slot = sb("pad_slot", [P, E], U32)
    wait_mark = sb("wait_mark", [P, 2], F32)

    steps_128 = sb("steps_128", [1, E, T // P], F32)
    under = sb("under", [1, E, T // P], F32)
    upto = sb("upto", [1, E, E], F32)
    cum = sb("cum", [1, E, E], F32)
    block_no = sb("block_no", [1, NB, E], F32)
    past = sb("past", [1, NB, E], F32)
    count1, blocks, ends = (sb(n, [1, E], F32) for n in ("count1", "blocks", "ends"))
    blk_e, blk_s = (sb(n, [1, NB], F32) for n in ("blk_e", "blk_s"))

    wq_sb = q32[:, 0:4, :].rearrange("p a g -> p (a g)").rearrange("p (k n) -> p k n", k=KD)
    wp_sb = q32[:, 4:8, :].rearrange("p a g -> p (a g)").rearrange("p (c n) -> p c n", c=KD)
    ctx_t = x2t[:, :, :].rearrange("p k (b c m) -> p k b c m", b=B, c=2)
    wk_sb = stage[:, 0:WN // 2].rearrange("p (k n) -> p k n", k=KD)
    wv_sb = stage[:, WN // 2:WN].rearrange("p (k n) -> p k n", k=KD)

    q_ps = psum("q_ps", [P, G])
    s_ps = psum("s_ps", [P, TG, 2, M])
    pt_ps = psum("pt_ps", [P, G])
    av_ps = psum("av_ps", [P, 2, G])
    ot_ps = psum("ot_ps", [P, G])
    pj_ps = psum("pj_ps", [P, TG, D])
    kv_banks = (pt_ps, ot_ps)
    av_heads = av_ps[:, :, 0:TG * VW].rearrange("p c (h w) -> p c h w", h=TG)

    gain_in, gate_in, bias_in, ctx_in, wk_in, wv_in, wq_in, wp_in, stage_in = (sem(n) for n in (
        "gain_in", "gate_in", "bias_in", "ctx_in", "wk_in", "wv_in", "wq_in", "wp_in", "stage_in"))
    x_in = [sem(f"x_in{i}") for i in range(2)]
    xres_in = [sem(f"xres_in{i}") for i in range(2)]
    records_in = [sem(f"records_in{i}") for i in range(2)]
    pads_in, x1_stored, split_stored = sem("pads_in"), sem("x1_stored"), sem("split_stored")
    base_set, consts_set, zeroed, setup_ops, tanh_done = (sem(n) for n in ("base_set", "consts_set", "zeroed", "setup_ops", "tanh_done"))
    ctx_tp, ctx_copied, gate_tp, gate_copied, wp_tp, wp_hi, wp_lo, wq_hi, wq_lo, bias_hi = (sem(n) for n in (
        "ctx_tp", "ctx_copied", "gate_tp", "gate_copied", "wp_tp", "wp_hi", "wp_lo", "wq_hi", "wq_lo", "bias_hi"))
    k_mm, k_hi, k_lo, v_mm, v_hi, v_lo = (sem(n) for n in ("k_mm", "k_hi", "k_lo", "v_mm", "v_hi", "v_lo"))
    ln1_ops, ln1_rstd, xn_done, xt_tp, xt_hi, xt_lo = (sem(n) for n in ("ln1_ops", "ln1_rstd", "xn_done", "xt_tp", "xt_hi", "xt_lo"))
    q_mm, q_sb, q_hi, q_lo, s_mm, s_max, s_sub, e_x, pt_mm, e_hi, e_lo = (sem(n) for n in (
        "q_mm", "q_sb", "q_hi", "q_lo", "s_mm", "s_max", "s_sub", "e_x", "pt_mm", "e_hi", "e_lo"))
    av_mm, o_inv, o_nrm, ot_mm, r_mul, r_hi, r_lo, pj_mm = (sem(n) for n in (
        "av_mm", "o_inv", "o_nrm", "ot_mm", "r_mul", "r_hi", "r_lo", "pj_mm"))
    x1_done, ln2_ops, ln2_rstd, ln2_done, rec_done, x2_tp, x2_copied = (sem(n) for n in (
        "x1_done", "ln2_ops", "ln2_rstd", "ln2_done", "rec_done", "x2_tp", "x2_copied"))
    lg_mm, lg_read, top_done, ed_done, m_done, pos_mm, pos_read, slots_done, route_ops = (sem(n) for n in (
        "lg_mm", "lg_read", "top_done", "ed_done", "m_done", "pos_mm", "pos_read", "slots_done", "route_ops"))
    split_hi, split_lo, count_mm, pad_slots, table_ops = (sem(n) for n in (
        "split_hi", "split_lo", "count_mm", "pad_slots", "table_ops"))

    CONSTS = 13
    ROUTE = 17

    def pair_no(g, p):
        return g * NP + p

    def known(g, least):
        return not isinstance(g, int) or g >= least

    def has_next(g):
        return not isinstance(g, int) or g < NG - 1

    def at(ap, i, pattern, **sizes):
        return ap[i] if isinstance(i, int) else ap[bass.ds(i, 1)].rearrange(pattern, **sizes)

    block = ctx.enter_context(nc.Block())

    @block.sync
    def _(sp):
        sp.dma_start(xin[:, 0], x_groups[0]).then_inc(x_in[0], 16)
        sp.dma_start(ctx_sb[:, :, :], dram["ctxt"].rearrange("(c b) m d -> (b m) c d", b=2)).then_inc(ctx_in, 16)
        for w, dst, done in ((dram["wk"], wk_sb, wk_in), (dram["wv"], wv_sb, wv_in)):
            for k in range(KD):
                sp.dma_start(dst[:, k].rearrange("p (h j) -> p h j", h=H),
                             w.rearrange("h (k p) j -> k p h j", p=P)[k]).then_inc(done, 16)
        sp.dma_start(xin[:, 1], x_groups[1]).then_inc(x_in[1], 16)

        def load_expert(g):
            if isinstance(g, int) and g == 0:
                sp.wait_ge(k_mm, NP)
                sp.wait_ge(v_mm, 2 * B)
            after(sp, split_lo, 2 * g)
            sp.dma_start(stage[:, 0:WN // 2].rearrange("p (k f) -> p k f", k=KD),
                         at(dram["w1"], g, "o d f -> (o d) f").rearrange("(k p) f -> p k f", p=P)).then_inc(stage_in, 16)
            sp.dma_start(stage[:, WN // 2:WN].rearrange("p (c d) -> p c d", c=FC),
                         at(dram["w2"], g, "o f d -> (o f) d").rearrange("(c p) d -> p c d", p=P)).then_inc(stage_in, 16)

        def load_residual(g, par):
            if known(g, 2):
                sp.wait_ge(x1_stored, 16 * (g - 1))
                sp.wait_ge(rec_done, g - 1)
            sp.dma_start(xres[:, par], at(x_groups, g, "o p t d -> (o p) t d")).then_inc(xres_in[par], 16)

        def load_x(g, par):
            sp.wait_ge(xn_done, g - 1)
            sp.dma_start(xin[:, par], at(x_groups, g, "o p t d -> (o p) t d")).then_inc(x_in[par], 16)

        def store_x1(g, par):
            sp.wait_ge(x1_done, g + 1)
            sp.dma_start(at(out_groups, g, "o p t d -> (o p) t d"), xres[:, par]).then_inc(x1_stored, 16)

        def store_split(e):
            sp.wait_ge(split_hi, 2 * e + 2)
            sp.wait_ge(split_lo, 2 * e + 2)
            sp.dma_start(at(w_split, e, "o p s n -> (o p) s n"), split[:, :, :]).then_inc(split_stored, 16)

        def group(g, par):
            load_residual(g, par)
            load_expert(g)
            if not isinstance(g, int) or g + 2 < NG:
                load_x(g + 2, par)
            if known(g, 1):
                store_x1(g - 1, 1 - par)
            if known(g, HELD):
                store_split(g)

        for k in range(GB):
            group(k, k)
        with sp.Fori(1, B - 1) as b:
            for k in range(GB):
                group(b * GB + k, k)
        for k in range(GB):
            group(NG - GB + k, k)
        store_x1(NG - 1, 1)
        sp.wait_ge(x1_stored, 16 * NG)
        sp.wait_ge(split_stored, 16 * (NG - HELD))

    @block.tensor
    def _(pe):
        pe.wait_ge(consts_set, CONSTS)

        def x_transpose(g, k):
            pe.wait_ge(xn_done, g + 1)
            for t in range(TG):
                last = nc.tensor.transpose(q_ps[:, t * P:(t + 1) * P], xn[:, t, k * P:(k + 1) * P], ident[:, :])
            last.then_inc(xt_tp, 1)

        pe.wait_ge(ctx_in, 16)
        for k in range(KD):
            for c in range(2):
                o = (k * 2 + c) * P
                last = nc.tensor.transpose(s_ps[:].rearrange("p t h m -> p (t h m)")[:, o:o + P],
                                           ctx_sb[:, c, k * P:(k + 1) * P], ident[:, :])
        last.then_inc(ctx_tp, 1)
        pe.wait_ge(gate_in, 16)
        for k in range(KD):
            last = nc.tensor.transpose(ot_ps[:, k * E:(k + 1) * E], gate_sb[:, k * P:(k + 1) * P], ident[0:E, 0:E])
        last.then_inc(gate_tp, 1)
        for k in range(KD):
            after(pe, xt_lo, k)
            x_transpose(0, k)
        pe.wait_ge(wp_in, 16)
        for half in range(2):
            after(pe, wp_lo, half)
            for j in range(TG):
                for c in range(KD):
                    o = (half * TG + j) * P
                    last = nc.tensor.transpose(pj_ps[:, j, c * P:(c + 1) * P], wp_sb[:, c, o:o + P], ident[:, :])
            last.then_inc(wp_tp, 1)
        pe.wait_ge(ctx_copied, 2)
        pe.wait_ge(gate_copied, 1)
        pe.wait_ge(wk_in, 16 * KD)
        for p in range(NP):
            after(pe, k_lo, p - 1)
            for k in range(KD):
                last = nc.tensor.matmul(kv_banks[p % 2][:, 0:B * M], wk_sb[:, k, p * P:(p + 1) * P], ctx_t[:, k, :, 0, :],
                                        start=(k == 0), stop=(k == KD - 1))
            last.then_inc(k_mm, 1)
        pe.wait_ge(wv_in, 16 * KD)
        for b in range(B):
            for half in range(2):
                after(pe, v_lo, 2 * b + half - 1)
                for k in range(KD):
                    last = nc.tensor.matmul(av_ps[:, half, :], ctx_t[:, k, b, :, :].rearrange("p c m -> p (c m)"),
                                            wv_sb[:, k, half * G:(half + 1) * G], start=(k == 0), stop=(k == KD - 1))
                last.then_inc(v_mm, 1)

        def q_bank_free(g, p):
            if p == 0 and known(g, 2):
                pe.wait_ge(x2_copied, 2 * g - 3)
            if p == 1 and known(g, 2):
                pe.wait_ge(x2_copied, 2 * g - 2)
            if p == 2 and known(g, 2):
                pe.wait_ge(lg_read, g - 1)
            if p == 4 and known(g, 2):
                pe.wait_ge(pos_read, g - 1)
            if p in (5, 6) and has_next(g):
                pe.wait_ge(xt_lo, 2 * g + p - 2)

        def project_q(g, p, par):
            after(pe, q_hi, pair_no(g, p))
            q_bank_free(g, p)
            if p == 0:
                pe.wait_ge(xt_lo, 2 * g + 2)
            for i, (wt, xt) in enumerate(((wq_h, xt_h), (wq_h, xt_l), (wq_l, xt_h))):
                for k in range(KD):
                    last = nc.tensor.matmul(q_ps[:, :], wt[:, k, p * P:(p + 1) * P], xt[:, par, k, :],
                                            start=(i == 0 and k == 0), stop=(i == 2 and k == KD - 1))
            last.then_inc(q_mm, 1)

        def scores(b, n, p):
            pe.wait_ge(q_lo, n + 1)
            after(pe, s_sub, n)
            for t in range(TG):
                for i, (qt, kt) in enumerate(((q_h, kb_h), (q_h, kb_l), (q_l, kb_h))):
                    last = nc.tensor.matmul(s_ps[:, t].rearrange("p h m -> p (h m)"), qt[:, p % 2, t * P:(t + 1) * P],
                                            kt[:, b, p, :] if isinstance(b, int)
                                            else kt[:, bass.ds(b, 1), p, :].rearrange("p o m -> p (o m)"),
                                            start=(i == 0), stop=(i == 2))
            last.then_inc(s_mm, 1)

        def transpose_probs(n, p):
            pe.wait_ge(e_x, n + 1)
            after(pe, e_lo, n)
            for t in range(TG):
                last = nc.tensor.transpose(pt_ps[:, t * P:(t + 1) * P], ex[:, p % 2, t, :], ident[:, :])
            last.then_inc(pt_mm, 1)

        def probs_v(b, n, p):
            pe.wait_ge(e_lo, n + 1)
            after(pe, o_nrm, n)
            for t in range(TG):
                o = (t % 2) * 2 * VW
                for i, (et, vt) in enumerate(((e_h, vb_h), (e_h, vb_l), (e_l, vb_h))):
                    last = nc.tensor.matmul(av_ps[:, t // 2, o:o + 2 * VW], et[:, p % 2, t * P:(t + 1) * P],
                                            vt[:, b, p].rearrange("p h w -> p (h w)") if isinstance(b, int)
                                            else vt[:, bass.ds(b, 1), p].rearrange("p o h w -> p (o h w)"),
                                            start=(i == 0), stop=(i == 2))
            last.then_inc(av_mm, 1)

        def transpose_out(n, p):
            pe.wait_ge(o_nrm, n + 1)
            after(pe, r_mul, n)
            for t in range(TG):
                last = nc.tensor.transpose(ot_ps[:, t * P:(t + 1) * P], on[:, p % 2, t, :], ident[:, :])
            last.then_inc(ot_mm, 1)

        def project_out(g, n, p):
            pe.wait_ge(r_lo, n + 1)
            if p == 0:
                after(pe, x1_done, g)
            for t in range(TG):
                for i, (rt, wt) in enumerate(((r_h, wp_h), (r_h, wp_l), (r_l, wp_h))):
                    last = nc.tensor.matmul(pj_ps[:, t, :], rt[:, p % 2, t * P:(t + 1) * P], wt[:, p, :],
                                            start=(p == 0 and i == 0 and t % 2 == 0), stop=False, skip_group_check=True)
                if p == NP - 1:
                    for i in range(2):
                        last = nc.tensor.matmul(pj_ps[:, t, :], ones[0:1, :], bias_rows[0:1, i, :],
                                                start=False, stop=(i == 1), skip_group_check=True)
            last.then_inc(pj_mm, 1)

        def x2_transpose(g, par, k):
            pe.wait_ge(ln2_done, g + 1)
            for t in range(TG):
                last = nc.tensor.transpose(q_ps[:, t * P:(t + 1) * P], rec[:, par, 0, t, k * P:(k + 1) * P], ident[:, :])
            last.then_inc(x2_tp, 1)

        def logits(g):
            pe.wait_ge(x2_copied, 2 * g + 2)
            for t in range(TG):
                for k in range(KD):
                    last = nc.tensor.matmul(q_ps[:, t * E:(t + 1) * E], x2t[:, k, t * P:(t + 1) * P], gate_t[:, k, :],
                                            start=(k == 0), stop=(k == KD - 1))
            last.then_inc(lg_mm, 1)

        def positions(g):
            pe.wait_ge(m_done, g + 1)
            for t in range(TG):
                o = q_ps[:, t * E:(t + 1) * E]
                nc.tensor.matmul(o, ones[:, :], seen_h[:, :], start=True, stop=False)
                for v in range(t):
                    nc.tensor.matmul(o, ones[:, :], mboth[:, v, :], start=False, stop=False)
                last = nc.tensor.matmul(o, before[:, :], mboth[:, t, :], start=False, stop=True)
            last.then_inc(pos_mm, 1)

        def small_job(g, k, p):
            n = pair_no(g, p)
            if p in (0, 1, 3) and known(g, 2) or p in (4, 5) and has_next(g) or p == 7 and known(g, 1):
                pe.wait_ge(q_hi, n + 1)
            if p == 0 and known(g, 2):
                x2_transpose(g - 2, k, 1)
            if p == 1 and known(g, 2):
                logits(g - 2)
            if p == 3 and known(g, 2):
                positions(g - 2)
            if p in (4, 5) and has_next(g):
                x_transpose(g + 1, p - 4)
            if p == 7 and known(g, 1):
                x2_transpose(g - 1, 1 - k, 0)

        def step(b, g, k, p, pairs_back=LAST):
            n = pair_no(g, p)

            def back(lag):
                if p >= lag:
                    return b, g, p - lag
                return (b if k else b - 1), g - 1, p - lag + NP
            project_q(g, p, k)
            if pairs_back >= 1:
                scores(back(1)[0], n - 1, back(1)[2])
            if pairs_back >= 2:
                transpose_probs(n - 2, back(2)[2])
            small_job(g, k, p)
            if pairs_back >= 3:
                probs_v(back(3)[0], n - 3, back(3)[2])
            if pairs_back >= 4:
                transpose_out(n - 4, back(4)[2])
            if pairs_back >= 5:
                project_out(back(5)[1], n - 5, back(5)[2])

        pe.wait_ge(wq_lo, 1)
        pe.wait_ge(k_lo, NP)
        pe.wait_ge(v_lo, 2 * B)
        pe.wait_ge(wp_lo, 2)
        pe.wait_ge(bias_hi, 2)
        for k in range(GB):
            for p in range(NP):
                step(0, k, k, p, pairs_back=min(LAST, k * NP + p))
        with pe.Fori(1, B - 1) as b:
            for k in range(GB):
                for p in range(NP):
                    step(b, b * GB + k, k, p)
        for k in range(GB):
            for p in range(NP):
                step(B - 1, NG - GB + k, k, p)
        for p in range(LAST):
            n = NS + p
            if p < 1:
                scores(B - 1, n - 1, NP + p - 1)
            if p < 2:
                transpose_probs(n - 2, NP + p - 2)
            if p == 0:
                pe.wait_ge(q_hi, NS)
                pe.wait_ge(x2_copied, 2 * NG - 3)
                x2_transpose(NG - 2, 0, 1)
            if p == 1:
                logits(NG - 2)
            if p == 3:
                pe.wait_ge(lg_read, NG - 1)
                positions(NG - 2)
            if p < 3:
                probs_v(B - 1, n - 3, NP + p - 3)
            if p < 4:
                transpose_out(n - 4, NP + p - 4)
            project_out(NG - 1, n - 5, NP + p - 5)
        pe.wait_ge(pos_read, NG - 1)
        for k in range(KD):
            after(pe, x2_copied, 2 * NG - 2 + k)
            x2_transpose(NG - 1, 1, k)
        logits(NG - 1)
        pe.wait_ge(lg_read, NG)
        positions(NG - 1)
        pe.wait_ge(pos_read, NG)
        pe.wait_ge(slots_done, NG)
        nc.tensor.matmul(q_ps[:, 0:E], ones[:, :], seen_h[:, :], start=True, stop=True).then_inc(count_mm, 1)

    @block.scalar
    def _(act):
        act.dma_start(tanhs[:, 0:1], dram["g_xattn"].partition_broadcast(P)).then_inc(gain_in, 16)
        act.dma_start(tanhs[:, 1:2], dram["g_ffn"].partition_broadcast(P)).then_inc(gain_in, 16)
        for k in range(KD):
            act.dma_start(wq_sb[:, k].rearrange("p (h j) -> p h j", h=H),
                          dram["wq"].rearrange("h (k p) j -> k p h j", p=P)[k]).then_inc(wq_in, 16)
        act.dma_start(gate_sb[:, :], dram["gate"]).then_inc(gate_in, 16)
        act.dma_start(bias_sb[:, :], dram["bproj"].rearrange("(o d) -> o d", o=1)).then_inc(bias_in, 16)
        act.dma_start(wp_sb, dram["wproj"].rearrange("(c p) n -> p c n", p=P)).then_inc(wp_in, 16)
        act.wait_ge(gain_in, 32)
        nc.scalar.activation(tanhs[:, :], tanhs[:, :], ACT.Tanh).then_inc(tanh_done, 1)
        act.wait_ge(bias_in, 16)
        nc.scalar.mul(bias_rows[:, 0, :], bias_sb[:, :], WS).then_inc(bias_hi, 1)

        def split_x(g, par, k):
            act.wait_ge(xt_tp, 2 * g + k + 1)
            if known(g, 3) or isinstance(g, int) and g == 2:
                act.wait_ge(q_mm, pair_no(g - 2, NP))
            nc.scalar.copy(xt_h[:, par, k, :], q_ps[:, :]).then_inc(xt_hi, 1)

        act.wait_ge(ctx_tp, 1)
        for c in range(2):
            nc.scalar.copy(ctx_t[:, :, :, c, :], s_ps[:].rearrange("p t h m -> p (t h m)").rearrange(
                "p (k b m) -> p k b m", k=KD, b=B)).then_inc(ctx_copied, 1)
        act.wait_ge(gate_tp, 1)
        nc.scalar.copy(gate_t[:, :, :], ot_ps[:, 0:KD * E].rearrange("p (k e) -> p k e", k=KD)).then_inc(gate_copied, 1)
        for k in range(KD):
            split_x(0, 0, k)
        act.wait_ge(wq_in, 16 * KD)
        nc.scalar.mul(wq_h[:, :, :], wq_sb, WS).then_inc(wq_hi, 1)
        for half in range(2):
            act.wait_ge(wp_tp, half + 1)
            nc.scalar.mul(wp_h[:, half * TG:half * TG + TG, :], pj_ps[:, :, :], WS).then_inc(wp_hi, 1)
        act.wait_ge(zeroed, 4)
        for p in range(NP):
            act.wait_ge(k_mm, p + 1)
            for h in range(2):
                r = slice(h * M, (h + 1) * M)
                last = nc.scalar.copy(kb_h[r, :, p, r], kv_banks[p % 2][r, 0:B * M].rearrange("p (b m) -> p b m", b=B))
            last.then_inc(k_hi, 1)
        for i in range(2 * B):
            b, half = i // 2, i % 2
            act.wait_ge(v_mm, i + 1)
            for h in range(2):
                r = slice(h * M, (h + 1) * M)
                last = nc.scalar.copy(vb_h[r, b, half * TG:half * TG + TG, h, 0:DK],
                                      av_ps[r, half, :].rearrange("p (q h j) -> p q h j", q=TG, h=2)[:, :, h, :])
            last.then_inc(v_hi, 1)
        act.wait_ge(wq_lo, 1)
        act.wait_ge(wp_lo, 2)

        def copy_q(n, p):
            act.wait_ge(q_mm, n + 1)
            after(act, r_mul, n - NP + 1)
            nc.scalar.mul(q32[:, p, :], q_ps[:, :], 1.0 / WS).then_inc(q_sb, 1)
            after(act, s_mm, n - 1)
            nc.scalar.mul(q_h[:, p % 2, :], q_ps[:, :], 1.0 / WS).then_inc(q_hi, 1)

        def probs_hi(n, p):
            act.wait_ge(pt_mm, n + 1)
            after(act, av_mm, n - 1)
            nc.scalar.copy(e_h[:, p % 2, :], pt_ps[:, :]).then_inc(e_hi, 1)

        def exps(n, p):
            act.wait_ge(s_sub, n + 1)
            after(act, pt_mm, n - 1)
            nc.scalar.activation(ex[:, p % 2].rearrange("p t m -> p (t m)"),
                                 ssub[:, p % 2].rearrange("p t h m -> p (t h m)"), ACT.Exp).then_inc(e_x, 1)

        def product_hi(n, p):
            act.wait_ge(r_mul, n + 1)
            after(act, pj_mm, n - 1)
            nc.scalar.copy(r_h[:, p % 2, :], r32[:, p % 2, :]).then_inc(r_hi, 1)

        def x2_copy(g, k):
            act.wait_ge(x2_tp, 2 * g + k + 1)
            if k == 0:
                after(act, lg_mm, g)
            nc.scalar.copy(x2t[:, k, :], q_ps[:, :]).then_inc(x2_copied, 1)

        def exp_delta(g):
            act.wait_ge(top_done, g + 1)
            nc.scalar.activation(edelta[:, :], delta[:, :], ACT.Exp).then_inc(ed_done, 1)

        def expert_hi(e, part):
            act.wait_ge(stage_in, 32 * e + 32)
            if known(e, HELD + 1):
                act.wait_ge(split_stored, 16 * (e - HELD))
            c = slice(part * WN // 2, (part + 1) * WN // 2)
            dst = weights[:, e] if isinstance(e, int) and e < HELD else split
            nc.scalar.mul(dst[:, 0, c], stage[:, c], WS).then_inc(split_hi, 1)

        def step(g, k, p, pairs_back=LAST):
            n = pair_no(g, p)
            copy_q(n, p)
            if pairs_back >= 2:
                probs_hi(n - 2, (p - 2) % NP)
            if p == 0 and known(g, 2):
                x2_copy(g - 2, 1)
            if p in (4, 5) and has_next(g):
                split_x(g + 1, 1 - k, p - 4)
            if p == 7 and known(g, 1):
                x2_copy(g - 1, 0)
            if pairs_back >= 1:
                exps(n - 1, (p - 1) % NP)
            if pairs_back >= 4:
                product_hi(n - 4, (p - 4) % NP)
            if p == 2 and known(g, 2):
                exp_delta(g - 2)
            if p in (3, 6):
                expert_hi(g, p // 6)

        for k in range(GB):
            for p in range(NP):
                step(k, k, p, pairs_back=min(LAST, k * NP + p))
        with act.Fori(1, B - 1) as b:
            for k in range(GB):
                for p in range(NP):
                    step(b * GB + k, k, p)
        for k in range(GB):
            for p in range(NP):
                step(NG - GB + k, k, p)
        for p in range(LAST):
            n = NS + p
            if p < 2:
                probs_hi(n - 2, NP + p - 2)
            if p == 0:
                x2_copy(NG - 2, 1)
            if p < 1:
                exps(n - 1, NP + p - 1)
            if p < 4:
                product_hi(n - 4, NP + p - 4)
            if p == 2:
                exp_delta(NG - 2)
        for k in range(KD):
            x2_copy(NG - 1, k)
        exp_delta(NG - 1)

    @block.vector
    def _(dve):
        for i, t in enumerate((kb_h, kb_l)):
            nc.vector.memset(t[:].rearrange("p b n m -> p (b n m)").bitcast(U32), 0).then_inc(zeroed, 1)
        nc.vector.memset(seen[:, :], 0.0)
        nc.vector.memset(seen_h[:, :], 0.0)

        def ln1(g, par):
            dve.wait_ge(x_in[par], 16 * (g // 2) + 16 if isinstance(g, int) else g)
            for t in range(TG):
                last = nc.vector.bn_stats(stats[:, 0, t, :], xin[:, par, t, :])
            last.then_inc(ln1_ops, 1)

        def ln1_moments(g):
            dve.wait_ge(ln1_ops, 3 * g + 1)
            after(dve, xn_done, g)
            nc.vector.memset(vare[:, 0, :], EPS)
            for t in range(TG):
                last = nc.vector.bn_aggr(mv[:, 0, t, :], stats[:, 0, t, :])
            last.then_inc(ln1_ops, 1)
            dve.wait_ge(ln1_ops, 3 * g + 2)
            nc.vector.tensor_tensor(vare[:, 0, :], vare[:, 0, :], mv[:, 0, :, 1], ALU.add).then_inc(ln1_ops, 1)

        def ln1_apply(g, par):
            dve.wait_ge(ln1_rstd, g + 1)
            after(dve, xt_tp, 2 * g)
            for t in range(TG):
                last = nc.vector.tensor_scalar(xn[:, t, :], xin[:, par, t, :], mv[:, 0, t, 0:1], rstd[:, 0, t:t + 1],
                                               ALU.subtract, ALU.mult)
            last.then_inc(xn_done, 1)

        def split_x(g, par, k):
            dve.wait_ge(xt_hi, 2 * g + k + 1)
            nc.vector.tensor_tensor(xt_l[:, par, k, :], q_ps[:, :], xt_h[:, par, k, :], ALU.subtract).then_inc(xt_lo, 1)

        ln1(0, 0)
        ln1_moments(0)
        dve.wait_ge(tanh_done, 1)
        nc.vector.tensor_scalar(gains[:, :], tanhs[:, :], 1.0 / WS, None, ALU.mult).then_inc(setup_ops, 1)
        dve.wait_ge(bias_hi, 1)
        nc.vector.scalar_tensor_tensor(bias_rows[:, 1, :], bias_sb[:, :], WS, bias_rows[:, 0, :],
                                       ALU.mult, ALU.subtract).then_inc(bias_hi, 1)
        ln1_apply(0, 0)
        for k in range(KD):
            split_x(0, 0, k)
        dve.wait_ge(wq_hi, 1)
        nc.vector.scalar_tensor_tensor(wq_l[:, :, :], wq_sb, WS, wq_h[:, :, :], ALU.mult, ALU.subtract).then_inc(wq_lo, 1)
        for half in range(2):
            dve.wait_ge(wp_hi, half + 1)
            o = slice(half * TG, half * TG + TG)
            nc.vector.scalar_tensor_tensor(wp_l[:, o, :], pj_ps[:, :, :], WS, wp_h[:, o, :], ALU.mult, ALU.subtract).then_inc(wp_lo, 1)
        for p in range(NP):
            dve.wait_ge(k_hi, p + 1)
            for h in range(2):
                r = slice(h * M, (h + 1) * M)
                last = nc.vector.tensor_tensor(kb_l[r, :, p, r], kv_banks[p % 2][r, 0:B * M].rearrange("p (b m) -> p b m", b=B),
                                               kb_h[r, :, p, r], ALU.subtract)
            last.then_inc(k_lo, 1)
        dve.wait_ge(zeroed, 4)
        for h in range(2):
            nc.vector.memset(vb_h[h * M:(h + 1) * M, :, :, h, DK:VW], 1.0)
        for i in range(2 * B):
            b, half = i // 2, i % 2
            dve.wait_ge(v_hi, i + 1)
            for h in range(2):
                r = slice(h * M, (h + 1) * M)
                dst = vb_l[r, b, half * TG:half * TG + TG, h, 0:DK]
                last = nc.vector.tensor_tensor(dst, av_ps[r, half, :].rearrange("p (q h j) -> p q h j", q=TG, h=2)[:, :, h, :],
                                               vb_h[r, b, half * TG:half * TG + TG, h, 0:DK], ALU.subtract)
            last.then_inc(v_lo, 1)

        def score_max(n, p):
            dve.wait_ge(s_mm, n + 1)
            nc.vector.tensor_reduce(smax[:, p % 2], s_ps[:, :, :, :], AX.X, ALU.max).then_inc(s_max, 1)

        def score_sub(n, p):
            dve.wait_ge(s_max, n + 1)
            after(dve, e_x, n - 1)
            nc.vector.tensor_tensor(ssub[:, p % 2], s_ps[:, :, :, :],
                                    smax[:, p % 2].unsqueeze(3).broadcast_to([P, TG, 2, M]), ALU.subtract).then_inc(s_sub, 1)

        def probs_lo(n, p):
            dve.wait_ge(e_hi, n + 1)
            nc.vector.tensor_tensor(e_l[:, p % 2, :], pt_ps[:, :], e_h[:, p % 2, :], ALU.subtract).then_inc(e_lo, 1)

        def out_inv(n, p):
            dve.wait_ge(av_mm, n + 1)
            nc.vector.reciprocal(rinv[:, p % 2], av_heads[:, :, :, DK]).then_inc(o_inv, 1)

        def out_norm(n, p):
            dve.wait_ge(o_inv, n + 1)
            after(dve, ot_mm, n - 1)
            nc.vector.tensor_tensor(on[:, p % 2].rearrange("p (c t) (h j) -> p c (t h) j", c=2, h=2), av_heads[:, :, :, 0:DK],
                                    rinv[:, p % 2].unsqueeze(3).broadcast_to([P, 2, TG, DK]), ALU.mult).then_inc(o_nrm, 1)

        def times_q(n, p):
            dve.wait_ge(ot_mm, n + 1)
            dve.wait_ge(q_sb, n + 1)
            after(dve, r_lo, n - 1)
            nc.vector.tensor_tensor(r32[:, p % 2, :], ot_ps[:, :], q32[:, p, :], ALU.mult).then_inc(r_mul, 1)

        def residual(g, par):
            dve.wait_ge(pj_mm, pair_no(g, NP))
            dve.wait_ge(xres_in[par], 16 * (g // 2) + 16 if isinstance(g, int) else g)
            nc.vector.scalar_tensor_tensor(xres[:, par], pj_ps[:, :, :], gains[:, 0:1], xres[:, par],
                                           ALU.mult, ALU.add).then_inc(x1_done, 1)

        def ln2(g, par):
            dve.wait_ge(x1_done, g + 1)
            for t in range(TG):
                last = nc.vector.bn_stats(stats[:, 1, t, :], xres[:, par, t, :])
            last.then_inc(ln2_ops, 1)
            dve.wait_ge(ln2_ops, 3 * g + 1)
            nc.vector.memset(vare[:, 1, :], EPS)
            for t in range(TG):
                last = nc.vector.bn_aggr(mv[:, 1, t, :], stats[:, 1, t, :])
            last.then_inc(ln2_ops, 1)
            dve.wait_ge(ln2_ops, 3 * g + 2)
            nc.vector.tensor_tensor(vare[:, 1, :], vare[:, 1, :], mv[:, 1, :, 1], ALU.add).then_inc(ln2_ops, 1)

        def ln2_apply(g, par, scattered):
            dve.wait_ge(ln2_rstd, g + 1)
            after(dve, records_in[par], scattered)
            for t in range(TG):
                last = nc.vector.tensor_scalar(rec[:, par, 0, t, 0:D], xres[:, par, t, :], mv[:, 1, t, 0:1],
                                               rstd[:, 1, t:t + 1], ALU.subtract, ALU.mult)
            last.then_inc(ln2_done, 1)

        def second_record(g, par):
            dve.wait_ge(ln2_done, g + 1)
            nc.vector.tensor_copy(rec[:, par, 1, :, 0:D], rec[:, par, 0, :, 0:D]).then_inc(rec_done, 1)

        def expert_lo(e, part):
            dve.wait_ge(split_hi, 2 * e + part + 1)
            c = slice(part * WN // 2, (part + 1) * WN // 2)
            dst = weights[:, e] if isinstance(e, int) and e < HELD else split
            nc.vector.scalar_tensor_tensor(dst[:, 1, c], stage[:, c], WS, dst[:, 0, c], ALU.mult, ALU.subtract).then_inc(split_lo, 1)

        def over_e(a):
            return a.unsqueeze(2).broadcast_to([P, TG, E])

        def choose(g):
            done = g * ROUTE

            def link(ins, i):
                ins.then_inc(route_ops, 1)
                dve.wait_ge(route_ops, done + i)

            dve.wait_ge(lg_mm, g + 1)
            nc.vector.tensor_copy(lg[:, :, :], q_ps[:, 0:TG * E].rearrange("p (t e) -> p t e", t=TG)).then_inc(lg_read, 1)
            dve.wait_ge(lg_read, g + 1)
            for c, src in enumerate((lg, lg2)):
                i = 6 * c
                link(nc.vector.tensor_reduce(top[:, c, :], src[:, :, :], AX.X, ALU.max), i + 1)
                link(nc.vector.tensor_tensor(cand[:, :, :], src[:, :, :], over_e(top[:, c, :]), ALU.is_lt), i + 2)
                link(nc.vector.scalar_tensor_tensor(cand[:, :, :], cand[:, :, :], float(E), iota_e[:, :, :], ALU.mult, ALU.add), i + 3)
                link(nc.vector.tensor_reduce(choice[:, c, :], cand[:, :, :], AX.X, ALU.min), i + 4)
                link(nc.vector.tensor_tensor(mask[:, c], iota_e[:, :, :], over_e(choice[:, c, :]), ALU.is_equal), i + 5)
                if c == 0:
                    link(nc.vector.scalar_tensor_tensor(lg2[:, :, :], mask[:, 0], -BIG, lg[:, :, :], ALU.mult, ALU.add), i + 6)
            nc.vector.tensor_tensor(delta[:, :], top[:, 1, :], top[:, 0, :], ALU.subtract).then_inc(top_done, 1)
            nc.vector.tensor_tensor(mboth[:, :, :], mask[:, 0], mask[:, 1], ALU.add).then_inc(m_done, 1)

        def place(g, par):
            done = g * ROUTE
            dve.wait_ge(pos_mm, g + 1)
            nc.vector.tensor_tensor(pos[:, :, :], q_ps[:, 0:TG * E].rearrange("p (t e) -> p t e", t=TG), e_off[:, :, :],
                                    ALU.add).then_inc(pos_read, 1)
            dve.wait_ge(ed_done, g + 1)
            nc.vector.tensor_scalar(wsum[:, :], edelta[:, :], 1.0, None, ALU.add).then_inc(route_ops, 1)
            nc.vector.tensor_reduce(mtiles[:, :], mboth[:, :, :].rearrange("p t e -> p e t"), AX.X, ALU.add).then_inc(route_ops, 1)
            dve.wait_ge(pos_read, g + 1)
            for c in range(2):
                nc.vector.tensor_tensor(mask[:, c], pos[:, :, :], mask[:, c], ALU.mult).then_inc(route_ops, 1)
            dve.wait_ge(route_ops, done + 13)
            nc.vector.reciprocal(wfirst[:, :], wsum[:, :]).then_inc(route_ops, 1)
            nc.vector.tensor_tensor(seen[:, :], seen[:, :], mtiles[:, :], ALU.add).then_inc(route_ops, 1)
            dve.wait_ge(route_ops, done + 15)
            with nc.allow_low_precision(reason="one term of each sum is not zero: a row number, exact in float32"):
                for c in range(2):
                    nc.vector.tensor_reduce(slot[:, par, c, :], mask[:, c], AX.X, ALU.add)
            dve.wait_ge(route_ops, done + 17)
            nc.vector.tensor_copy(seen_h[:, :], seen[:, :])
            nc.vector.tensor_scalar(rec[:, par, 0, :, D + 1], wfirst[:, :], gains[:, 1:2], None, ALU.mult)
            nc.vector.scalar_tensor_tensor(rec[:, par, 1, :, D + 1], wfirst[:, :], gains[:, 1:2], edelta[:, :], ALU.mult, ALU.mult)
            for c in range(2):
                nc.vector.tensor_copy(rec[:, par, c, :, D].bitcast(U32), tok_ids[:, :])
            nc.vector.tensor_scalar(tok_ids[:, :], tok_ids[:, :], float(G), None, ALU.add).then_inc(slots_done, 1)

        def step(b, g, k, p, pairs_back=LAST):
            n = pair_no(g, p)
            if pairs_back >= 1:
                score_max(n - 1, (p - 1) % NP)
            if pairs_back >= 2:
                probs_lo(n - 2, (p - 2) % NP)
            if pairs_back >= 1:
                score_sub(n - 1, (p - 1) % NP)
            if pairs_back >= 3:
                out_inv(n - 3, (p - 3) % NP)
            if p in (4, 5) and has_next(g):
                split_x(g + 1, 1 - k, p - 4)
            if pairs_back >= 4:
                times_q(n - 4, (p - 4) % NP)
            if pairs_back >= 3:
                out_norm(n - 3, (p - 3) % NP)
            if p == 0 and has_next(g):
                ln1_of(b, g, k)
            if p == 1 and has_next(g):
                ln1_moments(g + 1)
            if p == 1 and known(g, 2):
                choose(g - 2)
            if p == 3 and has_next(g):
                ln1_apply(g + 1, 1 - k)
            if p == 3 and known(g, 2):
                place(g - 2, k)
            if p in (4, 7):
                expert_lo(g, p // 7)
            if p == 5 and known(g, 1):
                residual_of(b, g, k)
                ln2(g - 1, 1 - k)
            if p == 6 and known(g, 1):
                ln2_apply(g - 1, 1 - k, (16 + 32 * TG * (b if k else b - 1)) if known(g, 3) else 0)
            if p == 7 and known(g, 1):
                second_record(g - 1, 1 - k)

        def ln1_of(b, g, k):
            if isinstance(b, int):
                ln1(g + 1, 1 - k)
                return
            par = 1 - k
            dve.wait_ge(x_in[par], (b + k) * 16 + 16)
            for t in range(TG):
                last = nc.vector.bn_stats(stats[:, 0, t, :], xin[:, par, t, :])
            last.then_inc(ln1_ops, 1)

        def residual_of(b, g, k):
            if isinstance(b, int):
                residual(g - 1, 1 - k)
                return
            par = 1 - k
            dve.wait_ge(pj_mm, pair_no(g - 1, NP))
            dve.wait_ge(xres_in[par], (b + k) * 16)
            nc.vector.scalar_tensor_tensor(xres[:, par], pj_ps[:, :, :], gains[:, 0:1], xres[:, par],
                                           ALU.mult, ALU.add).then_inc(x1_done, 1)

        for k in range(GB):
            for p in range(NP):
                step(0, k, k, p, pairs_back=min(LAST, k * NP + p))
        with dve.Fori(1, B - 1) as b:
            for k in range(GB):
                for p in range(NP):
                    step(b, b * GB + k, k, p)
        for k in range(GB):
            for p in range(NP):
                step(B - 1, NG - GB + k, k, p)
        for p in range(LAST):
            n = NS + p
            if p < 1:
                score_max(n - 1, NP + p - 1)
            if p < 2:
                probs_lo(n - 2, NP + p - 2)
            if p < 1:
                score_sub(n - 1, NP + p - 1)
            if p < 3:
                out_inv(n - 3, NP + p - 3)
            if p < 4:
                times_q(n - 4, NP + p - 4)
            if p < 3:
                out_norm(n - 3, NP + p - 3)
            if p == 1:
                choose(NG - 2)
            if p == 3:
                place(NG - 2, 0)
        residual(NG - 1, 1)
        ln2(NG - 1, 1)
        ln2_apply(NG - 1, 1, 16 + 32 * TG * (B - 1))
        second_record(NG - 1, 1)
        choose(NG - 1)
        place(NG - 1, 1)

        dve.wait_ge(count_mm, 1)
        nc.vector.tensor_tensor(pad_slot[:, :], q_ps[:, 0:E], pad_off[:, :], ALU.add).then_inc(pad_slots, 1)

        def link(ins, i):
            ins.then_inc(table_ops, 1)
            dve.wait_ge(table_ops, i)

        link(nc.vector.tensor_copy(count1[:, :], q_ps[0:1, 0:E]), 1)
        link(nc.vector.tensor_tensor(under[:, :, :], steps_128[:, :, :], count1[:, :].unsqueeze(2).broadcast_to([1, E, T // P]), ALU.is_lt), 2)
        link(nc.vector.tensor_reduce(blocks[:, :], under[:, :, :], AX.X, ALU.add), 3)
        link(nc.vector.tensor_tensor(cum[:, :, :], upto[:, :, :], blocks[:, :].unsqueeze(1).broadcast_to([1, E, E]), ALU.mult), 4)
        link(nc.vector.tensor_reduce(ends[:, :], cum[:, :, :], AX.X, ALU.add), 5)
        link(nc.vector.tensor_tensor(past[:, :, :], block_no[:, :, :], ends[:, :].unsqueeze(1).broadcast_to([1, NB, E]), ALU.is_ge), 6)
        link(nc.vector.tensor_reduce(blk_e[:, :], past[:, :, :], AX.X, ALU.add), 7)
        link(nc.vector.tensor_tensor(past[:, :, :], past[:, :, :], blocks[:, :].unsqueeze(1).broadcast_to([1, NB, E]), ALU.mult), 8)
        link(nc.vector.tensor_reduce(blk_s[:, :], past[:, :, :], AX.X, ALU.add), 9)
        link(nc.vector.tensor_tensor(blk_s[:, :], block_no[:, :, 0], blk_s[:, :], ALU.subtract), 10)
        link(nc.vector.tensor_scalar(blk_s[:, :], blk_s[:, :], float(P), None, ALU.mult), 11)
        link(nc.vector.scalar_tensor_tensor(blk_s[:, :], blk_e[:, :], float(REGION), blk_s[:, :], ALU.mult, ALU.add), 12)
        nc.vector.tensor_scalar(table[:, NB:2 * NB], blk_s[:, :], float(E * REGION), None, ALU.min).then_inc(table_ops, 1)
        nc.vector.tensor_scalar(table[:, 0:NB], blk_e[:, :], float(E - 1), None, ALU.min).then_inc(table_ops, 1)
        dve.wait_ge(table_ops, 14)

    @block.gpsimd
    def _(pool):
        nc.gpsimd.memset(ident[:, :], 0.0).then_inc(base_set, 1)
        nc.gpsimd.memset(ones[:, :], 1.0).then_inc(base_set, 1)
        nc.gpsimd.memset(before[:, :], 1.0).then_inc(base_set, 1)
        nc.gpsimd.memset(upto[:, :, :], 1.0).then_inc(base_set, 1)
        nc.gpsimd.memset(pad_rec[:, :], 0.0).then_inc(base_set, 1)
        pool.wait_ge(base_set, 5)
        nc.gpsimd.affine_select(out=ident[:, :], in_=ident[:, :], compare_op=ALU.not_equal, fill=1.0, base=0,
                                pattern=[[-1, P]], channel_multiplier=1).then_inc(consts_set, 1)
        nc.gpsimd.affine_select(out=before[:, :], in_=before[:, :], compare_op=ALU.is_gt, fill=0.0, base=0,
                                pattern=[[1, P]], channel_multiplier=-1).then_inc(consts_set, 1)
        nc.gpsimd.affine_select(out=upto[:, :, :], in_=upto[:, :, :], compare_op=ALU.is_ge, fill=0.0, base=0,
                                pattern=[[1, E], [-1, E]], channel_multiplier=0).then_inc(consts_set, 1)
        nc.gpsimd.memset(minus_half[:, :], -0.5).then_inc(consts_set, 1)

        def count_up(dst, pattern, channel):
            nc.gpsimd.iota(dst, pattern=pattern, base=0, channel_multiplier=channel,
                           allow_small_or_imprecise_dtypes=True).then_inc(consts_set, 1)

        nc.gpsimd.iota(pad_rec[:, D:D + 1].bitcast(U32), pattern=[[0, 1]], base=T, channel_multiplier=1).then_inc(consts_set, 1)
        nc.gpsimd.iota(spare_slot[:, :], pattern=[[0, 1]], base=E * REGION, channel_multiplier=1).then_inc(consts_set, 1)
        count_up(iota_e[:, :, :], [[0, TG], [1, E]], 0)
        count_up(e_off[:, :, :], [[0, TG], [REGION, E]], 0)
        count_up(pad_off[:, :], [[REGION, E]], 1)
        count_up(tok_ids[:, :], [[1, TG]], TG)
        count_up(steps_128[:, :, :], [[0, E], [P, T // P]], 0)
        count_up(block_no[:, :, :], [[1, NB], [0, E]], 0)
        for i, t in enumerate((vb_h, vb_l)):
            nc.gpsimd.memset(t[:, :, :, :, :], 0.0).then_inc(zeroed, 1)
        nc.gpsimd.memset(wait_mark[:, :], 0.0).then_inc(consts_set, 1)
        pool.wait_ge(consts_set, CONSTS)
        pool.indirect_dma_start(dram["out"], bass.IndirectOffsetOnAxis(pad_rec[:, D:D + 1].bitcast(U32), 0), pad_rec[:, 0:D],
                                None).then_inc(records_in[0], 16)
        pool.indirect_dma_start(records, bass.IndirectOffsetOnAxis(spare_slot[:, :], 0), pad_rec[:, :], None).then_inc(records_in[1], 16)

        def ln_rstd(i, g, ops, done):
            pool.wait_ge(ops, 3 * g + 3)
            nc.gpsimd.tensor_tensor(rstd[:, i, :], vare[:, i, :], minus_half[:, :], ALU.pow).then_inc(done, 1)

        def split_q(n, p):
            pool.wait_ge(q_hi, n + 1)
            nc.gpsimd.tensor_tensor(q_l[:, p % 2, :], q32[:, p, :], q_h[:, p % 2, :], ALU.subtract).then_inc(q_lo, 1)

        def product_lo(n, p):
            pool.wait_ge(r_hi, n + 1)
            nc.gpsimd.tensor_tensor(r_l[:, p % 2, :], r32[:, p % 2, :], r_h[:, p % 2, :], ALU.subtract).then_inc(r_lo, 1)

        def scatter(g, par):
            pool.wait_ge(slots_done, g + 1)
            nc.gpsimd.tensor_tensor(wait_mark[:, 1:2], wait_mark[:, 0:1], wait_mark[:, 0:1], ALU.add)
            for c in range(2):
                for t in range(TG):
                    pool.indirect_dma_start(records, bass.IndirectOffsetOnAxis(slot[:, par, c, t:t + 1], 0),
                                            rec[:, par, c, t, :], None).then_inc(records_in[par], 16)

        def step(g, k, p, pairs_back=LAST):
            n = pair_no(g, p)
            split_q(n, p)
            if pairs_back >= 4:
                product_lo(n - 4, (p - 4) % NP)
            if p == 2 and has_next(g):
                ln_rstd(0, g + 1, ln1_ops, ln1_rstd)
            if p == 4 and known(g, 2):
                scatter(g - 2, k)
            if p == 5 and known(g, 1):
                ln_rstd(1, g - 1, ln2_ops, ln2_rstd)

        ln_rstd(0, 0, ln1_ops, ln1_rstd)
        for k in range(GB):
            for p in range(NP):
                step(k, k, p, pairs_back=min(LAST, k * NP + p))
        with pool.Fori(1, B - 1) as b:
            for k in range(GB):
                for p in range(NP):
                    step(b * GB + k, k, p)
        for k in range(GB):
            for p in range(NP):
                step(NG - GB + k, k, p)
        for p in range(4):
            product_lo(NS + p - 4, NP + p - 4)
        scatter(NG - 2, 0)
        ln_rstd(1, NG - 1, ln2_ops, ln2_rstd)
        scatter(NG - 1, 1)
        pool.wait_ge(pad_slots, 1)
        for e in range(E):
            pool.indirect_dma_start(records, bass.IndirectOffsetOnAxis(pad_slot[:, e:e + 1], 0), pad_rec[:, :], None).then_inc(pads_in, 16)
        for par in range(2):
            pool.wait_ge(records_in[par], 16 + 32 * TG * B)
        pool.wait_ge(pads_in, 16 * E)


def experts(nc, ctx, dram, ident, table, loads_base, weights):
    records, out = dram["records"], dram["out"]

    def sb(name, shape, dt):
        return ctx.enter_context(nc.sbuf_tensor(name, shape, dt))

    def psum(name, shape):
        return ctx.enter_context(nc.psum_tensor(name, shape, F32))

    def sem(name):
        return ctx.enter_context(nc.semaphore(name))

    RB = 4
    sb("weights_rest", [P, E - HELD, 2, WN], F16)
    rows = sb("rows", [P, RB, ROW], F32)
    meta = sb("meta", [P, RB, 2], F32)
    xt_h, xt_l = (sb(f"bx_{s}", [P, 2, KD, P], F16) for s in "hl")
    hid = sb("hid", [P, 2, F], F32)
    ht_h, ht_l = (sb(f"ht_{s}", [P, 2, FC, P], F16) for s in "hl")
    y = sb("y", [P, 2, D], F32)
    wait_mark = sb("b_wait_mark", [P, 2], F32)

    xt_ps = psum("bxt_ps", [P, KD, P])
    h_ps = psum("h_ps", [P, F])
    ht_ps = psum("ht_ps", [P, FC, P])
    y_ps = [psum(f"y_ps{i}", [P, 512]) for i in range(2)]

    rows_in = [sem(f"rows_in{i}") for i in range(RB)]
    mark_set = sem("mark_set")
    loads = sem("weight_loads")
    xt_mm, x_hi, x_lo, meta_done, h_mm, h_act, ht_mm, h_hi, h_lo, y_mm, y_out, added = (sem(n) for n in (
        "xt_mm", "x_hi", "x_lo", "meta_done", "h_mm", "h_act", "ht_mm", "h_hi", "h_lo", "y_mm", "y_out", "added"))

    HEAD = RB
    TRIPS = (NB - HEAD - RB) // RB
    TAIL = HEAD + TRIPS * RB

    def run(eng, step):
        for i in range(HEAD):
            step(i, i % RB)
        with eng.Fori(1, 1 + TRIPS) as trip:
            for r in range(RB):
                step(trip * RB + r, r)
        for i in range(TAIL, NB):
            step(i, i % RB)

    def there(i):
        return not isinstance(i, int) or i < NB

    def before_now(i):
        return not isinstance(i, int) or i >= 0

    def block_loads(i, r):
        if isinstance(i, int):
            return 16 * (i // RB + 1)
        return (i - r) * (16 // RB) + 16

    block = ctx.enter_context(nc.Block())

    @block.sync
    def _(sp):
        sp.wait_ge(loads, 1)
        for e in range(HELD, E):
            sp.dma_start(weights[:, e], dram["w_split"][e]).then_inc(loads, 16)
            sp.wait_ge(loads, 1 + 16 * (e - HELD + 1))

    @block.tensor
    def _(pe):
        def transpose_x(i, r):
            pe.wait_ge(rows_in[r], block_loads(i, r))
            after(pe, x_lo, i)
            for k in range(KD):
                last = nc.tensor.transpose(xt_ps[:, k, :], rows[:, r, k * P:(k + 1) * P], ident[:, :])
            last.then_inc(xt_mm, 1)

        def expert_of(i):
            return pe.value_load(table[0:1, i:i + 1] if isinstance(i, int) else table[0:1, bass.ds(i, 1)], min_val=0, max_val=E - 1)

        def w_at(e, s, start, n):
            return weights[:, bass.ds(e, 1), s, start:start + n].rearrange("p o n -> p (o n)")

        def hidden(i, r, e):
            pe.wait_ge(x_lo, i + 1)
            after(pe, h_act, i)
            pe.wait_ge(loads, e * 16 + 1)
            for half in range(2):
                for j, (xt, s) in enumerate(((xt_h, 0), (xt_h, 1), (xt_l, 0))):
                    for k in range(KD):
                        last = nc.tensor.matmul(h_ps[:, half * 512:(half + 1) * 512], xt[:, r % 2, k, :],
                                                w_at(e, s, k * F + half * 512, 512),
                                                start=(j == 0 and k == 0), stop=(j == 2 and k == KD - 1))
            last.then_inc(h_mm, 1)

        def transpose_h(i, r):
            pe.wait_ge(h_act, i + 1)
            after(pe, h_lo, i)
            for c in range(FC):
                last = nc.tensor.transpose(ht_ps[:, c, :], hid[:, r % 2, c * P:(c + 1) * P], ident[:, :])
            last.then_inc(ht_mm, 1)

        def down(i, r, e):
            pe.wait_ge(h_lo, i + 1)
            after(pe, y_out, i - 1)
            for c in range(FC):
                for j, (ht, s) in enumerate(((ht_h, 0), (ht_h, 1), (ht_l, 0))):
                    last = nc.tensor.matmul(y_ps[r % 2][:, 0:D], ht[:, r % 2, c, :], w_at(e, s, WN // 2 + c * D, D),
                                            start=(c == 0 and j == 0), stop=(c == FC - 1 and j == 2))
            last.then_inc(y_mm, 1)

        def step(i, r):
            if there(i + 1):
                transpose_x(i + 1, (r + 1) % RB)
            hidden(i, r, expert_of(i))
            if before_now(i - 1):
                down(i - 1, (r - 1) % RB, expert_of(i - 1))
            transpose_h(i, r)

        transpose_x(0, 0)
        run(pe, step)
        down(NB - 1, (NB - 1) % RB, expert_of(NB - 1))

    @block.scalar
    def _(act):
        def load_rows(i, r):
            first = act.value_load(table[0:1, NB + i:NB + i + 1] if isinstance(i, int) else table[0:1, bass.ds(i + NB, 1)],
                                   min_val=0, max_val=E * REGION)
            after(act, x_lo, i - RB + 1)
            after(act, meta_done, i - RB + 1)
            act.dma_start(rows[:, r, :], records[bass.ds(first, P), :]).then_inc(rows_in[r], 16)

        def x_high(i, r):
            act.wait_ge(xt_mm, i + 1)
            after(act, h_mm, i - 1)
            nc.scalar.copy(xt_h[:, r % 2], xt_ps[:, :, :]).then_inc(x_hi, 1)

        def silu(i, r):
            act.wait_ge(h_mm, i + 1)
            after(act, ht_mm, i - 1)
            nc.scalar.activation(hid[:, r % 2, :], h_ps[:, :], ACT.Silu, scale=1.0 / WS).then_inc(h_act, 1)

        def weigh(i, r):
            act.wait_ge(y_mm, i + 1)
            act.wait_ge(meta_done, i + 1)
            after(act, added, (i - 1) * 16)
            nc.scalar.mul(y[:, r % 2, :], y_ps[r % 2][:, 0:D], meta[:, r, 1:2]).then_inc(y_out, 1)

        def h_high(i, r):
            act.wait_ge(ht_mm, i + 1)
            after(act, y_mm, i - 1)
            nc.scalar.copy(ht_h[:, r % 2], ht_ps[:, :, :]).then_inc(h_hi, 1)

        def step(i, r):
            if there(i + 1):
                x_high(i + 1, (r + 1) % RB)
            if there(i + RB):
                load_rows(i + RB, r)
            silu(i, r)
            if before_now(i - 1):
                weigh(i - 1, (r - 1) % RB)
            h_high(i, r)

        for i in range(RB):
            load_rows(i, i)
        x_high(0, 0)
        run(act, step)
        weigh(NB - 1, (NB - 1) % RB)

    @block.vector
    def _(dve):
        def x_low(i, r):
            dve.wait_ge(rows_in[r], block_loads(i, r))
            after(dve, added, (i - RB + 1) * 16)
            nc.vector.tensor_copy(meta[:, r, :], rows[:, r, D:D + 2]).then_inc(meta_done, 1)
            dve.wait_ge(x_hi, i + 1)
            nc.vector.tensor_tensor(xt_l[:, r % 2], xt_ps[:, :, :], xt_h[:, r % 2], ALU.subtract).then_inc(x_lo, 1)

        def h_low(i, r):
            dve.wait_ge(h_hi, i + 1)
            nc.vector.tensor_tensor(ht_l[:, r % 2], ht_ps[:, :, :], ht_h[:, r % 2], ALU.subtract).then_inc(h_lo, 1)

        def step(i, r):
            if there(i + 1):
                x_low(i + 1, (r + 1) % RB)
            h_low(i, r)

        nc.vector.memset(loads_base[:, :], 0.0).then_inc(loads, 1)
        x_low(0, 0)
        run(dve, step)

    @block.gpsimd
    def _(pool):
        def step(i, r):
            pool.wait_ge(y_out, i + 1)
            after(pool, added, i * 16)
            pool.wait_ge(mark_set, i + 1)
            nc.gpsimd.tensor_tensor(wait_mark[:, 1:2], wait_mark[:, 0:1], wait_mark[:, 0:1], ALU.add).then_inc(mark_set, 1)
            pool.indirect_dma_start(out, bass.IndirectOffsetOnAxis(meta[:, r, 0:1].bitcast(U32), 0), y[:, r % 2, :], None,
                                    compute_op=ALU.add).then_inc(added, 16)

        nc.gpsimd.memset(wait_mark[:, :], 0.0).then_inc(mark_set, 1)
        run(pool, step)
        pool.wait_ge(added, 16 * NB)


def kernel(x, ctx_1024, g_xattn, g_ffn, L0_xattn_w_qs, L0_xattn_w_ks, L0_xattn_w_vs, L0_xattn_w_proj, L0_xattn_b_proj,
           L0_ffn_gate_w, L0_ffn_w1, L0_ffn_w2):
    import concourse.bacc as bacc
    from concourse.bass_utils import run_bass_kernel_spmd

    nc = bacc.Bacc("TRN2", target_bir_lowering=False, num_devices=1)
    given = dict(x=x, ctxt=ctx_1024, g_xattn=g_xattn, g_ffn=g_ffn, wq=L0_xattn_w_qs, wk=L0_xattn_w_ks, wv=L0_xattn_w_vs,
                 wproj=L0_xattn_w_proj, bproj=L0_xattn_b_proj, gate=L0_ffn_gate_w, w1=L0_ffn_w1, w2=L0_ffn_w2)
    arrays = {f"in_{n}": np.ascontiguousarray(a) for n, a in given.items()}
    inputs = {n: nc.dram_tensor(f"in_{n}", given[n].shape, F32, kind="ExternalInput").ap() for n in given}
    out = nc.dram_tensor("out", (T + P, D), F32, kind="ExternalOutput").ap()
    build(nc, out=out, **inputs)
    got = run_bass_kernel_spmd(nc, [arrays], core_ids=[0])
    return got.results[0]["out"][0:T].reshape(B, L, D)
```

```python
from contextlib import ExitStack

import numpy as np
import concourse.bass as bass
from concourse import mybir

F32 = mybir.dt.float32
F16 = mybir.dt.float16
U32 = mybir.dt.uint32
I32 = mybir.dt.int32
ACT = mybir.ActivationFunctionType
ALU = mybir.AluOpType
AX = mybir.AxisListType

P = 128
B, L, D = 4, 1024, 256
M, H, DK = 64, 16, 64
E, F = 8, 1024
T = B * L
KD = D // P
NP = H // 2
TG = 4
G = TG * P
NG = T // G
GB = L // G
NS = NG * NP
FC = F // P
EPS = 1e-5
WS = 64.0
PS = 64.0
REGION = T + P
ROW = D + 2
NB = (2 * T + E * (P - 1)) // P
HELD = 1
BIG = 3.0e38
WN = 2 * KD * F
LAST = 6
WC = 8


def after(eng, sem, count):
    if isinstance(count, int) and count <= 0:
        return
    eng.wait_ge(sem, count)


def build(nc, x, ctxt, g_xattn, g_ffn, wq, wk, wv, wproj, bproj, gate, w1, w2, out):
    dram = dict(
        x=x, ctxt=ctxt, g_xattn=g_xattn, g_ffn=g_ffn, wq=wq, wk=wk, wv=wv, wproj=wproj, bproj=bproj, gate=gate, w1=w1, w2=w2,
        out=out,
        records=nc.dram_tensor("records", (E * REGION + P, ROW), F32, kind="Internal").ap(),
        w_split=nc.dram_tensor("w_split", (E, P, 2, WN), F16, kind="Internal").ap(),
    )
    with ExitStack() as keep:
        def sb(name, shape, dt):
            return keep.enter_context(nc.sbuf_tensor(name, shape, dt))

        ident = sb("ident", [P, P], F32)
        table = sb("table", [1, 2 * NB], I32)
        loads_base = sb("loads_base", [1, 8], F32)
        weights = nc.alloc_sbuf_tensor_at("weights", [P, E, 2, WN], F16, offset=nc.sbuf_base)
        sb("weights_held", [P, HELD, 2, WN], F16)
        with ExitStack() as stage_ctx:
            attention(nc, stage_ctx, dram, ident, table, weights)
        with ExitStack() as stage_ctx:
            experts(nc, stage_ctx, dram, ident, table, loads_base, weights)


def attention(nc, ctx, dram, ident, table, weights):
    x_groups = dram["x"].rearrange("b l d -> (b l) d").rearrange("(g p t) d -> g p t d", p=P, t=TG)
    out_groups = dram["out"][0:T, :].rearrange("(g p t) d -> g p t d", p=P, t=TG)
    records, w_split = dram["records"], dram["w_split"]

    def sb(name, shape, dt):
        return ctx.enter_context(nc.sbuf_tensor(name, shape, dt))

    def psum(name, shape):
        return ctx.enter_context(nc.psum_tensor(name, shape, F32))

    def sem(name):
        return ctx.enter_context(nc.semaphore(name))

    wq_h, wq_l = (sb(f"wq_{s}", [P, KD, H * DK], F16) for s in "hl")
    wp_h, wp_l = (sb(f"wp_{s}", [P, NP, D], F16) for s in "hl")
    kb_h, kb_l = (sb(f"kb_{s}", [P, B, NP, 2 * M], F16) for s in "hl")
    vb_h, vb_l = (sb(f"vb_{s}", [P, B, NP, 2, DK], F16) for s in "hl")
    gate_t = sb("gate_t", [P, KD, E], F32)
    bias_rows = sb("bias_rows", [1, 2, D], F16)
    ones = sb("ones", [P, P], F16)
    before = sb("before", [P, P], F16)
    iota_e = sb("iota_e", [P, TG, E], F32)
    e_off = sb("e_off", [P, TG, E], F32)
    tok_ids = sb("tok_ids", [P, TG], F32)
    minus_half = sb("minus_half", [P, TG], F32)
    pad_rec = sb("pad_rec", [P, ROW], F32)
    tanhs = sb("tanhs", [P, 2], F32)
    gains = sb("gains", [P, 2], F32)
    seen = sb("seen", [P, E], F32)
    seen_h = sb("seen_h", [P, E], F16)

    stage = sb("stage", [P, WN], F32)
    split = sb("split", [P, 2, WN], F16)
    ctx_sb = sb("ctx_sb", [P, 2, D], F32)
    gate_sb = sb("gate_sb", [E, D], F32)
    bias_sb = sb("bias_sb", [1, D], F32)

    xin = sb("xin", [P, 2, TG, D], F32)
    xres = sb("xres", [P, 2, TG, D], F32)
    stats = sb("stats", [P, 2, TG, 6], F32)
    mv = sb("mv", [P, 2, TG, 2], F32)
    vare = sb("vare", [P, 2, TG], F32)
    rstd = sb("rstd", [P, 2, TG], F32)
    shift = sb("shift", [P, 2, TG], F32)
    xn = sb("xn", [P, TG, D], F32)
    xt_h, xt_l = (sb(f"xt_{s}", [P, 2, KD, G], F16) for s in "hl")
    q32 = sb("q32", [P, NP, G], F32)
    q_h, q_l = (sb(f"q_{s}", [P, 2, G], F16) for s in "hl")
    smax = sb("smax", [P, 2, TG, 2], F32)
    ssub = sb("ssub", [P, 2, TG, 2, M], F32)
    ex = sb("ex", [P, 2, TG, 2 * M], F32)
    e_h, e_l = (sb(f"e_{s}", [P, 2, G], F16) for s in "hl")
    esum, rinv = (sb(n, [P, 2, TG, 2], F32) for n in ("esum", "rinv"))
    pn = sb("pn", [P, 2, TG, 2 * M], F32)
    r32 = sb("r32", [P, 2, G], F32)
    r_h, r_l = (sb(f"r_{s}", [P, 2, G], F16) for s in "hl")
    rec = sb("rec", [P, 2, 2, TG, ROW], F32)
    x2t = sb("x2t", [P, KD, G], F32)
    lg, lg2, cand, pos = (sb(n, [P, TG, E], F32) for n in ("lg", "lg2", "cand", "pos"))
    mask = sb("mask", [P, 2, TG, E], F32)
    mboth = sb("mboth", [P, TG, E], F16)
    mtiles = sb("mtiles", [P, E], F32)
    top = sb("top", [P, 2, TG], F32)
    choice = sb("choice", [P, 2, TG], F32)
    delta, edelta, wsum, wfirst = (sb(n, [P, TG], F32) for n in ("delta", "edelta", "wsum", "wfirst"))
    slot = sb("slot", [P, 2, 2, TG], U32)
    spare_slot = sb("spare_slot", [P, 1], U32)
    pad_first = sb("pad_first", [1, E], I32)
    wait_mark = sb("wait_mark", [P, 2], F32)

    steps_128 = sb("steps_128", [1, E, T // P], F32)
    under = sb("under", [1, E, T // P], F32)
    upto = sb("upto", [1, E, E], F32)
    cum = sb("cum", [1, E, E], F32)
    block_no = sb("block_no", [1, NB, E], F32)
    past = sb("past", [1, NB, E], F32)
    count1, blocks, ends = (sb(n, [1, E], F32) for n in ("count1", "blocks", "ends"))
    blk_e, blk_s = (sb(n, [1, NB], F32) for n in ("blk_e", "blk_s"))

    wq_sb = q32[:, 0:4, :].rearrange("p a g -> p (a g)")
    wp_sb = q32[:, 4:8, :].rearrange("p a g -> p (a g)").rearrange("p (c n) -> p c n", c=KD)
    ctx_t = x2t[:, :, :].rearrange("p k (b c m) -> p k b c m", b=B, c=2)
    wk_sb, wv_sb = (split[:, i, :].bitcast(F32) for i in range(2))
    wk_cols = rec[:, 0].rearrange("p c t w -> p (c t w)")[:, 0:KD * H * DK].rearrange("p (k n) -> p k n", k=KD)

    q_ps = [psum(f"q_ps{i}", [P, G]) for i in range(2)]
    s_ps = psum("s_ps", [P, TG, 2, M])
    pt_ps = psum("pt_ps", [P, G])
    ot_ps = psum("ot_ps", [P, G])
    pj_ps = psum("pj_ps", [P, TG, D])
    job_ps = psum("job_ps", [P, G])

    gain_in, gate_in, bias_in, ctx_in, wk_in, wv_in, wq_in, wp_in = (sem(n) for n in (
        "gain_in", "gate_in", "bias_in", "ctx_in", "wk_in", "wv_in", "wq_in", "wp_in"))
    stage_in = [sem(f"stage_in{i}") for i in range(2)]
    split_stored = [sem(f"split_stored{i}") for i in range(2)]
    x_in = [sem(f"x_in{i}") for i in range(2)]
    xres_in = [sem(f"xres_in{i}") for i in range(2)]
    records_in = [sem(f"records_in{i}") for i in range(2)]
    pads_in, x1_stored = sem("pads_in"), sem("x1_stored")
    base_set, consts_set, k_zeroed, v_zeroed, wk_laid, setup_ops, tanh_done = (sem(n) for n in (
        "base_set", "consts_set", "k_zeroed", "v_zeroed", "wk_laid", "setup_ops", "tanh_done"))
    ctx_tp, ctx_copied, gate_tp, gate_copied, wp_tp, wp_hi, wp_lo, wq_hi, wq_lo, bias_hi = (sem(n) for n in (
        "ctx_tp", "ctx_copied", "gate_tp", "gate_copied", "wp_tp", "wp_hi", "wp_lo", "wq_hi", "wq_lo", "bias_hi"))
    k_mm, k_hi, k_lo, v_mm, v_hi, v_lo = (sem(n) for n in ("k_mm", "k_hi", "k_lo", "v_mm", "v_hi", "v_lo"))
    ln1_ops, ln1_rstd, ln1_shift, xn_done, xt_tp, xt_hi, xt_lo = (sem(n) for n in ("ln1_ops", "ln1_rstd", "ln1_shift", "xn_done", "xt_tp", "xt_hi", "xt_lo"))
    q_mm, q_sb, q_hi, q_lo, s_mm, s_max, s_sub, e_x, pt_mm, e_hi, e_lo = (sem(n) for n in (
        "q_mm", "q_sb", "q_hi", "q_lo", "s_mm", "s_max", "s_sub", "e_x", "pt_mm", "e_hi", "e_lo"))
    e_sum, e_inv, p_nrm, ot_mm, r_mul, r_hi, r_lo, pj_mm = (sem(n) for n in (
        "e_sum", "e_inv", "p_nrm", "ot_mm", "r_mul", "r_hi", "r_lo", "pj_mm"))
    x1_done, ln2_ops, ln2_rstd, ln2_shift, ln2_done, rec_done, x2_tp, x2_copied = (sem(n) for n in (
        "x1_done", "ln2_ops", "ln2_rstd", "ln2_shift", "ln2_done", "rec_done", "x2_tp", "x2_copied"))
    lg_mm, lg_read, top_done, ed_done, m_done, pos_mm, pos_read, slots_done, route_ops = (sem(n) for n in (
        "lg_mm", "lg_read", "top_done", "ed_done", "m_done", "pos_mm", "pos_read", "slots_done", "route_ops"))
    split_hi, split_lo, pad_slots, table_ops = (sem(n) for n in ("split_hi", "split_lo", "pad_slots", "table_ops"))

    CONSTS = 12
    ROUTE = 17

    def pair_no(g, p):
        return g * NP + p

    def known(g, least):
        return not isinstance(g, int) or g >= least

    def has_next(g):
        return not isinstance(g, int) or g < NG - 1

    def at(ap, i, pattern, **sizes):
        return ap[i] if isinstance(i, int) else ap[bass.ds(i, 1)].rearrange(pattern, **sizes)

    def pieces(g, p):
        if isinstance(g, int) and g == 0:
            return range(2 * (p - 4), 2 * (p - 4) + 2) if p >= 4 else ()
        return (p,)

    def d_chunk(a, k):
        return a.rearrange("p (n k) -> p k n", k=KD)[:, k]

    def rows_by_head(w):
        return w.rearrange("h (p k) j -> p h (k j)", k=KD)

    def by_head(w_sb):
        return w_sb.rearrange("p (h n) -> p h n", h=H)

    def w_chunk(w_sb, k, first, n):
        return w_sb.rearrange("p (h k j) -> p k h j", h=H, k=KD)[:, k, first:first + n, :]

    def heads_of(wq, k, half):
        return wq[:, k, half * H * DK // 2:(half + 1) * H * DK // 2].rearrange("p (h j) -> p h j", j=DK)

    block = ctx.enter_context(nc.Block())

    @block.sync
    def _(sp):
        sp.dma_start(xin[:, 0], x_groups[0]).then_inc(x_in[0], 16)
        sp.dma_start(ctx_sb[:, :, :], dram["ctxt"].rearrange("(c b) m d -> (b m) c d", b=2)).then_inc(ctx_in, 16)
        sp.dma_start(by_head(wq_sb), rows_by_head(dram["wq"])).then_inc(wq_in, 16)
        sp.dma_start(by_head(wk_sb), rows_by_head(dram["wk"])).then_inc(wk_in, 16)
        sp.dma_start(gate_sb[:, :], dram["gate"]).then_inc(gate_in, 16)
        sp.dma_start(bias_sb[:, :], dram["bproj"].rearrange("(o d) -> o d", o=1)).then_inc(bias_in, 16)
        sp.dma_start(wp_sb, dram["wproj"].rearrange("(c p) n -> p c n", p=P)).then_inc(wp_in, 16)
        sp.dma_start(by_head(wv_sb), rows_by_head(dram["wv"])).then_inc(wv_in, 16)
        sp.dma_start(tanhs[:, 0:1], dram["g_xattn"].partition_broadcast(P)).then_inc(gain_in, 16)
        sp.dma_start(tanhs[:, 1:2], dram["g_ffn"].partition_broadcast(P)).then_inc(gain_in, 16)
        sp.dma_start(xin[:, 1], x_groups[1]).then_inc(x_in[1], 16)

        def load_w1(e):
            after(sp, split_lo, WC * e - WC // 2)
            sp.dma_start(stage[:, 0:WN // 2].rearrange("p (k f) -> p k f", k=KD),
                         at(dram["w1"], e, "o d f -> (o d) f").rearrange("(k p) f -> p k f", p=P)).then_inc(stage_in[0], 16)

        def load_w2(e):
            after(sp, split_lo, WC * e)
            sp.dma_start(stage[:, WN // 2:WN].rearrange("p (c d) -> p c d", c=FC),
                         at(dram["w2"], e, "o f d -> (o f) d").rearrange("(c p) d -> p c d", p=P)).then_inc(stage_in[1], 16)

        def load_residual(g, par):
            if known(g, 2):
                sp.wait_ge(x1_stored, 16 * (g - 1))
                sp.wait_ge(rec_done, g - 1)
            sp.dma_start(xres[:, par], at(x_groups, g, "o p t d -> (o p) t d")).then_inc(xres_in[par], 16)

        def load_x(g, par):
            sp.wait_ge(xn_done, g - 1)
            sp.dma_start(xin[:, par], at(x_groups, g, "o p t d -> (o p) t d")).then_inc(x_in[par], 16)

        def store_x1(g, par):
            sp.wait_ge(x1_done, g + 1)
            sp.dma_start(at(out_groups, g, "o p t d -> (o p) t d"), xres[:, par]).then_inc(x1_stored, 16)

        def store_split(e, half):
            done = WC * e + (half + 1) * WC // 2
            sp.wait_ge(split_hi, done)
            sp.wait_ge(split_lo, done)
            c = slice(half * WN // 2, (half + 1) * WN // 2)
            sp.dma_start(at(w_split, e, "o p s n -> (o p) s n")[:, :, c], split[:, :, c]).then_inc(split_stored[half], 16)

        def group(g, par):
            load_residual(g, par)
            if not isinstance(g, int) or g + 2 < NG:
                load_x(g + 2, par)
            if known(g, 1):
                store_x1(g - 1, 1 - par)
            if known(g, HELD):
                store_split(g, 0)
            if has_next(g):
                load_w1(g + 1)
            if known(g, HELD):
                store_split(g, 1)
            if has_next(g):
                load_w2(g + 1)

        load_w1(0)
        load_w2(0)
        for k in range(GB):
            group(k, k)
        with sp.Fori(1, B - 1) as b:
            for k in range(GB):
                group(b * GB + k, k)
        for k in range(GB):
            group(NG - GB + k, k)
        store_x1(NG - 1, 1)
        sp.wait_ge(pad_slots, 1)
        for e in range(E):
            first = sp.value_load(pad_first[0:1, e:e + 1], min_val=0, max_val=E * REGION)
            sp.dma_start(records[bass.ds(first, P), :], pad_rec[:, :]).then_inc(pads_in, 16)
        sp.wait_ge(pads_in, 16 * E)
        sp.wait_ge(x1_stored, 16 * NG)
        for half in range(2):
            sp.wait_ge(split_stored[half], 16 * (NG - HELD))

    @block.tensor
    def _(pe):
        pe.wait_ge(consts_set, 1)

        def x_transpose(g, k, bank):
            pe.wait_ge(xn_done, g + 1)
            for t in range(TG):
                last = nc.tensor.transpose(bank[:, t * P:(t + 1) * P], d_chunk(xn[:, t, :], k), ident[:, :])
            last.then_inc(xt_tp, 1)

        pe.wait_ge(ctx_in, 16)
        for k in range(KD):
            for c in range(2):
                o = (k * 2 + c) * P
                last = nc.tensor.transpose(s_ps[:].rearrange("p t h m -> p (t h m)")[:, o:o + P],
                                           d_chunk(ctx_sb[:, c, :], k), ident[:, :])
        last.then_inc(ctx_tp, 1)
        for k in range(KD):
            x_transpose(0, k, q_ps[k])
        pe.wait_ge(gate_in, 16)
        for k in range(KD):
            last = nc.tensor.transpose(ot_ps[:, k * E:(k + 1) * E], gate_sb[:, k * P:(k + 1) * P], ident[0:E, 0:E])
        last.then_inc(gate_tp, 1)

        def transpose_wp(part):
            pe.wait_ge(wp_in, 16)
            pe.wait_ge(gate_copied, 1)
            after(pe, wp_lo, part)
            for j in range(2):
                for c in range(KD):
                    o = (part * 2 + j) * P
                    last = nc.tensor.transpose(ot_ps[:, j * D + c * P:j * D + (c + 1) * P], wp_sb[:, c, o:o + P], ident[:, :])
            last.then_inc(wp_tp, 1)

        def project_k(p):
            pe.wait_ge(ctx_copied, 2)
            pe.wait_ge(wk_laid, 1)
            after(pe, k_lo, p)
            if p == 6:
                pe.wait_ge(xt_lo, KD + 1)
            if p == 7:
                pe.wait_ge(xt_lo, 2 * KD)
            for k in range(KD):
                last = nc.tensor.matmul(job_ps[:, 0:B * M], wk_cols[:, k, p * P:(p + 1) * P], ctx_t[:, k, :, 0, :],
                                        start=(k == 0), stop=(k == KD - 1))
            last.then_inc(k_mm, 1)

        def project_v(b):
            pe.wait_ge(wv_in, 16)
            for half in range(2):
                after(pe, v_lo, 2 * b + half - 1)
                for k in range(KD):
                    last = nc.tensor.matmul(pj_ps[:, 2 * half:2 * half + 2, :].rearrange("p a d -> p (a d)"),
                                            ctx_t[:, k, b, :, :].rearrange("p c m -> p (c m)"),
                                            w_chunk(wv_sb, k, half * H // 2, H // 2), start=(k == 0), stop=(k == KD - 1))
                last.then_inc(v_mm, 1)

        def project_q(g, p, par):
            n = pair_no(g, p)
            after(pe, q_hi, n - 1)
            if p == 0:
                pe.wait_ge(xt_lo, 2 * g + 2)
            if isinstance(g, int) and g == 0 and p % 4 == 0:
                pe.wait_ge(wq_lo, p // 4 + 1)
            for i, (wt, xt) in enumerate(((wq_h, xt_h), (wq_h, xt_l), (wq_l, xt_h))):
                for k in range(KD):
                    last = nc.tensor.matmul(q_ps[p % 2][:, :], wt[:, k, p * P:(p + 1) * P], xt[:, par, k, :],
                                            start=(i == 0 and k == 0), stop=(i == 2 and k == KD - 1))
            last.then_inc(q_mm, 1)

        def scores(b, n, p):
            pe.wait_ge(q_lo, n + 1)
            if isinstance(n, int) and n < NP:
                pe.wait_ge(k_lo, n + 1)
            after(pe, s_sub, n)
            for t in range(TG):
                for i, (qt, kt) in enumerate(((q_h, kb_h), (q_h, kb_l), (q_l, kb_h))):
                    last = nc.tensor.matmul(s_ps[:, t].rearrange("p h m -> p (h m)"), qt[:, p % 2, t * P:(t + 1) * P],
                                            kt[:, b, p, :] if isinstance(b, int)
                                            else kt[:, bass.ds(b, 1), p, :].rearrange("p o m -> p (o m)"),
                                            start=(i == 0), stop=(i == 2))
            last.then_inc(s_mm, 1)

        def transpose_probs(n, p):
            pe.wait_ge(p_nrm, n + 1)
            after(pe, e_lo, n)
            for t in range(TG):
                last = nc.tensor.transpose(pt_ps[:, t * P:(t + 1) * P], pn[:, p % 2, t, :], ident[:, :])
            last.then_inc(pt_mm, 1)

        def probs_v(b, n, p):
            pe.wait_ge(e_lo, n + 1)
            if isinstance(n, int) and n == 0:
                pe.wait_ge(v_lo, 2)
                pe.wait_ge(wp_lo, 4)
            after(pe, r_mul, n)
            for i, (vt, et) in enumerate(((vb_h, e_h), (vb_h, e_l), (vb_l, e_h))):
                last = nc.tensor.matmul(ot_ps[:, :], vt[:, b, p].rearrange("p h w -> p (h w)") if isinstance(b, int)
                                        else vt[:, bass.ds(b, 1), p].rearrange("p o h w -> p (o h w)"),
                                        et[:, p % 2, :], start=(i == 0), stop=(i == 2))
            last.then_inc(ot_mm, 1)

        def project_out(g, n, p):
            pe.wait_ge(r_lo, n + 1)
            if isinstance(n, int) and n == 0:
                pe.wait_ge(v_lo, 2 * B)
                pe.wait_ge(bias_hi, 2)
                pe.wait_ge(consts_set, CONSTS)
            if p == 0:
                after(pe, x1_done, g)
            for t in range(TG):
                for i, (rt, wt) in enumerate(((r_h, wp_h), (r_h, wp_l), (r_l, wp_h))):
                    last = nc.tensor.matmul(pj_ps[:, t, :], rt[:, p % 2, t * P:(t + 1) * P], wt[:, p, :],
                                            start=(p == 0 and i == 0 and t % 2 == 0), stop=False, skip_group_check=True)
                if p == NP - 1:
                    for i in range(2):
                        last = nc.tensor.matmul(pj_ps[:, t, :], ones[0:1, :], bias_rows[0:1, i, :],
                                                start=False, stop=(i == 1), skip_group_check=True)
            last.then_inc(pj_mm, 1)

        def x2_transpose(g, par, k):
            pe.wait_ge(ln2_done, g + 1)
            for t in range(TG):
                last = nc.tensor.transpose(job_ps[:, t * P:(t + 1) * P], rec[:, par, 0, t, k * P:(k + 1) * P], ident[:, :])
            last.then_inc(x2_tp, 1)

        def logits(g):
            pe.wait_ge(x2_copied, 2 * g + 2)
            for t in range(TG):
                for k in range(KD):
                    last = nc.tensor.matmul(job_ps[:, t * E:(t + 1) * E], x2t[:, k, t * P:(t + 1) * P], gate_t[:, k, :],
                                            start=(k == 0), stop=(k == KD - 1))
            last.then_inc(lg_mm, 1)

        def positions(g, count=False):
            pe.wait_ge(m_done, g + 1)
            for t in range(TG):
                o = job_ps[:, t * E:(t + 1) * E]
                nc.tensor.matmul(o, ones[:, :], seen_h[:, :], start=True, stop=False)
                for v in range(t):
                    nc.tensor.matmul(o, ones[:, :], mboth[:, v, :], start=False, stop=False)
                last = nc.tensor.matmul(o, before[:, :], mboth[:, t, :], start=False, stop=True)
            if count:
                o = job_ps[:, TG * E:(TG + 1) * E]
                nc.tensor.matmul(o, ones[:, :], seen_h[:, :], start=True, stop=False)
                for v in range(TG):
                    last = nc.tensor.matmul(o, ones[:, :], mboth[:, v, :], start=False, stop=(v == TG - 1))
            last.then_inc(pos_mm, 1)

        def small_job(g, k, p):
            if p == 1 and known(g, 2):
                x2_transpose(g - 2, k, 0)
            if p == 2 and known(g, 2):
                logits(g - 2)
            if p == 4 and known(g, 2):
                positions(g - 2)
            if p == 5 and has_next(g):
                if known(g, 2):
                    pe.wait_ge(pos_read, g - 1)
                elif g == 0:
                    pe.wait_ge(k_lo, p + 1)
                x_transpose(g + 1, 0, job_ps)
            if p == 6 and has_next(g):
                pe.wait_ge(xt_lo, 2 * g + 3)
                if isinstance(g, int) and g == 0:
                    pe.wait_ge(k_lo, p + 1)
                x_transpose(g + 1, 1, job_ps)

        def step(b, g, k, p, pairs_back=LAST):
            n = pair_no(g, p)

            def back(lag):
                if p >= lag:
                    return b, g, p - lag
                return (b if k else b - 1), g - 1, p - lag + NP
            project_q(g, p, k)
            if isinstance(g, int) and g == 0:
                project_k(p)
            if pairs_back >= 1:
                scores(back(1)[0], n - 1, back(1)[2])
            if p == 2 and known(g, 2):
                pe.wait_ge(x2_copied, 2 * g - 3)
                x2_transpose(g - 2, k, 1)
            if pairs_back >= 4:
                transpose_probs(n - 4, back(4)[2])
            if isinstance(g, int) and g == 0 and p < 4:
                transpose_wp(p)
            if isinstance(g, int) and g == 0 and 1 <= p <= B:
                project_v(p - 1)
            if pairs_back >= 5:
                probs_v(back(5)[0], n - 5, back(5)[2])
            if pairs_back >= 6:
                project_out(back(6)[1], n - 6, back(6)[2])
            small_job(g, k, p)

        for k in range(GB):
            for p in range(NP):
                step(0, k, k, p, pairs_back=min(LAST, k * NP + p))
        with pe.Fori(1, B - 1) as b:
            for k in range(GB):
                for p in range(NP):
                    step(b, b * GB + k, k, p)
        for k in range(GB):
            for p in range(NP):
                step(B - 1, NG - GB + k, k, p)
        for p in range(LAST):
            n = NS + p
            if p < 1:
                scores(B - 1, n - 1, NP + p - 1)
            if p < 4:
                transpose_probs(n - 4, NP + p - 4)
            if p < 5:
                probs_v(B - 1, n - 5, NP + p - 5)
            project_out(NG - 1, n - 6, NP + p - 6)
            if p == 1:
                pe.wait_ge(pos_read, NG - 2)
                x2_transpose(NG - 2, 0, 0)
            if p == 2:
                pe.wait_ge(x2_copied, 2 * NG - 3)
                x2_transpose(NG - 2, 0, 1)
                logits(NG - 2)
            if p == 4:
                positions(NG - 2)
        pe.wait_ge(pos_read, NG - 1)
        for k in range(KD):
            after(pe, x2_copied, 2 * NG - 2 + k)
            x2_transpose(NG - 1, 1, k)
        logits(NG - 1)
        positions(NG - 1, count=True)

    @block.scalar
    def _(act):
        act.wait_ge(consts_set, 1)
        nc.scalar.activation(esum[:, 0, 0, 0:1], ident[:, 0:1], ACT.Exp)

        def ln1_apply(g, par, tiles=range(TG)):
            if tiles[0] == 0:
                act.wait_ge(ln1_shift, g)
                after(act, xt_tp, 2 * g)
            for t in tiles:
                last = nc.scalar.activation(xn[:, t, :], xin[:, par, t, :], ACT.Identity, bias=shift[:, 0, t:t + 1], scale=rstd[:, 0, t:t + 1])
            if tiles[-1] == TG - 1:
                last.then_inc(xn_done, 1)

        def split_x(g, par, k, bank):
            act.wait_ge(xt_tp, 2 * g + k + 1)
            if known(g, 2):
                act.wait_ge(q_mm, pair_no(g - 2, NP))
            nc.scalar.copy(xt_h[:, par, k, :], bank[:, :]).then_inc(xt_hi, 1)

        def split_wq(half):
            for k in range(KD):
                last = nc.scalar.mul(heads_of(wq_h, k, half), w_chunk(wq_sb, k, half * H // 2, H // 2), WS)
            last.then_inc(wq_hi, 1)

        act.wait_ge(ctx_tp, 1)
        for c in range(2):
            nc.scalar.copy(ctx_t[:, :, :, c, :], s_ps[:].rearrange("p t h m -> p (t h m)").rearrange(
                "p (k b m) -> p k b m", k=KD, b=B)).then_inc(ctx_copied, 1)
        act.wait_ge(wq_in, 16)
        split_wq(0)
        for k in range(KD):
            split_x(0, 0, k, q_ps[k])
        split_wq(1)
        act.wait_ge(gate_tp, 1)
        nc.scalar.copy(gate_t[:, :, :], ot_ps[:, 0:KD * E].rearrange("p (k e) -> p k e", k=KD)).then_inc(gate_copied, 1)
        act.wait_ge(bias_in, 16)
        nc.scalar.mul(bias_rows[:, 0, :], bias_sb[:, :], WS).then_inc(bias_hi, 1)

        def split_k(p):
            act.wait_ge(k_mm, p + 1)
            if p == 0:
                act.wait_ge(k_zeroed, 2)
            for h in range(2):
                r = slice(h * M, (h + 1) * M)
                last = nc.scalar.copy(kb_h[r, :, p, r], job_ps[r, 0:B * M].rearrange("p (b m) -> p b m", b=B))
            last.then_inc(k_hi, 1)

        def split_v(b):
            if b == 0:
                act.wait_ge(v_zeroed, 2)
            for half in range(2):
                act.wait_ge(v_mm, 2 * b + half + 1)
                for h in range(2):
                    r = slice(h * M, (h + 1) * M)
                    last = nc.scalar.copy(vb_h[r, b, half * TG:half * TG + TG, h, :],
                                          pj_ps[r, 2 * half:2 * half + 2, :].rearrange("p a (q h j) -> p (a q) h j", q=2, h=2)[:, :, h, :])
                last.then_inc(v_hi, 1)

        def split_wp(part):
            act.wait_ge(wp_tp, part + 1)
            nc.scalar.mul(wp_h[:, 2 * part:2 * part + 2, :], ot_ps[:, :].rearrange("p (q d) -> p q d", q=2), WS).then_inc(wp_hi, 1)

        def copy_q(n, p):
            act.wait_ge(q_mm, n + 1)
            if isinstance(n, int) and n == 0:
                act.wait_ge(wq_lo, 2)
            if isinstance(n, int) and n == 4:
                act.wait_ge(wp_lo, 4)
            after(act, r_mul, n - NP + 1)
            nc.scalar.mul(q32[:, p, :], q_ps[p % 2][:, :], 1.0 / WS).then_inc(q_sb, 1)
            after(act, s_mm, n - 1)
            nc.scalar.mul(q_h[:, p % 2, :], q_ps[p % 2][:, :], 1.0 / WS).then_inc(q_hi, 1)

        def probs_hi(n, p):
            act.wait_ge(pt_mm, n + 1)
            after(act, ot_mm, n - 1)
            nc.scalar.mul(e_h[:, p % 2, :], pt_ps[:, :], PS).then_inc(e_hi, 1)

        def exps(n, p):
            act.wait_ge(s_sub, n + 1)
            after(act, p_nrm, n - 1)
            nc.scalar.activation(ex[:, p % 2].rearrange("p t m -> p (t m)"),
                                 ssub[:, p % 2].rearrange("p t h m -> p (t h m)"), ACT.Exp).then_inc(e_x, 1)

        def product_hi(n, p):
            act.wait_ge(r_mul, n + 1)
            after(act, pj_mm, n - 1)
            nc.scalar.copy(r_h[:, p % 2, :], r32[:, p % 2, :]).then_inc(r_hi, 1)

        def x2_copy(g, k):
            act.wait_ge(x2_tp, 2 * g + k + 1)
            if k == 0:
                after(act, lg_mm, g)
            nc.scalar.copy(x2t[:, k, :], job_ps[:, :]).then_inc(x2_copied, 1)

        def exp_delta(g):
            act.wait_ge(top_done, g + 1)
            nc.scalar.activation(edelta[:, :], delta[:, :], ACT.Exp).then_inc(ed_done, 1)

        def ln2_apply(g, par, scattered, tiles=range(TG)):
            if tiles[0] == 0:
                act.wait_ge(ln2_shift, g + 1)
                after(act, records_in[par], scattered)
            for t in tiles:
                last = nc.scalar.activation(rec[:, par, 0, t, 0:D], xres[:, par, t, :], ACT.Identity,
                                            bias=shift[:, 1, t:t + 1], scale=rstd[:, 1, t:t + 1])
            if tiles[-1] == TG - 1:
                last.then_inc(ln2_done, 1)

        def second_record(g, par):
            act.wait_ge(ln2_done, g + 1)
            nc.scalar.copy(rec[:, par, 1, :, 0:D], rec[:, par, 0, :, 0:D]).then_inc(rec_done, 1)

        def expert_hi(e, i):
            half = 2 * i // WC
            act.wait_ge(stage_in[half], 16 * e + 16)
            if known(e, HELD + 1):
                act.wait_ge(split_stored[half], 16 * (e - HELD))
            c = slice(i * WN // WC, (i + 1) * WN // WC)
            dst = weights[:, e] if isinstance(e, int) and e < HELD else split
            nc.scalar.mul(dst[:, 0, c], stage[:, c], WS).then_inc(split_hi, 1)

        def step(b, g, k, p, pairs_back=LAST):
            n = pair_no(g, p)
            first = isinstance(g, int) and g == 0
            if p == 2 and known(g, 2):
                x2_copy(g - 2, 0)
            if p in (6, 7) and has_next(g):
                split_x(g + 1, 1 - k, p - 6, job_ps)
            copy_q(n, p)
            if first:
                split_k(p)
            if p == 2 and known(g, 2):
                x2_copy(g - 2, 1)
            if pairs_back >= 4:
                probs_hi(n - 4, (p - 4) % NP)
            if first and p < 4:
                split_wp(p)
            if first and 1 <= p <= B:
                split_v(p - 1)
            if pairs_back >= 2:
                exps(n - 2, (p - 2) % NP)
            if p == 0 and known(g, 2):
                ln2_apply(g - 2, k, 16 + 32 * TG * (b - 1), range(TG // 2))
            if p == 1 and known(g, 2):
                ln2_apply(g - 2, k, 0, range(TG // 2, TG))
            if p == 4 and has_next(g):
                ln1_apply(g + 1, 1 - k, range(TG // 2))
            if p == 5 and has_next(g):
                ln1_apply(g + 1, 1 - k, range(TG // 2, TG))
            for i in pieces(g, p):
                expert_hi(g, i)
            if pairs_back >= 5:
                product_hi(n - 5, (p - 5) % NP)
            if p == 2 and known(g, 2):
                second_record(g - 2, k)
            if p == 4 and known(g, 2):
                exp_delta(g - 2)

        for k in range(GB):
            for p in range(NP):
                step(0, k, k, p, pairs_back=min(LAST, k * NP + p))
            if k == 0:
                act.wait_ge(gain_in, 32)
                nc.scalar.activation(tanhs[:, :], tanhs[:, :], ACT.Tanh).then_inc(tanh_done, 1)
        with act.Fori(1, B - 1) as b:
            for k in range(GB):
                for p in range(NP):
                    step(b, b * GB + k, k, p)
        for k in range(GB):
            for p in range(NP):
                step(B - 1, NG - GB + k, k, p)
        for p in range(LAST):
            n = NS + p
            if p == 2:
                x2_copy(NG - 2, 0)
                x2_copy(NG - 2, 1)
            if p < 4:
                probs_hi(n - 4, NP + p - 4)
            if p < 2:
                exps(n - 2, NP + p - 2)
            if p == 0:
                ln2_apply(NG - 2, 0, 16 + 32 * TG * (B - 1))
            if p < 5:
                product_hi(n - 5, NP + p - 5)
            if p == 2:
                second_record(NG - 2, 0)
            if p == 4:
                exp_delta(NG - 2)
        ln2_apply(NG - 1, 1, 16 + 32 * TG * (B - 1))
        for k in range(KD):
            x2_copy(NG - 1, k)
        second_record(NG - 1, 1)
        exp_delta(NG - 1)

    @block.vector
    def _(dve):
        for i, t in enumerate((kb_h, kb_l)):
            nc.vector.memset(t[:].rearrange("p b n m -> p (b n m)").bitcast(U32), 0).then_inc(k_zeroed, 1)
        nc.vector.memset(seen[:, :], 0.0)
        nc.vector.memset(seen_h[:, :], 0.0)

        def ln1(g, par):
            dve.wait_ge(x_in[par], 16 * (g // 2) + 16 if isinstance(g, int) else g)
            for t in range(TG):
                last = nc.vector.bn_stats(stats[:, 0, t, :], xin[:, par, t, :])
            last.then_inc(ln1_ops, 1)

        def ln1_moments(g):
            dve.wait_ge(ln1_ops, 3 * g + 1)
            after(dve, xn_done, g)
            nc.vector.memset(vare[:, 0, :], EPS)
            for t in range(TG):
                last = nc.vector.bn_aggr(mv[:, 0, t, :], stats[:, 0, t, :])
            last.then_inc(ln1_ops, 1)
            dve.wait_ge(ln1_ops, 3 * g + 2)
            nc.vector.tensor_tensor(vare[:, 0, :], vare[:, 0, :], mv[:, 0, :, 1], ALU.add).then_inc(ln1_ops, 1)

        def ln1_shift_of(g):
            dve.wait_ge(ln1_rstd, g + 1)
            nc.vector.scalar_tensor_tensor(shift[:, 0, :], mv[:, 0, :, 0], -1.0, rstd[:, 0, :], ALU.mult, ALU.mult).then_inc(ln1_shift, 1)

        def split_x(g, par, k, bank):
            dve.wait_ge(xt_hi, 2 * g + k + 1)
            nc.vector.tensor_tensor(xt_l[:, par, k, :], bank[:, :], xt_h[:, par, k, :], ALU.subtract).then_inc(xt_lo, 1)

        def split_wq(half):
            dve.wait_ge(wq_hi, half + 1)
            for k in range(KD):
                last = nc.vector.scalar_tensor_tensor(heads_of(wq_l, k, half), w_chunk(wq_sb, k, half * H // 2, H // 2), WS,
                                                      heads_of(wq_h, k, half), ALU.mult, ALU.subtract)
            last.then_inc(wq_lo, 1)

        ln1(0, 0)
        ln1_moments(0)
        dve.wait_ge(ln1_rstd, 1)
        for t in range(TG):
            last = nc.vector.tensor_scalar(xn[:, t, :], xin[:, 0, t, :], mv[:, 0, t, 0:1], rstd[:, 0, t:t + 1], ALU.subtract, ALU.mult)
        last.then_inc(xn_done, 1)
        split_wq(0)
        for k in range(KD):
            split_x(0, 0, k, q_ps[k])
        split_wq(1)
        dve.wait_ge(wk_in, 16)
        for k in range(KD):
            last = nc.vector.tensor_copy(wk_cols[:, k].rearrange("p (h j) -> p h j", h=H), w_chunk(wk_sb, k, 0, H))
        last.then_inc(wk_laid, 1)
        dve.wait_ge(bias_hi, 1)
        nc.vector.scalar_tensor_tensor(bias_rows[:, 1, :], bias_sb[:, :], WS, bias_rows[:, 0, :],
                                       ALU.mult, ALU.subtract).then_inc(bias_hi, 1)

        def split_k(p):
            dve.wait_ge(k_hi, p + 1)
            for h in range(2):
                r = slice(h * M, (h + 1) * M)
                last = nc.vector.tensor_tensor(kb_l[r, :, p, r], job_ps[r, 0:B * M].rearrange("p (b m) -> p b m", b=B),
                                               kb_h[r, :, p, r], ALU.subtract)
            last.then_inc(k_lo, 1)

        def split_v(b):
            for half in range(2):
                dve.wait_ge(v_hi, 2 * b + half + 1)
                for h in range(2):
                    r = slice(h * M, (h + 1) * M)
                    c = slice(half * TG, half * TG + TG)
                    last = nc.vector.tensor_tensor(vb_l[r, b, c, h, :],
                                                   pj_ps[r, 2 * half:2 * half + 2, :].rearrange("p a (q h j) -> p (a q) h j", q=2, h=2)[:, :, h, :],
                                                   vb_h[r, b, c, h, :], ALU.subtract)
                last.then_inc(v_lo, 1)

        def split_wp(part):
            dve.wait_ge(wp_hi, part + 1)
            nc.vector.scalar_tensor_tensor(wp_l[:, 2 * part:2 * part + 2, :], ot_ps[:, :].rearrange("p (q d) -> p q d", q=2), WS,
                                           wp_h[:, 2 * part:2 * part + 2, :], ALU.mult, ALU.subtract).then_inc(wp_lo, 1)

        def score_max(n, p):
            dve.wait_ge(s_mm, n + 1)
            nc.vector.tensor_reduce(smax[:, p % 2], s_ps[:, :, :, :], AX.X, ALU.max).then_inc(s_max, 1)

        def score_sub(n, p):
            dve.wait_ge(s_max, n + 1)
            after(dve, e_x, n - 1)
            nc.vector.tensor_tensor(ssub[:, p % 2], s_ps[:, :, :, :],
                                    smax[:, p % 2].unsqueeze(3).broadcast_to([P, TG, 2, M]), ALU.subtract).then_inc(s_sub, 1)

        def exp_sum(n, p):
            dve.wait_ge(e_x, n + 1)
            nc.vector.tensor_reduce(esum[:, p % 2], ex[:, p % 2].rearrange("p t (h m) -> p t h m", h=2), AX.X, ALU.add).then_inc(e_sum, 1)
            dve.wait_ge(e_sum, n + 1)
            after(dve, p_nrm, n - 1)
            nc.vector.reciprocal(rinv[:, p % 2], esum[:, p % 2]).then_inc(e_inv, 1)

        def probs_lo(n, p):
            dve.wait_ge(e_hi, n + 1)
            nc.vector.scalar_tensor_tensor(e_l[:, p % 2, :], pt_ps[:, :], PS, e_h[:, p % 2, :], ALU.mult, ALU.subtract).then_inc(e_lo, 1)

        def times_q(n, p):
            dve.wait_ge(ot_mm, n + 1)
            dve.wait_ge(q_sb, n + 1)
            after(dve, r_lo, n - 1)
            nc.vector.scalar_tensor_tensor(r32[:, p % 2, :], ot_ps[:, :], 1.0 / PS, q32[:, p, :], ALU.mult, ALU.mult).then_inc(r_mul, 1)

        def residual(g, par):
            dve.wait_ge(pj_mm, pair_no(g, NP))
            dve.wait_ge(xres_in[par], 16 * (g // 2) + 16 if isinstance(g, int) else g)
            nc.vector.scalar_tensor_tensor(xres[:, par], pj_ps[:, :, :], gains[:, 0:1], xres[:, par],
                                           ALU.mult, ALU.add).then_inc(x1_done, 1)

        def ln2(g, par):
            dve.wait_ge(x1_done, g + 1)
            for t in range(TG):
                last = nc.vector.bn_stats(stats[:, 1, t, :], xres[:, par, t, :])
            last.then_inc(ln2_ops, 1)
            dve.wait_ge(ln2_ops, 3 * g + 1)
            nc.vector.memset(vare[:, 1, :], EPS)
            for t in range(TG):
                last = nc.vector.bn_aggr(mv[:, 1, t, :], stats[:, 1, t, :])
            last.then_inc(ln2_ops, 1)
            dve.wait_ge(ln2_ops, 3 * g + 2)
            nc.vector.tensor_tensor(vare[:, 1, :], vare[:, 1, :], mv[:, 1, :, 1], ALU.add).then_inc(ln2_ops, 1)

        def ln2_shift_of(g):
            dve.wait_ge(ln2_rstd, g + 1)
            nc.vector.scalar_tensor_tensor(shift[:, 1, :], mv[:, 1, :, 0], -1.0, rstd[:, 1, :], ALU.mult, ALU.mult).then_inc(ln2_shift, 1)

        def expert_lo(e, i):
            dve.wait_ge(split_hi, WC * e + i + 1)
            c = slice(i * WN // WC, (i + 1) * WN // WC)
            dst = weights[:, e] if isinstance(e, int) and e < HELD else split
            nc.vector.scalar_tensor_tensor(dst[:, 1, c], stage[:, c], WS, dst[:, 0, c], ALU.mult, ALU.subtract).then_inc(split_lo, 1)

        def over_e(a):
            return a.unsqueeze(2).broadcast_to([P, TG, E])

        def choose(g, c):
            done = g * ROUTE + 6 * c

            def link(ins, i):
                ins.then_inc(route_ops, 1)
                dve.wait_ge(route_ops, done + i)

            if c == 0:
                dve.wait_ge(lg_mm, g + 1)
                nc.vector.tensor_copy(lg[:, :, :], job_ps[:, 0:TG * E].rearrange("p (t e) -> p t e", t=TG)).then_inc(lg_read, 1)
                dve.wait_ge(lg_read, g + 1)
            src = lg2 if c else lg
            link(nc.vector.tensor_reduce(top[:, c, :], src[:, :, :], AX.X, ALU.max), 1)
            link(nc.vector.tensor_tensor(cand[:, :, :], src[:, :, :], over_e(top[:, c, :]), ALU.is_lt), 2)
            link(nc.vector.scalar_tensor_tensor(cand[:, :, :], cand[:, :, :], float(E), iota_e[:, :, :], ALU.mult, ALU.add), 3)
            link(nc.vector.tensor_reduce(choice[:, c, :], cand[:, :, :], AX.X, ALU.min), 4)
            link(nc.vector.tensor_tensor(mask[:, c], iota_e[:, :, :], over_e(choice[:, c, :]), ALU.is_equal), 5)
            if c == 0:
                link(nc.vector.scalar_tensor_tensor(lg2[:, :, :], mask[:, 0], -BIG, lg[:, :, :], ALU.mult, ALU.add), 6)
            else:
                nc.vector.tensor_tensor(delta[:, :], top[:, 1, :], top[:, 0, :], ALU.subtract).then_inc(top_done, 1)
                nc.vector.tensor_tensor(mboth[:, :, :], mask[:, 0], mask[:, 1], ALU.add).then_inc(m_done, 1)

        def place(g, par):
            done = g * ROUTE
            dve.wait_ge(pos_mm, g + 1)
            nc.vector.tensor_tensor(pos[:, :, :], job_ps[:, 0:TG * E].rearrange("p (t e) -> p t e", t=TG), e_off[:, :, :],
                                    ALU.add).then_inc(pos_read, 1)
            dve.wait_ge(ed_done, g + 1)
            nc.vector.tensor_scalar(wsum[:, :], edelta[:, :], 1.0, None, ALU.add).then_inc(route_ops, 1)
            nc.vector.tensor_reduce(mtiles[:, :], mboth[:, :, :].rearrange("p t e -> p e t"), AX.X, ALU.add).then_inc(route_ops, 1)
            dve.wait_ge(pos_read, g + 1)
            for c in range(2):
                nc.vector.tensor_tensor(mask[:, c], pos[:, :, :], mask[:, c], ALU.mult).then_inc(route_ops, 1)
            dve.wait_ge(route_ops, done + 13)
            nc.vector.reciprocal(wfirst[:, :], wsum[:, :]).then_inc(route_ops, 1)
            nc.vector.tensor_tensor(seen[:, :], seen[:, :], mtiles[:, :], ALU.add).then_inc(route_ops, 1)
            dve.wait_ge(route_ops, done + 15)
            with nc.allow_low_precision(reason="one term of each sum is not zero: a row number, exact in float32"):
                for c in range(2):
                    nc.vector.tensor_reduce(slot[:, par, c, :], mask[:, c], AX.X, ALU.add)
            dve.wait_ge(route_ops, done + 17)
            nc.vector.tensor_copy(seen_h[:, :], seen[:, :])
            nc.vector.tensor_scalar(rec[:, par, 0, :, D + 1], wfirst[:, :], gains[:, 1:2], None, ALU.mult)
            nc.vector.scalar_tensor_tensor(rec[:, par, 1, :, D + 1], wfirst[:, :], gains[:, 1:2], edelta[:, :], ALU.mult, ALU.mult)
            for c in range(2):
                nc.vector.tensor_copy(rec[:, par, c, :, D].bitcast(U32), tok_ids[:, :])
            nc.vector.tensor_scalar(tok_ids[:, :], tok_ids[:, :], float(G), None, ALU.add).then_inc(slots_done, 1)

        def step(b, g, k, p, pairs_back=LAST):
            n = pair_no(g, p)
            first = isinstance(g, int) and g == 0
            if p == 6 and known(g, 1):
                residual_of(b, g, k)
            if pairs_back >= 3:
                exp_sum(n - 3, (p - 3) % NP)
            if p == 4 and has_next(g):
                ln1_shift_of(g + 1)
            if p == 1 and has_next(g):
                ln1_of(b, g, k)
            if p == 2 and has_next(g):
                ln1_moments(g + 1)
            if p == 7 and known(g, 1):
                ln2(g - 1, 1 - k)
            if p in (6, 7) and has_next(g):
                split_x(g + 1, 1 - k, p - 6, job_ps)
            if first:
                split_k(p)
            if p in (3, 4) and known(g, 2):
                choose(g - 2, p - 3)
            if p == 5 and known(g, 2):
                place(g - 2, k)
            if pairs_back >= 1:
                score_max(n - 1, (p - 1) % NP)
                score_sub(n - 1, (p - 1) % NP)
            if pairs_back >= 4:
                probs_lo(n - 4, (p - 4) % NP)
            if first and p < 4:
                split_wp(p)
            if first and 1 <= p <= B:
                split_v(p - 1)
            if pairs_back >= 5:
                times_q(n - 5, (p - 5) % NP)
            for i in pieces(g, p):
                expert_lo(g, i)
            if p == 7 and known(g, 1):
                ln2_shift_of(g - 1)

        def ln1_of(b, g, k):
            if isinstance(b, int):
                ln1(g + 1, 1 - k)
                return
            par = 1 - k
            dve.wait_ge(x_in[par], (b + k) * 16 + 16)
            for t in range(TG):
                last = nc.vector.bn_stats(stats[:, 0, t, :], xin[:, par, t, :])
            last.then_inc(ln1_ops, 1)

        def residual_of(b, g, k):
            if isinstance(b, int):
                residual(g - 1, 1 - k)
                return
            par = 1 - k
            dve.wait_ge(pj_mm, pair_no(g - 1, NP))
            dve.wait_ge(xres_in[par], (b + k) * 16)
            nc.vector.scalar_tensor_tensor(xres[:, par], pj_ps[:, :, :], gains[:, 0:1], xres[:, par],
                                           ALU.mult, ALU.add).then_inc(x1_done, 1)

        for k in range(GB):
            for p in range(NP):
                step(0, k, k, p, pairs_back=min(LAST, k * NP + p))
            if k == 0:
                dve.wait_ge(tanh_done, 1)
                nc.vector.tensor_scalar(gains[:, :], tanhs[:, :], 1.0 / WS, None, ALU.mult).then_inc(setup_ops, 1)
                dve.wait_ge(setup_ops, 1)
        with dve.Fori(1, B - 1) as b:
            for k in range(GB):
                for p in range(NP):
                    step(b, b * GB + k, k, p)
        for k in range(GB):
            for p in range(NP):
                step(B - 1, NG - GB + k, k, p)
        for p in range(LAST):
            n = NS + p
            if p < 3:
                exp_sum(n - 3, NP + p - 3)
            if p < 1:
                score_max(n - 1, NP + p - 1)
                score_sub(n - 1, NP + p - 1)
            if p in (3, 4):
                choose(NG - 2, p - 3)
            if p == 5:
                place(NG - 2, 0)
            if p < 4:
                probs_lo(n - 4, NP + p - 4)
            if p < 5:
                times_q(n - 5, NP + p - 5)
        residual(NG - 1, 1)
        ln2(NG - 1, 1)
        ln2_shift_of(NG - 1)
        choose(NG - 1, 0)
        choose(NG - 1, 1)

        dve.wait_ge(pos_mm, NG)
        counts = job_ps[0:1, TG * E:(TG + 1) * E]
        nc.vector.tensor_copy(count1[:, :], counts).then_inc(table_ops, 1)
        nc.vector.tensor_tensor(pad_first[:, :], counts, e_off[0:1, 0, :], ALU.add).then_inc(pad_slots, 1)
        place(NG - 1, 1)
        dve.wait_ge(table_ops, 1)

        def link(ins, i):
            ins.then_inc(table_ops, 1)
            dve.wait_ge(table_ops, i)

        link(nc.vector.tensor_tensor(under[:, :, :], steps_128[:, :, :], count1[:, :].unsqueeze(2).broadcast_to([1, E, T // P]), ALU.is_lt), 2)
        link(nc.vector.tensor_reduce(blocks[:, :], under[:, :, :], AX.X, ALU.add), 3)
        link(nc.vector.tensor_tensor(cum[:, :, :], upto[:, :, :], blocks[:, :].unsqueeze(1).broadcast_to([1, E, E]), ALU.mult), 4)
        link(nc.vector.tensor_reduce(ends[:, :], cum[:, :, :], AX.X, ALU.add), 5)
        link(nc.vector.tensor_tensor(past[:, :, :], block_no[:, :, :], ends[:, :].unsqueeze(1).broadcast_to([1, NB, E]), ALU.is_ge), 6)
        link(nc.vector.tensor_reduce(blk_e[:, :], past[:, :, :], AX.X, ALU.add), 7)
        link(nc.vector.tensor_tensor(past[:, :, :], past[:, :, :], blocks[:, :].unsqueeze(1).broadcast_to([1, NB, E]), ALU.mult), 8)
        link(nc.vector.tensor_reduce(blk_s[:, :], past[:, :, :], AX.X, ALU.add), 9)
        link(nc.vector.tensor_tensor(blk_s[:, :], block_no[:, :, 0], blk_s[:, :], ALU.subtract), 10)
        link(nc.vector.tensor_scalar(blk_s[:, :], blk_s[:, :], float(P), None, ALU.mult), 11)
        link(nc.vector.scalar_tensor_tensor(blk_s[:, :], blk_e[:, :], float(REGION), blk_s[:, :], ALU.mult, ALU.add), 12)
        nc.vector.tensor_scalar(table[:, NB:2 * NB], blk_s[:, :], float(E * REGION), None, ALU.min).then_inc(table_ops, 1)
        nc.vector.tensor_scalar(table[:, 0:NB], blk_e[:, :], float(E - 1), None, ALU.min).then_inc(table_ops, 1)
        dve.wait_ge(table_ops, 14)

    @block.gpsimd
    def _(pool):
        nc.gpsimd.memset(ident[:, :], 0.0).then_inc(base_set, 1)
        nc.gpsimd.memset(ones[:, :], 1.0).then_inc(base_set, 1)
        nc.gpsimd.memset(before[:, :], 1.0).then_inc(base_set, 1)
        nc.gpsimd.memset(upto[:, :, :], 1.0).then_inc(base_set, 1)
        nc.gpsimd.memset(pad_rec[:, :], 0.0).then_inc(base_set, 1)
        pool.wait_ge(base_set, 5)
        nc.gpsimd.affine_select(out=ident[:, :], in_=ident[:, :], compare_op=ALU.not_equal, fill=1.0, base=0,
                                pattern=[[-1, P]], channel_multiplier=1).then_inc(consts_set, 1)
        nc.gpsimd.affine_select(out=before[:, :], in_=before[:, :], compare_op=ALU.is_gt, fill=0.0, base=0,
                                pattern=[[1, P]], channel_multiplier=-1).then_inc(consts_set, 1)
        nc.gpsimd.affine_select(out=upto[:, :, :], in_=upto[:, :, :], compare_op=ALU.is_ge, fill=0.0, base=0,
                                pattern=[[1, E], [-1, E]], channel_multiplier=0).then_inc(consts_set, 1)
        nc.gpsimd.memset(minus_half[:, :], -0.5).then_inc(consts_set, 1)

        def ln_rstd(i, g, ops, done):
            pool.wait_ge(ops, 3 * g + 3)
            nc.gpsimd.tensor_tensor(rstd[:, i, :], vare[:, i, :], minus_half[:, :], ALU.pow).then_inc(done, 1)

        def count_up(dst, pattern, channel):
            nc.gpsimd.iota(dst, pattern=pattern, base=0, channel_multiplier=channel,
                           allow_small_or_imprecise_dtypes=True).then_inc(consts_set, 1)

        pool.wait_ge(consts_set, 4)
        ln_rstd(0, 0, ln1_ops, ln1_rstd)
        for t in (vb_h, vb_l):
            nc.gpsimd.memset(t[:].rearrange("p b n h w -> p (b n h w)").bitcast(U32), 0).then_inc(v_zeroed, 1)
        nc.gpsimd.iota(pad_rec[:, D:D + 1].bitcast(U32), pattern=[[0, 1]], base=T, channel_multiplier=1).then_inc(consts_set, 1)
        nc.gpsimd.iota(spare_slot[:, :], pattern=[[0, 1]], base=E * REGION, channel_multiplier=1).then_inc(consts_set, 1)
        count_up(iota_e[:, :, :], [[0, TG], [1, E]], 0)
        count_up(e_off[:, :, :], [[0, TG], [REGION, E]], 0)
        count_up(tok_ids[:, :], [[1, TG]], TG)
        count_up(steps_128[:, :, :], [[0, E], [P, T // P]], 0)
        count_up(block_no[:, :, :], [[1, NB], [0, E]], 0)
        nc.gpsimd.memset(wait_mark[:, :], 0.0).then_inc(consts_set, 1)

        def split_q(n, p):
            pool.wait_ge(q_hi, n + 1)
            nc.gpsimd.tensor_tensor(q_l[:, p % 2, :], q32[:, p, :], q_h[:, p % 2, :], ALU.subtract).then_inc(q_lo, 1)

        def normalize(n, p):
            pool.wait_ge(e_inv, n + 1)
            after(pool, pt_mm, n - 1)
            nc.gpsimd.tensor_tensor(pn[:, p % 2].rearrange("p t (h m) -> p t h m", h=2), ex[:, p % 2].rearrange("p t (h m) -> p t h m", h=2),
                                    rinv[:, p % 2].unsqueeze(3).broadcast_to([P, TG, 2, M]), ALU.mult).then_inc(p_nrm, 1)

        def product_lo(n, p):
            pool.wait_ge(r_hi, n + 1)
            nc.gpsimd.tensor_tensor(r_l[:, p % 2, :], r32[:, p % 2, :], r_h[:, p % 2, :], ALU.subtract).then_inc(r_lo, 1)

        def scatter(g, par, i):
            if i == 0:
                pool.wait_ge(slots_done, g + 1)
                pool.wait_ge(rec_done, g + 1)
                nc.gpsimd.tensor_tensor(wait_mark[:, 1:2], wait_mark[:, 0:1], wait_mark[:, 0:1], ALU.add)
            c, t = i // TG, i % TG
            pool.indirect_dma_start(records, bass.IndirectOffsetOnAxis(slot[:, par, c, t:t + 1], 0),
                                    rec[:, par, c, t, :], None).then_inc(records_in[par], 16)

        def step(g, k, p, pairs_back=LAST):
            n = pair_no(g, p)
            if pairs_back >= 3:
                normalize(n - 3, (p - 3) % NP)
            split_q(n, p)
            if p == 3 and has_next(g):
                ln_rstd(0, g + 1, ln1_ops, ln1_rstd)
            if p == 7 and known(g, 1):
                ln_rstd(1, g - 1, ln2_ops, ln2_rstd)
            if p >= 5 and known(g, 2):
                scatter(g - 2, k, p - 5)
            if p < 5 and known(g, 3):
                scatter(g - 3, 1 - k, p + 3)
            if pairs_back >= 5:
                product_lo(n - 5, (p - 5) % NP)

        for g in range(GB + 1):
            for p in range(NP):
                step(g, g % 2, p, pairs_back=min(LAST, g * NP + p))
                if g == 0 and p == 2:
                    pool.wait_ge(consts_set, CONSTS)
                    pool.indirect_dma_start(dram["out"], bass.IndirectOffsetOnAxis(pad_rec[:, D:D + 1].bitcast(U32), 0), pad_rec[:, 0:D],
                                            None).then_inc(records_in[0], 16)
                    pool.indirect_dma_start(records, bass.IndirectOffsetOnAxis(spare_slot[:, :], 0), pad_rec[:, :],
                                            None).then_inc(records_in[1], 16)
        with pool.Fori(1, B - 1) as b:
            for k in range(GB):
                for p in range(NP):
                    step(b * GB + 1 + k, (1 + k) % 2, p)
        for p in range(NP):
            step(NG - 1, 1, p)
        for p in range(LAST - 1):
            if p < 3:
                normalize(NS + p - 3, NP + p - 3)
            product_lo(NS + p - 5, NP + p - 5)
            scatter(NG - 3, 1, p + 3)
        for i in range(2 * TG):
            scatter(NG - 2, 0, i)
            if i == 3:
                ln_rstd(1, NG - 1, ln2_ops, ln2_rstd)
        for i in range(2 * TG):
            scatter(NG - 1, 1, i)
        for par in range(2):
            pool.wait_ge(records_in[par], 16 + 32 * TG * B)


def experts(nc, ctx, dram, ident, table, loads_base, weights):
    records, out = dram["records"], dram["out"]

    def sb(name, shape, dt):
        return ctx.enter_context(nc.sbuf_tensor(name, shape, dt))

    def psum(name, shape):
        return ctx.enter_context(nc.psum_tensor(name, shape, F32))

    def sem(name):
        return ctx.enter_context(nc.semaphore(name))

    RB = 4
    sb("weights_rest", [P, E - HELD, 2, WN], F16)
    rows = sb("rows", [P, RB, ROW], F32)
    meta = sb("meta", [P, RB, 2], F32)
    xt_h, xt_l = (sb(f"bx_{s}", [P, 2, KD, P], F16) for s in "hl")
    w1_now = sb("w1_now", [P, 2, 2, KD * F], F16)
    hid = sb("hid", [P, 2, FC, P], F32)
    ht_h, ht_l = (sb(f"ht_{s}", [P, 2, FC, P], F16) for s in "hl")
    y = sb("y", [P, 2, D], F32)
    wait_mark = sb("b_wait_mark", [P, 2], F32)

    xt_ps = psum("bxt_ps", [P, 4, P])
    h_ps = [psum(f"h_ps{i}", [P, FC, P]) for i in range(2)]
    y_ps = [psum(f"y_ps{i}", [P, 512]) for i in range(2)]

    rows_in = [sem(f"rows_in{i}") for i in range(RB)]
    mark_set = sem("mark_set")
    loads = sem("weight_loads")
    xt_mm, x_hi, x_lo, meta_done, w1_ready, h_mm, h_act, h_hi, h_lo, y_mm, y_out, added = (sem(n) for n in (
        "xt_mm", "x_hi", "x_lo", "meta_done", "w1_ready", "h_mm", "h_act", "h_hi", "h_lo", "y_mm", "y_out", "added"))

    HEAD = RB
    TRIPS = (NB - HEAD - RB) // RB
    TAIL = HEAD + TRIPS * RB

    def run(eng, step):
        for i in range(HEAD):
            step(i, i % RB)
        with eng.Fori(1, 1 + TRIPS) as trip:
            for r in range(RB):
                step(trip * RB + r, r)
        for i in range(TAIL, NB):
            step(i, i % RB)

    def there(i):
        return not isinstance(i, int) or i < NB

    def before_now(i):
        return not isinstance(i, int) or i >= 0

    def expert_of(eng, i):
        return eng.value_load(table[0:1, i:i + 1] if isinstance(i, int) else table[0:1, bass.ds(i, 1)], min_val=0, max_val=E - 1)

    def weights_at(e, s, start, n):
        return weights[:, bass.ds(e, 1), s, start:start + n]

    def block_loads(i, r):
        if isinstance(i, int):
            return 16 * (i // RB + 1)
        return (i - r) * (16 // RB) + 16

    block = ctx.enter_context(nc.Block())

    @block.sync
    def _(sp):
        sp.wait_ge(loads, 1)
        for r in range(RB):
            sp.wait_ge(rows_in[r], 16)
        for e in range(HELD, E):
            sp.dma_start(weights[:, e], dram["w_split"][e]).then_inc(loads, 16)
            sp.wait_ge(loads, 1 + 16 * (e - HELD + 1))

    @block.tensor
    def _(pe):
        def transpose_x(i, r):
            pe.wait_ge(rows_in[r], block_loads(i, r))
            after(pe, x_lo, i)
            for k in range(KD):
                last = nc.tensor.transpose(xt_ps[:, k, :], rows[:, r, k * P:(k + 1) * P], ident[:, :])
            last.then_inc(xt_mm, 1)

        def hidden(i, r):
            pe.wait_ge(x_lo, i + 1)
            after(pe, h_act, i - 1)
            pe.wait_ge(w1_ready, i + 1)
            for c in range(FC):
                for j, (xt, s) in enumerate(((xt_h, 0), (xt_h, 1), (xt_l, 0))):
                    for k in range(KD):
                        last = nc.tensor.matmul(h_ps[r % 2][:, c, :], w1_now[:, r % 2, s, k * F + c * P:k * F + c * P + P],
                                                xt[:, r % 2, k, :],
                                                start=(j == 0 and k == 0), stop=(j == 2 and k == KD - 1))
            last.then_inc(h_mm, 1)

        def down(i, r, e):
            pe.wait_ge(h_lo, i + 1)
            after(pe, y_out, i - 1)
            for c in range(FC):
                for j, (ht, s) in enumerate(((ht_h, 0), (ht_h, 1), (ht_l, 0))):
                    last = nc.tensor.matmul(y_ps[r % 2][:, 0:D], ht[:, r % 2, c, :], weights_at(e, s, WN // 2 + c * D, D).rearrange("p o n -> p (o n)"),
                                            start=(c == 0 and j == 0), stop=(c == FC - 1 and j == 2))
            last.then_inc(y_mm, 1)

        def step(i, r):
            if there(i + 1):
                transpose_x(i + 1, (r + 1) % RB)
            hidden(i, r)
            if before_now(i - 1):
                down(i - 1, (r - 1) % RB, expert_of(pe, i - 1))

        transpose_x(0, 0)
        run(pe, step)
        down(NB - 1, (NB - 1) % RB, expert_of(pe, NB - 1))

    @block.scalar
    def _(act):
        def load_rows(i, r):
            first = act.value_load(table[0:1, NB + i:NB + i + 1] if isinstance(i, int) else table[0:1, bass.ds(i + NB, 1)],
                                   min_val=0, max_val=E * REGION)
            after(act, x_lo, i - RB + 1)
            after(act, meta_done, i - RB + 1)
            act.dma_start(rows[:, r, :], records[bass.ds(first, P), :]).then_inc(rows_in[r], 16)

        def x_high(i, r):
            act.wait_ge(xt_mm, i + 1)
            after(act, h_mm, i - 1)
            nc.scalar.copy(xt_h[:, r % 2], xt_ps[:, 0:KD, :]).then_inc(x_hi, 1)

        def silu(i, r):
            act.wait_ge(h_mm, i + 1)
            after(act, h_lo, i - 1)
            nc.scalar.activation(hid[:, r % 2], h_ps[r % 2][:, :, :], ACT.Silu, scale=1.0 / WS).then_inc(h_act, 1)

        def weigh(i, r):
            act.wait_ge(y_mm, i + 1)
            act.wait_ge(meta_done, i + 1)
            after(act, added, (i - 1) * 16)
            nc.scalar.mul(y[:, r % 2, :], y_ps[r % 2][:, 0:D], meta[:, r, 1:2]).then_inc(y_out, 1)

        def step(i, r):
            if there(i + 1):
                x_high(i + 1, (r + 1) % RB)
            if there(i + RB):
                load_rows(i + RB, r)
            silu(i, r)
            if before_now(i - 1):
                weigh(i - 1, (r - 1) % RB)

        for i in range(RB):
            load_rows(i, i)
        nc.scalar.activation(hid[:, 0, 0, 0:1], ident[:, 0:1], ACT.Silu)
        x_high(0, 0)
        run(act, step)
        weigh(NB - 1, (NB - 1) % RB)

    @block.vector
    def _(dve):
        def x_low(i, r):
            dve.wait_ge(rows_in[r], block_loads(i, r))
            after(dve, added, (i - RB + 1) * 16)
            nc.vector.tensor_copy(meta[:, r, :], rows[:, r, D:D + 2]).then_inc(meta_done, 1)
            dve.wait_ge(x_hi, i + 1)
            nc.vector.tensor_tensor(xt_l[:, r % 2], xt_ps[:, 0:KD, :], xt_h[:, r % 2], ALU.subtract).then_inc(x_lo, 1)

        def take_w1(i, r):
            e = expert_of(dve, i)
            dve.wait_ge(loads, e * 16 + 1)
            after(dve, h_mm, i - 1)
            nc.vector.tensor_copy(w1_now[:, r % 2], weights[:, bass.ds(e, 1), :, 0:KD * F].rearrange("p o s n -> p (o s) n")).then_inc(w1_ready, 1)

        def split_h(i, r):
            dve.wait_ge(h_act, i + 1)
            after(dve, y_mm, i - 1)
            nc.vector.tensor_copy(ht_h[:, r % 2], hid[:, r % 2]).then_inc(h_hi, 1)
            dve.wait_ge(h_hi, i + 1)
            nc.vector.tensor_tensor(ht_l[:, r % 2], hid[:, r % 2], ht_h[:, r % 2], ALU.subtract).then_inc(h_lo, 1)

        def step(i, r):
            if there(i + 1):
                x_low(i + 1, (r + 1) % RB)
                take_w1(i + 1, (r + 1) % RB)
            split_h(i, r)

        nc.vector.memset(loads_base[:, :], 0.0).then_inc(loads, 1)
        x_low(0, 0)
        take_w1(0, 0)
        run(dve, step)

    @block.gpsimd
    def _(pool):
        def step(i, r):
            pool.wait_ge(y_out, i + 1)
            after(pool, added, i * 16)
            pool.wait_ge(mark_set, i + 1)
            nc.gpsimd.tensor_tensor(wait_mark[:, 1:2], wait_mark[:, 0:1], wait_mark[:, 0:1], ALU.add).then_inc(mark_set, 1)
            pool.indirect_dma_start(out, bass.IndirectOffsetOnAxis(meta[:, r, 0:1].bitcast(U32), 0), y[:, r % 2, :], None,
                                    compute_op=ALU.add).then_inc(added, 16)

        nc.gpsimd.memset(wait_mark[:, :], 0.0).then_inc(mark_set, 1)
        run(pool, step)
        pool.wait_ge(added, 16 * NB)


def kernel(x, ctx_1024, g_xattn, g_ffn, L0_xattn_w_qs, L0_xattn_w_ks, L0_xattn_w_vs, L0_xattn_w_proj, L0_xattn_b_proj,
           L0_ffn_gate_w, L0_ffn_w1, L0_ffn_w2):
    import concourse.bacc as bacc
    from concourse.bass_utils import run_bass_kernel_spmd

    nc = bacc.Bacc("TRN2", target_bir_lowering=False, num_devices=1)
    given = dict(x=x, ctxt=ctx_1024, g_xattn=g_xattn, g_ffn=g_ffn, wq=L0_xattn_w_qs, wk=L0_xattn_w_ks, wv=L0_xattn_w_vs,
                 wproj=L0_xattn_w_proj, bproj=L0_xattn_b_proj, gate=L0_ffn_gate_w, w1=L0_ffn_w1, w2=L0_ffn_w2)
    arrays = {f"in_{n}": np.ascontiguousarray(a) for n, a in given.items()}
    inputs = {n: nc.dram_tensor(f"in_{n}", given[n].shape, F32, kind="ExternalInput").ap() for n in given}
    out = nc.dram_tensor("out", (T + P, D), F32, kind="ExternalOutput").ap()
    build(nc, out=out, **inputs)
    got = run_bass_kernel_spmd(nc, [arrays], core_ids=[0])
    return got.results[0]["out"][0:T].reshape(B, L, D)
```

```python
from contextlib import ExitStack

import numpy as np
import concourse.bass as bass
from concourse import mybir

F32 = mybir.dt.float32
F16 = mybir.dt.float16
U32 = mybir.dt.uint32
I32 = mybir.dt.int32
ACT = mybir.ActivationFunctionType
ALU = mybir.AluOpType
AX = mybir.AxisListType

P = 128
B, L, D = 4, 1024, 256
M, H, DK = 64, 16, 64
E, F = 8, 1024
T = B * L
KD = D // P
NP = H // 2
TG = 4
G = TG * P
NG = T // G
GB = L // G
NS = NG * NP
FC = F // P
EPS = 1e-5
WS = 64.0
PS = 64.0
REGION = T + P
ROW = D + 2
NB = (2 * T + E * (P - 1)) // P
EARLY = NG - 3
SAFE = (2 * EARLY * G - E * (P - 1) + P - 1) // P
SBUF_END = 229344
RB = 4
LEFT = 5
HELD = 1
BIG = 3.0e38
WN = 2 * KD * F
ROUTE = 17
LAST = 6
WC = 8


def after(eng, sem, count):
    if isinstance(count, int) and count <= 0:
        return
    eng.wait_ge(sem, count)


def build(nc, x, ctxt, g_xattn, g_ffn, wq, wk, wv, wproj, bproj, gate, w1, w2, out):
    dram = dict(
        x=x, ctxt=ctxt, g_xattn=g_xattn, g_ffn=g_ffn, wq=wq, wk=wk, wv=wv, wproj=wproj, bproj=bproj, gate=gate, w1=w1, w2=w2,
        out=out,
        records=nc.dram_tensor("records", (E * REGION + P, ROW), F32, kind="Internal").ap(),
        w_split=nc.dram_tensor("w_split", (E, P, 2, WN), F16, kind="Internal").ap(),
    )
    with ExitStack() as keep:
        def sb(name, shape, dt):
            return keep.enter_context(nc.sbuf_tensor(name, shape, dt))

        ident = sb("ident", [P, P], F32)
        table = sb("table", [1, 2 * NB], I32)
        loads_base = sb("loads_base", [1, 8], F32)
        weights = nc.alloc_sbuf_tensor_at("weights", [P, E, 2, WN], F16, offset=nc.sbuf_base)
        sb("weights_held", [P, HELD, 2, WN], F16)

        top = SBUF_END

        def carried(name, shape, dt):
            nonlocal top
            top -= -(-int(np.prod(shape[1:])) * (2 if dt == F16 else 4) // 32) * 32
            return nc.alloc_sbuf_tensor_at(name, shape, dt, offset=top)

        carry = Named()
        carry.ident, carry.table = ident, table
        carry.x1 = [carried(f"x1_{i}", [P, TG, D], F32) for i in ("even", "odd")]
        carry.rec = carried("rec_odd", [P, 2, TG, ROW], F32)
        carry.slot = carried("slot_odd", [P, 2, TG], U32)
        carry.rows = carried("rows", [P, RB, ROW], F32)
        carry.rows_in = [keep.enter_context(nc.semaphore(f"rows_in{r}")) for r in range(RB)]
        carry.pair_ps = keep.enter_context(nc.psum_tensor("pair_ps", [P, TG, D], F32))
        carry.gate_t = carried("gate_t", [P, KD, E], F32)
        carry.ones = carried("ones", [P, P], F16)
        carry.before = carried("before", [P, P], F16)
        carry.iota_e = carried("iota_e", [P, TG, E], F32)
        carry.e_off = carried("e_off", [P, TG, E], F32)
        carry.tok_ids = carried("tok_ids", [P, TG], F32)
        carry.minus_half = carried("minus_half", [P, TG], F32)
        carry.pad_rec = carried("pad_rec", [P, ROW], F32)
        carry.gains = carried("gains", [P, 2], F32)
        carry.seen = carried("seen", [P, E], F32)
        carry.seen_h = carried("seen_h", [P, E], F16)
        carry.wait_mark = carried("wait_mark", [P, 2], F32)
        carry.steps_128 = carried("steps_128", [1, E, T // P], F32)
        carry.upto = carried("upto", [1, E, E], F32)
        carry.block_no = carried("block_no", [1, max(SAFE, NB - SAFE), E], F32)
        carry.full = carried("full", [1, E], F32)
        carry.full_ends = carried("full_ends", [1, E], F32)
        with ExitStack() as stage_ctx:
            attention(nc, stage_ctx, dram, carry, weights)
            assert nc.sbuf_base <= top
        with ExitStack() as stage_ctx:
            experts(nc, stage_ctx, dram, carry, loads_base, weights)
            assert nc.sbuf_base <= top


class Named:
    pass


def over_e(a):
    return a.unsqueeze(2).broadcast_to([P, TG, E])


def routing_buffers(sb):
    r = Named()
    r.lg, r.lg2, r.cand, r.pos = (sb(n, [P, TG, E], F32) for n in ("lg", "lg2", "cand", "pos"))
    r.mask = sb("mask", [P, 2, TG, E], F32)
    r.mboth = sb("mboth", [P, TG, E], F16)
    r.mtiles = sb("mtiles", [P, E], F32)
    r.top, r.choice = (sb(n, [P, 2, TG], F32) for n in ("top", "choice"))
    r.delta, r.edelta, r.wsum, r.wfirst = (sb(n, [P, TG], F32) for n in ("delta", "edelta", "wsum", "wfirst"))
    return r


def routing_semaphores(sem):
    s = Named()
    s.lg_mm, s.lg_read, s.top_done, s.ed_done, s.m_done, s.pos_mm, s.pos_read, s.slots_done, s.route_ops = (sem(n) for n in (
        "lg_mm", "lg_read", "top_done", "ed_done", "m_done", "pos_mm", "pos_read", "slots_done", "route_ops"))
    return s


def logits_products(nc, job_ps, x2t, gate_t):
    for t in range(TG):
        for k in range(KD):
            last = nc.tensor.matmul(job_ps[:, t * E:(t + 1) * E], x2t[:, k, t * P:(t + 1) * P], gate_t[:, k, :],
                                    start=(k == 0), stop=(k == KD - 1))
    return last


def position_products(nc, job_ps, r, carry):
    for t in range(TG):
        o = job_ps[:, t * E:(t + 1) * E]
        nc.tensor.matmul(o, carry.ones[:, :], carry.seen_h[:, :], start=True, stop=False)
        for v in range(t):
            nc.tensor.matmul(o, carry.ones[:, :], r.mboth[:, v, :], start=False, stop=False)
        last = nc.tensor.matmul(o, carry.before[:, :], r.mboth[:, t, :], start=False, stop=True)
    return last


def choose(nc, dve, job_ps, r, s, carry, g, c):
    done = g * ROUTE + 6 * c

    def link(ins, i):
        ins.then_inc(s.route_ops, 1)
        dve.wait_ge(s.route_ops, done + i)

    if c == 0:
        dve.wait_ge(s.lg_mm, g + 1)
        nc.vector.tensor_copy(r.lg[:, :, :], job_ps[:, 0:TG * E].rearrange("p (t e) -> p t e", t=TG)).then_inc(s.lg_read, 1)
        dve.wait_ge(s.lg_read, g + 1)
    src = r.lg2 if c else r.lg
    link(nc.vector.tensor_reduce(r.top[:, c, :], src[:, :, :], AX.X, ALU.max), 1)
    link(nc.vector.tensor_tensor(r.cand[:, :, :], src[:, :, :], over_e(r.top[:, c, :]), ALU.is_lt), 2)
    link(nc.vector.scalar_tensor_tensor(r.cand[:, :, :], r.cand[:, :, :], float(E), carry.iota_e[:, :, :], ALU.mult, ALU.add), 3)
    link(nc.vector.tensor_reduce(r.choice[:, c, :], r.cand[:, :, :], AX.X, ALU.min), 4)
    link(nc.vector.tensor_tensor(r.mask[:, c], carry.iota_e[:, :, :], over_e(r.choice[:, c, :]), ALU.is_equal), 5)
    if c == 0:
        link(nc.vector.scalar_tensor_tensor(r.lg2[:, :, :], r.mask[:, 0], -BIG, r.lg[:, :, :], ALU.mult, ALU.add), 6)
    else:
        nc.vector.tensor_tensor(r.delta[:, :], r.top[:, 1, :], r.top[:, 0, :], ALU.subtract).then_inc(s.top_done, 1)
        nc.vector.tensor_tensor(r.mboth[:, :, :], r.mask[:, 0], r.mask[:, 1], ALU.add).then_inc(s.m_done, 1)


def place(nc, dve, job_ps, r, s, carry, g, slot, rec):
    done = g * ROUTE
    dve.wait_ge(s.pos_mm, g + 1)
    nc.vector.tensor_tensor(r.pos[:, :, :], job_ps[:, 0:TG * E].rearrange("p (t e) -> p t e", t=TG), carry.e_off[:, :, :],
                            ALU.add).then_inc(s.pos_read, 1)
    dve.wait_ge(s.ed_done, g + 1)
    nc.vector.tensor_scalar(r.wsum[:, :], r.edelta[:, :], 1.0, None, ALU.add).then_inc(s.route_ops, 1)
    nc.vector.tensor_reduce(r.mtiles[:, :], r.mboth[:, :, :].rearrange("p t e -> p e t"), AX.X, ALU.add).then_inc(s.route_ops, 1)
    dve.wait_ge(s.pos_read, g + 1)
    for c in range(2):
        nc.vector.tensor_tensor(r.mask[:, c], r.pos[:, :, :], r.mask[:, c], ALU.mult).then_inc(s.route_ops, 1)
    dve.wait_ge(s.route_ops, done + 13)
    nc.vector.reciprocal(r.wfirst[:, :], r.wsum[:, :]).then_inc(s.route_ops, 1)
    nc.vector.tensor_tensor(carry.seen[:, :], carry.seen[:, :], r.mtiles[:, :], ALU.add).then_inc(s.route_ops, 1)
    dve.wait_ge(s.route_ops, done + 15)
    with nc.allow_low_precision(reason="one term of each sum is not zero: a row number, exact in float32"):
        for c in range(2):
            nc.vector.tensor_reduce(slot[:, c, :], r.mask[:, c], AX.X, ALU.add)
    dve.wait_ge(s.route_ops, done + 17)
    nc.vector.tensor_copy(carry.seen_h[:, :], carry.seen[:, :])
    nc.vector.tensor_scalar(rec[:, 0, :, D + 1], r.wfirst[:, :], carry.gains[:, 1:2], None, ALU.mult)
    nc.vector.scalar_tensor_tensor(rec[:, 1, :, D + 1], r.wfirst[:, :], carry.gains[:, 1:2], r.edelta[:, :], ALU.mult, ALU.mult)
    for c in range(2):
        nc.vector.tensor_copy(rec[:, c, :, D].bitcast(U32), carry.tok_ids[:, :])
    nc.vector.tensor_scalar(carry.tok_ids[:, :], carry.tok_ids[:, :], float(G), None, ALU.add).then_inc(s.slots_done, 1)


def attention(nc, ctx, dram, carry, weights):
    ident = carry.ident
    gate_t, ones, before, iota_e, e_off, tok_ids, minus_half = (
        carry.gate_t, carry.ones, carry.before, carry.iota_e, carry.e_off, carry.tok_ids, carry.minus_half)
    pad_rec, gains, seen, seen_h, wait_mark = carry.pad_rec, carry.gains, carry.seen, carry.seen_h, carry.wait_mark
    x_groups = dram["x"].rearrange("b l d -> (b l) d").rearrange("(g p t) d -> g p t d", p=P, t=TG)
    out_groups = dram["out"][0:T, :].rearrange("(g p t) d -> g p t d", p=P, t=TG)
    records, w_split = dram["records"], dram["w_split"]

    def sb(name, shape, dt):
        return ctx.enter_context(nc.sbuf_tensor(name, shape, dt))

    def psum(name, shape):
        return ctx.enter_context(nc.psum_tensor(name, shape, F32))

    def sem(name):
        return ctx.enter_context(nc.semaphore(name))

    wq_h, wq_l = (sb(f"wq_{s}", [P, KD, H * DK], F16) for s in "hl")
    wp_h, wp_l = (sb(f"wp_{s}", [P, NP, D], F16) for s in "hl")
    kb_h, kb_l = (sb(f"kb_{s}", [P, B, NP, 2 * M], F16) for s in "hl")
    vb_h, vb_l = (sb(f"vb_{s}", [P, B, NP, 2, DK], F16) for s in "hl")
    bias_rows = sb("bias_rows", [1, 2, D], F16)
    tanhs = sb("tanhs", [P, 2], F32)

    stage = sb("stage", [P, WN], F32)
    split = sb("split", [P, 2, WN], F16)
    ctx_sb = sb("ctx_sb", [P, 2, D], F32)
    gate_sb = sb("gate_sb", [E, D], F32)
    bias_sb = sb("bias_sb", [1, D], F32)

    xin = sb("xin", [P, 2, TG, D], F32)
    xres = carry.x1
    stats = sb("stats", [P, 2, TG, 6], F32)
    mv = sb("mv", [P, 2, TG, 2], F32)
    vare = sb("vare", [P, 2, TG], F32)
    rstd = sb("rstd", [P, 2, TG], F32)
    shift = sb("shift", [P, 2, TG], F32)
    xn = sb("xn", [P, TG, D], F32)
    xt_h, xt_l = (sb(f"xt_{s}", [P, 2, KD, G], F16) for s in "hl")
    q32 = sb("q32", [P, NP, G], F32)
    q_h, q_l = (sb(f"q_{s}", [P, 2, G], F16) for s in "hl")
    smax = sb("smax", [P, 2, TG, 2], F32)
    ssub = sb("ssub", [P, 2, TG, 2, M], F32)
    ex = sb("ex", [P, 2, TG, 2 * M], F32)
    e_h, e_l = (sb(f"e_{s}", [P, 2, G], F16) for s in "hl")
    esum, rinv = (sb(n, [P, 2, TG, 2], F32) for n in ("esum", "rinv"))
    pn = sb("pn", [P, 2, TG, 2 * M], F32)
    r32 = sb("r32", [P, 2, G], F32)
    r_h, r_l = (sb(f"r_{s}", [P, 2, G], F16) for s in "hl")
    x2t = sb("x2t", [P, KD, G], F32)
    route = routing_buffers(sb)
    rec = [sb("rec_even", [P, 2, TG, ROW], F32), carry.rec]
    slot = [sb("slot_even", [P, 2, TG], U32), carry.slot]
    spare_slot = sb("spare_slot", [P, 1], U32)

    under = sb("under", [1, E, T // P], F32)
    cum = sb("cum", [1, E, E], F32)
    past = sb("past", [1, SAFE, E], F32)
    count1 = sb("count1", [1, E], F32)
    blk_e, blk_s = (sb(n, [1, SAFE], F32) for n in ("blk_e", "blk_s"))

    wq_sb = q32[:, 0:4, :].rearrange("p a g -> p (a g)")
    wp_sb = q32[:, 4:8, :].rearrange("p a g -> p (a g)").rearrange("p (c n) -> p c n", c=KD)
    ctx_t = x2t[:, :, :].rearrange("p k (b c m) -> p k b c m", b=B, c=2)
    wk_sb, wv_sb = (split[:, i, :].bitcast(F32) for i in range(2))
    wk_cols = rec[0][:, :, :, :].rearrange("p c t w -> p (c t w)")[:, 0:KD * H * DK].rearrange("p (k n) -> p k n", k=KD)

    q_ps = [psum(f"q_ps{i}", [P, G]) for i in range(2)]
    s_ps = psum("s_ps", [P, TG, 2, M])
    pt_ps = psum("pt_ps", [P, G])
    ot_ps = psum("ot_ps", [P, G])
    pj_ps = carry.pair_ps
    job_ps = psum("job_ps", [P, G])

    gain_in, gate_in, bias_in, ctx_in, wk_in, wv_in, wq_in, wp_in = (sem(n) for n in (
        "gain_in", "gate_in", "bias_in", "ctx_in", "wk_in", "wv_in", "wq_in", "wp_in"))
    stage_in = [sem(f"stage_in{i}") for i in range(2)]
    split_stored = [sem(f"split_stored{i}") for i in range(2)]
    x_in = [sem(f"x_in{i}") for i in range(2)]
    xres_in = [sem(f"xres_in{i}") for i in range(2)]
    records_in = [sem(f"records_in{i}") for i in range(2)]
    x1_stored = sem("x1_stored")
    base_set, consts_set, k_zeroed, v_zeroed, wk_laid, setup_ops, tanh_done = (sem(n) for n in (
        "base_set", "consts_set", "k_zeroed", "v_zeroed", "wk_laid", "setup_ops", "tanh_done"))
    ctx_tp, ctx_copied, gate_tp, gate_copied, wp_tp, wp_hi, wp_lo, wq_hi, wq_lo, bias_hi = (sem(n) for n in (
        "ctx_tp", "ctx_copied", "gate_tp", "gate_copied", "wp_tp", "wp_hi", "wp_lo", "wq_hi", "wq_lo", "bias_hi"))
    k_mm, k_hi, k_lo, v_mm, v_hi, v_lo = (sem(n) for n in ("k_mm", "k_hi", "k_lo", "v_mm", "v_hi", "v_lo"))
    ln1_ops, ln1_rstd, ln1_shift, xn_done, xt_tp, xt_hi, xt_lo = (sem(n) for n in ("ln1_ops", "ln1_rstd", "ln1_shift", "xn_done", "xt_tp", "xt_hi", "xt_lo"))
    q_mm, q_sb, q_hi, q_lo, s_mm, s_max, s_sub, e_x, pt_mm, e_hi, e_lo = (sem(n) for n in (
        "q_mm", "q_sb", "q_hi", "q_lo", "s_mm", "s_max", "s_sub", "e_x", "pt_mm", "e_hi", "e_lo"))
    e_sum, e_inv, p_nrm, ot_mm, r_mul, r_hi, r_lo, pj_mm = (sem(n) for n in (
        "e_sum", "e_inv", "p_nrm", "ot_mm", "r_mul", "r_hi", "r_lo", "pj_mm"))
    x1_done, ln2_ops, ln2_rstd, ln2_shift, ln2_done, rec_done, x2_tp, x2_copied = (sem(n) for n in (
        "x1_done", "ln2_ops", "ln2_rstd", "ln2_shift", "ln2_done", "rec_done", "x2_tp", "x2_copied"))
    routed = routing_semaphores(sem)
    split_hi, split_lo, table_ops = (sem(n) for n in ("split_hi", "split_lo", "table_ops"))

    CONSTS = 12

    def pair_no(g, p):
        return g * NP + p

    def known(g, least):
        return not isinstance(g, int) or g >= least

    def has_next(g):
        return not isinstance(g, int) or g < NG - 1

    def at(ap, i, pattern, **sizes):
        return ap[i] if isinstance(i, int) else ap[bass.ds(i, 1)].rearrange(pattern, **sizes)

    def pieces(g, p):
        if isinstance(g, int) and g == 0:
            return range(2 * (p - 4), 2 * (p - 4) + 2) if p >= 4 else ()
        return (p,)

    def d_chunk(a, k):
        return a.rearrange("p (n k) -> p k n", k=KD)[:, k]

    def rows_by_head(w):
        return w.rearrange("h (p k) j -> p h (k j)", k=KD)

    def by_head(w_sb):
        return w_sb.rearrange("p (h n) -> p h n", h=H)

    def w_chunk(w_sb, k, first, n):
        return w_sb.rearrange("p (h k j) -> p k h j", h=H, k=KD)[:, k, first:first + n, :]

    def heads_of(wq, k, half):
        return wq[:, k, half * H * DK // 2:(half + 1) * H * DK // 2].rearrange("p (h j) -> p h j", j=DK)

    block = ctx.enter_context(nc.Block())

    @block.sync
    def _(sp):
        sp.dma_start(xin[:, 0], x_groups[0]).then_inc(x_in[0], 16)
        sp.dma_start(ctx_sb[:, :, :], dram["ctxt"].rearrange("(c b) m d -> (b m) c d", b=2)).then_inc(ctx_in, 16)
        sp.dma_start(by_head(wq_sb), rows_by_head(dram["wq"])).then_inc(wq_in, 16)
        sp.dma_start(by_head(wk_sb), rows_by_head(dram["wk"])).then_inc(wk_in, 16)
        sp.dma_start(gate_sb[:, :], dram["gate"]).then_inc(gate_in, 16)
        sp.dma_start(bias_sb[:, :], dram["bproj"].rearrange("(o d) -> o d", o=1)).then_inc(bias_in, 16)
        sp.dma_start(wp_sb, dram["wproj"].rearrange("(c p) n -> p c n", p=P)).then_inc(wp_in, 16)
        sp.dma_start(by_head(wv_sb), rows_by_head(dram["wv"])).then_inc(wv_in, 16)
        sp.dma_start(tanhs[:, 0:1], dram["g_xattn"].partition_broadcast(P)).then_inc(gain_in, 16)
        sp.dma_start(tanhs[:, 1:2], dram["g_ffn"].partition_broadcast(P)).then_inc(gain_in, 16)
        sp.dma_start(xin[:, 1], x_groups[1]).then_inc(x_in[1], 16)

        def load_w1(e):
            after(sp, split_lo, WC * e - WC // 2)
            sp.dma_start(stage[:, 0:WN // 2].rearrange("p (k f) -> p k f", k=KD),
                         at(dram["w1"], e, "o d f -> (o d) f").rearrange("(k p) f -> p k f", p=P)).then_inc(stage_in[0], 16)

        def load_w2(e):
            after(sp, split_lo, WC * e)
            sp.dma_start(stage[:, WN // 2:WN].rearrange("p (c d) -> p c d", c=FC),
                         at(dram["w2"], e, "o f d -> (o f) d").rearrange("(c p) d -> p c d", p=P)).then_inc(stage_in[1], 16)

        def load_residual(g, par):
            if known(g, 2):
                sp.wait_ge(x1_stored, 16 * (g - 1))
                sp.wait_ge(rec_done, g - 1)
            sp.dma_start(xres[par][:, :, :], at(x_groups, g, "o p t d -> (o p) t d")).then_inc(xres_in[par], 16)

        def load_x(g, par):
            sp.wait_ge(xn_done, g - 1)
            sp.dma_start(xin[:, par], at(x_groups, g, "o p t d -> (o p) t d")).then_inc(x_in[par], 16)

        def store_x1(g, par):
            sp.wait_ge(x1_done, g + 1)
            sp.dma_start(at(out_groups, g, "o p t d -> (o p) t d"), xres[par][:, :, :]).then_inc(x1_stored, 16)

        def store_split(e, half):
            done = WC * e + (half + 1) * WC // 2
            sp.wait_ge(split_hi, done)
            sp.wait_ge(split_lo, done)
            c = slice(half * WN // 2, (half + 1) * WN // 2)
            sp.dma_start(at(w_split, e, "o p s n -> (o p) s n")[:, :, c], split[:, :, c]).then_inc(split_stored[half], 16)

        def group(g, par):
            load_residual(g, par)
            if not isinstance(g, int) or g + 2 < NG:
                load_x(g + 2, par)
            if known(g, 1):
                store_x1(g - 1, 1 - par)
            if known(g, HELD):
                store_split(g, 0)
            if has_next(g):
                load_w1(g + 1)
            if known(g, HELD):
                store_split(g, 1)
            if has_next(g):
                load_w2(g + 1)

        load_w1(0)
        load_w2(0)
        for k in range(GB):
            group(k, k)
        with sp.Fori(1, B - 1) as b:
            for k in range(GB):
                group(b * GB + k, k)
        for k in range(GB):
            group(NG - GB + k, k)
        sp.wait_ge(table_ops, 13)
        sp.wait_ge(records_in[0], 16 + 32 * TG * (B - 1))
        sp.wait_ge(records_in[1], 16 + 32 * TG * (B - 2))
        for i in range(RB):
            first = sp.value_load(carry.table[0:1, NB + i:NB + i + 1], min_val=0, max_val=E * REGION)
            sp.dma_start(carry.rows[:, i, :], records[bass.ds(first, P), :]).then_inc(carry.rows_in[i], 16)
        sp.wait_ge(x1_stored, 16 * (NG - 1))
        sp.wait_ge(xres_in[1], 16 * (NG // 2))
        for half in range(2):
            sp.wait_ge(split_stored[half], 16 * (NG - HELD))

    @block.tensor
    def _(pe):
        pe.wait_ge(consts_set, 1)

        def x_transpose(g, k, bank):
            pe.wait_ge(xn_done, g + 1)
            for t in range(TG):
                last = nc.tensor.transpose(bank[:, t * P:(t + 1) * P], d_chunk(xn[:, t, :], k), ident[:, :])
            last.then_inc(xt_tp, 1)

        pe.wait_ge(ctx_in, 16)
        for k in range(KD):
            for c in range(2):
                o = (k * 2 + c) * P
                last = nc.tensor.transpose(s_ps[:].rearrange("p t h m -> p (t h m)")[:, o:o + P],
                                           d_chunk(ctx_sb[:, c, :], k), ident[:, :])
        last.then_inc(ctx_tp, 1)
        for k in range(KD):
            x_transpose(0, k, q_ps[k])
        pe.wait_ge(gate_in, 16)
        for k in range(KD):
            last = nc.tensor.transpose(ot_ps[:, k * E:(k + 1) * E], gate_sb[:, k * P:(k + 1) * P], ident[0:E, 0:E])
        last.then_inc(gate_tp, 1)

        def transpose_wp(part):
            pe.wait_ge(wp_in, 16)
            pe.wait_ge(gate_copied, 1)
            after(pe, wp_lo, part)
            for j in range(2):
                for c in range(KD):
                    o = (part * 2 + j) * P
                    last = nc.tensor.transpose(ot_ps[:, j * D + c * P:j * D + (c + 1) * P], wp_sb[:, c, o:o + P], ident[:, :])
            last.then_inc(wp_tp, 1)

        def project_k(p):
            pe.wait_ge(ctx_copied, 2)
            pe.wait_ge(wk_laid, 1)
            after(pe, k_lo, p)
            if p == 6:
                pe.wait_ge(xt_lo, KD + 1)
            if p == 7:
                pe.wait_ge(xt_lo, 2 * KD)
            for k in range(KD):
                last = nc.tensor.matmul(job_ps[:, 0:B * M], wk_cols[:, k, p * P:(p + 1) * P], ctx_t[:, k, :, 0, :],
                                        start=(k == 0), stop=(k == KD - 1))
            last.then_inc(k_mm, 1)

        def project_v(b):
            pe.wait_ge(wv_in, 16)
            for half in range(2):
                after(pe, v_lo, 2 * b + half - 1)
                for k in range(KD):
                    last = nc.tensor.matmul(pj_ps[:, 2 * half:2 * half + 2, :].rearrange("p a d -> p (a d)"),
                                            ctx_t[:, k, b, :, :].rearrange("p c m -> p (c m)"),
                                            w_chunk(wv_sb, k, half * H // 2, H // 2), start=(k == 0), stop=(k == KD - 1))
                last.then_inc(v_mm, 1)

        def project_q(g, p, par):
            n = pair_no(g, p)
            after(pe, q_hi, n - 1)
            if p == 0:
                pe.wait_ge(xt_lo, 2 * g + 2)
            if isinstance(g, int) and g == 0 and p % 4 == 0:
                pe.wait_ge(wq_lo, p // 4 + 1)
            for i, (wt, xt) in enumerate(((wq_h, xt_h), (wq_h, xt_l), (wq_l, xt_h))):
                for k in range(KD):
                    last = nc.tensor.matmul(q_ps[p % 2][:, :], wt[:, k, p * P:(p + 1) * P], xt[:, par, k, :],
                                            start=(i == 0 and k == 0), stop=(i == 2 and k == KD - 1))
            last.then_inc(q_mm, 1)

        def scores(b, n, p):
            pe.wait_ge(q_lo, n + 1)
            if isinstance(n, int) and n < NP:
                pe.wait_ge(k_lo, n + 1)
            after(pe, s_sub, n)
            for t in range(TG):
                for i, (qt, kt) in enumerate(((q_h, kb_h), (q_h, kb_l), (q_l, kb_h))):
                    last = nc.tensor.matmul(s_ps[:, t].rearrange("p h m -> p (h m)"), qt[:, p % 2, t * P:(t + 1) * P],
                                            kt[:, b, p, :] if isinstance(b, int)
                                            else kt[:, bass.ds(b, 1), p, :].rearrange("p o m -> p (o m)"),
                                            start=(i == 0), stop=(i == 2))
            last.then_inc(s_mm, 1)

        def transpose_probs(n, p):
            pe.wait_ge(p_nrm, n + 1)
            after(pe, e_lo, n)
            for t in range(TG):
                last = nc.tensor.transpose(pt_ps[:, t * P:(t + 1) * P], pn[:, p % 2, t, :], ident[:, :])
            last.then_inc(pt_mm, 1)

        def probs_v(b, n, p):
            pe.wait_ge(e_hi, n + 1)
            if isinstance(n, int) and n == 0:
                pe.wait_ge(v_lo, 2)
                pe.wait_ge(wp_lo, 4)
            after(pe, r_mul, n)
            for i, (vt, et) in enumerate(((vb_h, e_h), (vb_l, e_h), (vb_h, e_l))):
                if i == 2:
                    pe.wait_ge(e_lo, n + 1)
                last = nc.tensor.matmul(ot_ps[:, :], vt[:, b, p].rearrange("p h w -> p (h w)") if isinstance(b, int)
                                        else vt[:, bass.ds(b, 1), p].rearrange("p o h w -> p (o h w)"),
                                        et[:, p % 2, :], start=(i == 0), stop=(i == 2))
            last.then_inc(ot_mm, 1)

        def project_out(g, n, p):
            pe.wait_ge(r_hi, n + 1)
            if isinstance(n, int) and n == 0:
                pe.wait_ge(v_lo, 2 * B)
                pe.wait_ge(bias_hi, 2)
                pe.wait_ge(consts_set, CONSTS)
            if p == 0:
                after(pe, x1_done, g)
            for t in range(TG):
                for i, wt in enumerate((wp_h, wp_l)):
                    nc.tensor.matmul(pj_ps[:, t, :], r_h[:, p % 2, t * P:(t + 1) * P], wt[:, p, :],
                                     start=(p == 0 and i == 0 and t % 2 == 0), stop=False, skip_group_check=True)
                if p == NP - 1:
                    for i in range(2):
                        nc.tensor.matmul(pj_ps[:, t, :], ones[0:1, :], bias_rows[0:1, i, :],
                                         start=False, stop=False, skip_group_check=True)
            pe.wait_ge(r_lo, n + 1)
            for t in range(TG):
                last = nc.tensor.matmul(pj_ps[:, t, :], r_l[:, p % 2, t * P:(t + 1) * P], wp_h[:, p, :],
                                        start=False, stop=(p == NP - 1), skip_group_check=True)
            last.then_inc(pj_mm, 1)

        def x2_transpose(g, par, k):
            pe.wait_ge(ln2_done, g + 1)
            for t in range(TG):
                last = nc.tensor.transpose(job_ps[:, t * P:(t + 1) * P], rec[par][:, 0, t, k * P:(k + 1) * P], ident[:, :])
            last.then_inc(x2_tp, 1)

        def logits(g):
            pe.wait_ge(x2_copied, 2 * g + 2)
            logits_products(nc, job_ps, x2t, gate_t).then_inc(routed.lg_mm, 1)

        def positions(g):
            pe.wait_ge(routed.m_done, g + 1)
            if isinstance(g, int) and g == EARLY:
                nc.tensor.matmul(job_ps[:, TG * E:(TG + 1) * E], ones[:, :], seen_h[:, :], start=True, stop=True)
            position_products(nc, job_ps, route, carry).then_inc(routed.pos_mm, 1)

        def small_job(g, k, p):
            if p == 1 and known(g, 2):
                x2_transpose(g - 2, k, 0)
            if p == 2 and known(g, 2):
                logits(g - 2)
            if p == 4 and known(g, 2):
                positions(g - 2)
            if p == 5 and has_next(g):
                if known(g, 2):
                    pe.wait_ge(routed.pos_read, g - 1)
                elif g == 0:
                    pe.wait_ge(k_lo, p + 1)
                x_transpose(g + 1, 0, job_ps)
            if p == 6 and has_next(g):
                pe.wait_ge(xt_lo, 2 * g + 3)
                if isinstance(g, int) and g == 0:
                    pe.wait_ge(k_lo, p + 1)
                x_transpose(g + 1, 1, job_ps)

        def step(b, g, k, p, pairs_back=LAST):
            n = pair_no(g, p)

            def back(lag):
                if p >= lag:
                    return b, g, p - lag
                return (b if k else b - 1), g - 1, p - lag + NP
            project_q(g, p, k)
            if isinstance(g, int) and g == 0:
                project_k(p)
            if pairs_back >= 1:
                scores(back(1)[0], n - 1, back(1)[2])
            if p == 2 and known(g, 2):
                pe.wait_ge(x2_copied, 2 * g - 3)
                x2_transpose(g - 2, k, 1)
            if pairs_back >= 4:
                transpose_probs(n - 4, back(4)[2])
            if isinstance(g, int) and g == 0 and p < 4:
                transpose_wp(p)
            if isinstance(g, int) and g == 0 and 1 <= p <= B:
                project_v(p - 1)
            if pairs_back >= 5:
                probs_v(back(5)[0], n - 5, back(5)[2])
            if pairs_back >= 6:
                project_out(back(6)[1], n - 6, back(6)[2])
            small_job(g, k, p)

        for k in range(GB):
            for p in range(NP):
                step(0, k, k, p, pairs_back=min(LAST, k * NP + p))
        with pe.Fori(1, B - 1) as b:
            for k in range(GB):
                for p in range(NP):
                    step(b, b * GB + k, k, p)
        for k in range(GB):
            for p in range(NP):
                step(B - 1, NG - GB + k, k, p)
        for p in range(LAST):
            n = NS + p
            if p < 1:
                scores(B - 1, n - 1, NP + p - 1)
            if p < 4:
                transpose_probs(n - 4, NP + p - 4)
            if p < 5:
                probs_v(B - 1, n - 5, NP + p - 5)
            project_out(NG - 1, n - 6, NP + p - 6)
    @block.scalar
    def _(act):
        act.wait_ge(consts_set, 1)
        nc.scalar.activation(esum[:, 0, 0, 0:1], ident[:, 0:1], ACT.Exp)

        def ln1_apply(g, par, tiles=range(TG)):
            if tiles[0] == 0:
                act.wait_ge(ln1_shift, g)
                after(act, xt_tp, 2 * g)
            for t in tiles:
                last = nc.scalar.activation(xn[:, t, :], xin[:, par, t, :], ACT.Identity, bias=shift[:, 0, t:t + 1], scale=rstd[:, 0, t:t + 1])
            if tiles[-1] == TG - 1:
                last.then_inc(xn_done, 1)

        def split_x(g, par, k, bank):
            act.wait_ge(xt_tp, 2 * g + k + 1)
            if known(g, 2):
                act.wait_ge(q_mm, pair_no(g - 2, NP))
            nc.scalar.copy(xt_h[:, par, k, :], bank[:, :]).then_inc(xt_hi, 1)

        def split_wq(half):
            for k in range(KD):
                last = nc.scalar.mul(heads_of(wq_h, k, half), w_chunk(wq_sb, k, half * H // 2, H // 2), WS)
            last.then_inc(wq_hi, 1)

        act.wait_ge(ctx_tp, 1)
        for c in range(2):
            nc.scalar.copy(ctx_t[:, :, :, c, :], s_ps[:].rearrange("p t h m -> p (t h m)").rearrange(
                "p (k b m) -> p k b m", k=KD, b=B)).then_inc(ctx_copied, 1)
        act.wait_ge(wq_in, 16)
        split_wq(0)
        for k in range(KD):
            split_x(0, 0, k, q_ps[k])
        split_wq(1)
        act.wait_ge(gate_tp, 1)
        nc.scalar.copy(gate_t[:, :, :], ot_ps[:, 0:KD * E].rearrange("p (k e) -> p k e", k=KD)).then_inc(gate_copied, 1)
        act.wait_ge(bias_in, 16)
        nc.scalar.mul(bias_rows[:, 0, :], bias_sb[:, :], WS).then_inc(bias_hi, 1)

        def split_k(p):
            act.wait_ge(k_mm, p + 1)
            if p == 0:
                act.wait_ge(k_zeroed, 2)
            for h in range(2):
                r = slice(h * M, (h + 1) * M)
                last = nc.scalar.copy(kb_h[r, :, p, r], job_ps[r, 0:B * M].rearrange("p (b m) -> p b m", b=B))
            last.then_inc(k_hi, 1)

        def split_v(b):
            if b == 0:
                act.wait_ge(v_zeroed, 2)
            for half in range(2):
                act.wait_ge(v_mm, 2 * b + half + 1)
                for h in range(2):
                    r = slice(h * M, (h + 1) * M)
                    last = nc.scalar.copy(vb_h[r, b, half * TG:half * TG + TG, h, :],
                                          pj_ps[r, 2 * half:2 * half + 2, :].rearrange("p a (q h j) -> p (a q) h j", q=2, h=2)[:, :, h, :])
                last.then_inc(v_hi, 1)

        def split_wp(part):
            act.wait_ge(wp_tp, part + 1)
            nc.scalar.mul(wp_h[:, 2 * part:2 * part + 2, :], ot_ps[:, :].rearrange("p (q d) -> p q d", q=2), WS).then_inc(wp_hi, 1)

        def copy_q(n, p):
            act.wait_ge(q_mm, n + 1)
            if isinstance(n, int) and n == 0:
                act.wait_ge(wq_lo, 2)
            if isinstance(n, int) and n == 4:
                act.wait_ge(wp_lo, 4)
            after(act, r_mul, n - NP + 1)
            nc.scalar.mul(q32[:, p, :], q_ps[p % 2][:, :], 1.0 / WS).then_inc(q_sb, 1)
            after(act, s_mm, n - 1)
            nc.scalar.mul(q_h[:, p % 2, :], q_ps[p % 2][:, :], 1.0 / WS).then_inc(q_hi, 1)

        def probs_hi(n, p):
            act.wait_ge(pt_mm, n + 1)
            after(act, ot_mm, n - 1)
            nc.scalar.mul(e_h[:, p % 2, :], pt_ps[:, :], PS).then_inc(e_hi, 1)

        def exps(n, p):
            act.wait_ge(s_sub, n + 1)
            after(act, p_nrm, n - 1)
            nc.scalar.activation(ex[:, p % 2].rearrange("p t m -> p (t m)"),
                                 ssub[:, p % 2].rearrange("p t h m -> p (t h m)"), ACT.Exp).then_inc(e_x, 1)

        def product_hi(n, p):
            act.wait_ge(r_mul, n + 1)
            after(act, pj_mm, n - 1)
            nc.scalar.copy(r_h[:, p % 2, :], r32[:, p % 2, :]).then_inc(r_hi, 1)

        def x2_copy(g, k):
            act.wait_ge(x2_tp, 2 * g + k + 1)
            if k == 0:
                after(act, routed.lg_mm, g)
            nc.scalar.copy(x2t[:, k, :], job_ps[:, :]).then_inc(x2_copied, 1)

        def exp_delta(g):
            act.wait_ge(routed.top_done, g + 1)
            nc.scalar.activation(route.edelta[:, :], route.delta[:, :], ACT.Exp).then_inc(routed.ed_done, 1)

        def ln2_apply(g, par, scattered, tiles=range(TG)):
            if tiles[0] == 0:
                act.wait_ge(ln2_shift, g + 1)
                after(act, records_in[par], scattered)
            for t in tiles:
                last = nc.scalar.activation(rec[par][:, 0, t, 0:D], xres[par][:, t, :], ACT.Identity,
                                            bias=shift[:, 1, t:t + 1], scale=rstd[:, 1, t:t + 1])
            if tiles[-1] == TG - 1:
                last.then_inc(ln2_done, 1)

        def second_record(g, par):
            act.wait_ge(ln2_done, g + 1)
            nc.scalar.copy(rec[par][:, 1, :, 0:D], rec[par][:, 0, :, 0:D]).then_inc(rec_done, 1)

        def expert_hi(e, i):
            half = 2 * i // WC
            act.wait_ge(stage_in[half], 16 * e + 16)
            if known(e, HELD + 1):
                act.wait_ge(split_stored[half], 16 * (e - HELD))
            c = slice(i * WN // WC, (i + 1) * WN // WC)
            dst = weights[:, e] if isinstance(e, int) and e < HELD else split
            nc.scalar.mul(dst[:, 0, c], stage[:, c], WS).then_inc(split_hi, 1)

        def step(b, g, k, p, pairs_back=LAST):
            n = pair_no(g, p)
            first = isinstance(g, int) and g == 0
            if p == 2 and known(g, 2):
                x2_copy(g - 2, 0)
            if p in (6, 7) and has_next(g):
                split_x(g + 1, 1 - k, p - 6, job_ps)
            copy_q(n, p)
            if first:
                split_k(p)
            if p == 2 and known(g, 2):
                x2_copy(g - 2, 1)
            if pairs_back >= 4:
                probs_hi(n - 4, (p - 4) % NP)
            if first and p < 4:
                split_wp(p)
            if first and 1 <= p <= B:
                split_v(p - 1)
            if pairs_back >= 2:
                exps(n - 2, (p - 2) % NP)
            if p == 0 and known(g, 2):
                ln2_apply(g - 2, k, 16 + 32 * TG * (b - 1), range(TG // 2))
            if p == 1 and known(g, 2):
                ln2_apply(g - 2, k, 0, range(TG // 2, TG))
            if p == 4 and has_next(g):
                ln1_apply(g + 1, 1 - k, range(TG // 2))
            if p == 5 and has_next(g):
                ln1_apply(g + 1, 1 - k, range(TG // 2, TG))
            for i in pieces(g, p):
                expert_hi(g, i)
            if pairs_back >= 5:
                product_hi(n - 5, (p - 5) % NP)
            if p == 2 and known(g, 2):
                second_record(g - 2, k)
            if p == 4 and known(g, 2):
                exp_delta(g - 2)

        for k in range(GB):
            for p in range(NP):
                step(0, k, k, p, pairs_back=min(LAST, k * NP + p))
            if k == 0:
                act.wait_ge(gain_in, 32)
                nc.scalar.activation(tanhs[:, :], tanhs[:, :], ACT.Tanh).then_inc(tanh_done, 1)
        with act.Fori(1, B - 1) as b:
            for k in range(GB):
                for p in range(NP):
                    step(b, b * GB + k, k, p)
        for k in range(GB):
            for p in range(NP):
                step(B - 1, NG - GB + k, k, p)
        for p in range(LAST):
            n = NS + p
            if p < 4:
                probs_hi(n - 4, NP + p - 4)
            if p < 2:
                exps(n - 2, NP + p - 2)
            if p < 5:
                product_hi(n - 5, NP + p - 5)
    @block.vector
    def _(dve):
        for i, t in enumerate((kb_h, kb_l)):
            nc.vector.memset(t[:].rearrange("p b n m -> p (b n m)").bitcast(U32), 0).then_inc(k_zeroed, 1)
        nc.vector.memset(seen[:, :], 0.0)
        nc.vector.memset(seen_h[:, :], 0.0)

        def ln1(g, par):
            dve.wait_ge(x_in[par], 16 * (g // 2) + 16 if isinstance(g, int) else g)
            for t in range(TG):
                last = nc.vector.bn_stats(stats[:, 0, t, :], xin[:, par, t, :])
            last.then_inc(ln1_ops, 1)

        def ln1_moments(g):
            dve.wait_ge(ln1_ops, 3 * g + 1)
            after(dve, xn_done, g)
            nc.vector.memset(vare[:, 0, :], EPS)
            for t in range(TG):
                last = nc.vector.bn_aggr(mv[:, 0, t, :], stats[:, 0, t, :])
            last.then_inc(ln1_ops, 1)
            dve.wait_ge(ln1_ops, 3 * g + 2)
            nc.vector.tensor_tensor(vare[:, 0, :], vare[:, 0, :], mv[:, 0, :, 1], ALU.add).then_inc(ln1_ops, 1)

        def ln1_shift_of(g):
            dve.wait_ge(ln1_rstd, g + 1)
            nc.vector.scalar_tensor_tensor(shift[:, 0, :], mv[:, 0, :, 0], -1.0, rstd[:, 0, :], ALU.mult, ALU.mult).then_inc(ln1_shift, 1)

        def split_x(g, par, k, bank):
            dve.wait_ge(xt_hi, 2 * g + k + 1)
            nc.vector.tensor_tensor(xt_l[:, par, k, :], bank[:, :], xt_h[:, par, k, :], ALU.subtract).then_inc(xt_lo, 1)

        def split_wq(half):
            dve.wait_ge(wq_hi, half + 1)
            for k in range(KD):
                last = nc.vector.scalar_tensor_tensor(heads_of(wq_l, k, half), w_chunk(wq_sb, k, half * H // 2, H // 2), WS,
                                                      heads_of(wq_h, k, half), ALU.mult, ALU.subtract)
            last.then_inc(wq_lo, 1)

        ln1(0, 0)
        ln1_moments(0)
        dve.wait_ge(ln1_rstd, 1)
        for t in range(TG):
            last = nc.vector.tensor_scalar(xn[:, t, :], xin[:, 0, t, :], mv[:, 0, t, 0:1], rstd[:, 0, t:t + 1], ALU.subtract, ALU.mult)
        last.then_inc(xn_done, 1)
        split_wq(0)
        for k in range(KD):
            split_x(0, 0, k, q_ps[k])
        split_wq(1)
        dve.wait_ge(wk_in, 16)
        for k in range(KD):
            last = nc.vector.tensor_copy(wk_cols[:, k].rearrange("p (h j) -> p h j", h=H), w_chunk(wk_sb, k, 0, H))
        last.then_inc(wk_laid, 1)
        dve.wait_ge(bias_hi, 1)
        nc.vector.scalar_tensor_tensor(bias_rows[:, 1, :], bias_sb[:, :], WS, bias_rows[:, 0, :],
                                       ALU.mult, ALU.subtract).then_inc(bias_hi, 1)

        def split_k(p):
            dve.wait_ge(k_hi, p + 1)
            for h in range(2):
                r = slice(h * M, (h + 1) * M)
                last = nc.vector.tensor_tensor(kb_l[r, :, p, r], job_ps[r, 0:B * M].rearrange("p (b m) -> p b m", b=B),
                                               kb_h[r, :, p, r], ALU.subtract)
            last.then_inc(k_lo, 1)

        def split_v(b):
            for half in range(2):
                dve.wait_ge(v_hi, 2 * b + half + 1)
                for h in range(2):
                    r = slice(h * M, (h + 1) * M)
                    c = slice(half * TG, half * TG + TG)
                    last = nc.vector.tensor_tensor(vb_l[r, b, c, h, :],
                                                   pj_ps[r, 2 * half:2 * half + 2, :].rearrange("p a (q h j) -> p (a q) h j", q=2, h=2)[:, :, h, :],
                                                   vb_h[r, b, c, h, :], ALU.subtract)
                last.then_inc(v_lo, 1)

        def split_wp(part):
            dve.wait_ge(wp_hi, part + 1)
            nc.vector.scalar_tensor_tensor(wp_l[:, 2 * part:2 * part + 2, :], ot_ps[:, :].rearrange("p (q d) -> p q d", q=2), WS,
                                           wp_h[:, 2 * part:2 * part + 2, :], ALU.mult, ALU.subtract).then_inc(wp_lo, 1)

        def score_max(n, p):
            dve.wait_ge(s_mm, n + 1)
            nc.vector.tensor_reduce(smax[:, p % 2], s_ps[:, :, :, :], AX.X, ALU.max).then_inc(s_max, 1)

        def score_sub(n, p):
            dve.wait_ge(s_max, n + 1)
            after(dve, e_x, n - 1)
            nc.vector.tensor_tensor(ssub[:, p % 2], s_ps[:, :, :, :],
                                    smax[:, p % 2].unsqueeze(3).broadcast_to([P, TG, 2, M]), ALU.subtract).then_inc(s_sub, 1)

        def exp_sum(n, p):
            dve.wait_ge(e_x, n + 1)
            nc.vector.tensor_reduce(esum[:, p % 2], ex[:, p % 2].rearrange("p t (h m) -> p t h m", h=2), AX.X, ALU.add).then_inc(e_sum, 1)
            dve.wait_ge(e_sum, n + 1)
            after(dve, p_nrm, n - 1)
            nc.vector.reciprocal(rinv[:, p % 2], esum[:, p % 2]).then_inc(e_inv, 1)

        def probs_lo(n, p):
            dve.wait_ge(e_hi, n + 1)
            nc.vector.scalar_tensor_tensor(e_l[:, p % 2, :], pt_ps[:, :], PS, e_h[:, p % 2, :], ALU.mult, ALU.subtract).then_inc(e_lo, 1)

        def times_q(n, p):
            dve.wait_ge(ot_mm, n + 1)
            dve.wait_ge(q_sb, n + 1)
            after(dve, r_lo, n - 1)
            nc.vector.scalar_tensor_tensor(r32[:, p % 2, :], ot_ps[:, :], 1.0 / PS, q32[:, p, :], ALU.mult, ALU.mult).then_inc(r_mul, 1)

        def residual(g, par):
            dve.wait_ge(pj_mm, pair_no(g, NP))
            dve.wait_ge(xres_in[par], 16 * (g // 2) + 16 if isinstance(g, int) else g)
            nc.vector.scalar_tensor_tensor(xres[par][:, :, :], pj_ps[:, :, :], gains[:, 0:1], xres[par][:, :, :],
                                           ALU.mult, ALU.add).then_inc(x1_done, 1)

        def ln2(g, par):
            dve.wait_ge(x1_done, g + 1)
            for t in range(TG):
                last = nc.vector.bn_stats(stats[:, 1, t, :], xres[par][:, t, :])
            last.then_inc(ln2_ops, 1)
            dve.wait_ge(ln2_ops, 3 * g + 1)
            nc.vector.memset(vare[:, 1, :], EPS)
            for t in range(TG):
                last = nc.vector.bn_aggr(mv[:, 1, t, :], stats[:, 1, t, :])
            last.then_inc(ln2_ops, 1)
            dve.wait_ge(ln2_ops, 3 * g + 2)
            nc.vector.tensor_tensor(vare[:, 1, :], vare[:, 1, :], mv[:, 1, :, 1], ALU.add).then_inc(ln2_ops, 1)

        def ln2_shift_of(g):
            dve.wait_ge(ln2_rstd, g + 1)
            nc.vector.scalar_tensor_tensor(shift[:, 1, :], mv[:, 1, :, 0], -1.0, rstd[:, 1, :], ALU.mult, ALU.mult).then_inc(ln2_shift, 1)

        def expert_lo(e, i):
            dve.wait_ge(split_hi, WC * e + i + 1)
            c = slice(i * WN // WC, (i + 1) * WN // WC)
            dst = weights[:, e] if isinstance(e, int) and e < HELD else split
            nc.vector.scalar_tensor_tensor(dst[:, 1, c], stage[:, c], WS, dst[:, 0, c], ALU.mult, ALU.subtract).then_inc(split_lo, 1)

        def early_table(part):
            def link(ins, i):
                ins.then_inc(table_ops, 1)
                dve.wait_ge(table_ops, i)

            if part == 0:
                dve.wait_ge(routed.pos_mm, EARLY + 1)
                link(nc.vector.tensor_copy(count1[:, :], job_ps[0:1, TG * E:(TG + 1) * E]), 1)
            if part == 1:
                link(nc.vector.scalar_tensor_tensor(under[:, :, :], carry.steps_128[:, :, :], float(P),
                                                    count1[:, :].unsqueeze(2).broadcast_to([1, E, T // P]), ALU.add, ALU.is_le), 2)
                link(nc.vector.tensor_reduce(carry.full[:, :], under[:, :, :], AX.X, ALU.add), 3)
                link(nc.vector.tensor_tensor(cum[:, :, :], carry.upto[:, :, :], carry.full[:, :].unsqueeze(1).broadcast_to([1, E, E]), ALU.mult), 4)
                link(nc.vector.tensor_reduce(carry.full_ends[:, :], cum[:, :, :], AX.X, ALU.add), 5)
            if part == 2:
                link(nc.vector.tensor_tensor(past[:, :, :], carry.block_no[:, 0:SAFE, :],
                                             carry.full_ends[:, :].unsqueeze(1).broadcast_to([1, SAFE, E]), ALU.is_ge), 6)
                link(nc.vector.tensor_reduce(blk_e[:, :], past[:, :, :], AX.X, ALU.add), 7)
                link(nc.vector.tensor_tensor(past[:, :, :], past[:, :, :], carry.full[:, :].unsqueeze(1).broadcast_to([1, SAFE, E]), ALU.mult), 8)
                link(nc.vector.tensor_reduce(blk_s[:, :], past[:, :, :], AX.X, ALU.add), 9)
            if part == 3:
                link(nc.vector.tensor_tensor(blk_s[:, :], carry.block_no[:, 0:SAFE, 0], blk_s[:, :], ALU.subtract), 10)
                link(nc.vector.tensor_scalar(blk_s[:, :], blk_s[:, :], float(P), None, ALU.mult), 11)
                nc.vector.scalar_tensor_tensor(carry.table[:, NB:NB + SAFE], blk_e[:, :], float(REGION), blk_s[:, :], ALU.mult, ALU.add).then_inc(table_ops, 1)
                nc.vector.tensor_copy(carry.table[:, 0:SAFE], blk_e[:, :]).then_inc(table_ops, 1)

        def step(b, g, k, p, pairs_back=LAST):
            n = pair_no(g, p)
            first = isinstance(g, int) and g == 0
            if p == 6 and known(g, 1):
                residual_of(b, g, k)
            if pairs_back >= 3:
                exp_sum(n - 3, (p - 3) % NP)
            if p == 4 and has_next(g):
                ln1_shift_of(g + 1)
            if p == 1 and has_next(g):
                ln1_of(b, g, k)
            if p == 2 and has_next(g):
                ln1_moments(g + 1)
            if p == 7 and known(g, 1) and has_next(g):
                ln2(g - 1, 1 - k)
            if p in (6, 7) and has_next(g):
                split_x(g + 1, 1 - k, p - 6, job_ps)
            if first:
                split_k(p)
            if p in (3, 4) and known(g, 2):
                choose(nc, dve, job_ps, route, routed, carry, g - 2, p - 3)
            if p == 5 and isinstance(g, int) and g - 2 == EARLY:
                early_table(0)
            if p == 5 and known(g, 2):
                place(nc, dve, job_ps, route, routed, carry, g - 2, slot[k], rec[k])
            if pairs_back >= 1:
                score_max(n - 1, (p - 1) % NP)
                score_sub(n - 1, (p - 1) % NP)
            if pairs_back >= 4:
                probs_lo(n - 4, (p - 4) % NP)
            if first and p < 4:
                split_wp(p)
            if first and 1 <= p <= B:
                split_v(p - 1)
            if pairs_back >= 5:
                times_q(n - 5, (p - 5) % NP)
            for i in pieces(g, p):
                expert_lo(g, i)
            if p == 7 and known(g, 1) and has_next(g):
                ln2_shift_of(g - 1)

        def ln1_of(b, g, k):
            if isinstance(b, int):
                ln1(g + 1, 1 - k)
                return
            par = 1 - k
            dve.wait_ge(x_in[par], (b + k) * 16 + 16)
            for t in range(TG):
                last = nc.vector.bn_stats(stats[:, 0, t, :], xin[:, par, t, :])
            last.then_inc(ln1_ops, 1)

        def residual_of(b, g, k):
            if isinstance(b, int):
                residual(g - 1, 1 - k)
                return
            par = 1 - k
            dve.wait_ge(pj_mm, pair_no(g - 1, NP))
            dve.wait_ge(xres_in[par], (b + k) * 16)
            nc.vector.scalar_tensor_tensor(xres[par][:, :, :], pj_ps[:, :, :], gains[:, 0:1], xres[par][:, :, :],
                                           ALU.mult, ALU.add).then_inc(x1_done, 1)

        for k in range(GB):
            for p in range(NP):
                step(0, k, k, p, pairs_back=min(LAST, k * NP + p))
            if k == 0:
                dve.wait_ge(tanh_done, 1)
                nc.vector.tensor_scalar(gains[:, :], tanhs[:, :], 1.0 / WS, None, ALU.mult).then_inc(setup_ops, 1)
                dve.wait_ge(setup_ops, 1)
        with dve.Fori(1, B - 1) as b:
            for k in range(GB):
                for p in range(NP):
                    step(b, b * GB + k, k, p)
        for k in range(GB):
            for p in range(NP):
                step(B - 1, NG - GB + k, k, p)
        for p in range(LAST):
            n = NS + p
            if p < 3:
                exp_sum(n - 3, NP + p - 3)
            if p < 1:
                score_max(n - 1, NP + p - 1)
                score_sub(n - 1, NP + p - 1)
            if p < 4:
                probs_lo(n - 4, NP + p - 4)
            if p < 5:
                times_q(n - 5, NP + p - 5)
            if 1 <= p <= 3:
                early_table(p)

    @block.gpsimd
    def _(pool):
        nc.gpsimd.memset(ident[:, :], 0.0).then_inc(base_set, 1)
        nc.gpsimd.memset(ones[:, :], 1.0).then_inc(base_set, 1)
        nc.gpsimd.memset(before[:, :], 1.0).then_inc(base_set, 1)
        nc.gpsimd.memset(carry.upto[:, :, :], 1.0).then_inc(base_set, 1)
        nc.gpsimd.memset(pad_rec[:, :], 0.0).then_inc(base_set, 1)
        pool.wait_ge(base_set, 5)
        nc.gpsimd.affine_select(out=ident[:, :], in_=ident[:, :], compare_op=ALU.not_equal, fill=1.0, base=0,
                                pattern=[[-1, P]], channel_multiplier=1).then_inc(consts_set, 1)
        nc.gpsimd.affine_select(out=before[:, :], in_=before[:, :], compare_op=ALU.is_gt, fill=0.0, base=0,
                                pattern=[[1, P]], channel_multiplier=-1).then_inc(consts_set, 1)
        nc.gpsimd.affine_select(out=carry.upto[:, :, :], in_=carry.upto[:, :, :], compare_op=ALU.is_ge, fill=0.0, base=0,
                                pattern=[[1, E], [-1, E]], channel_multiplier=0).then_inc(consts_set, 1)
        nc.gpsimd.memset(minus_half[:, :], -0.5).then_inc(consts_set, 1)

        def ln_rstd(i, g, ops, done):
            pool.wait_ge(ops, 3 * g + 3)
            nc.gpsimd.tensor_tensor(rstd[:, i, :], vare[:, i, :], minus_half[:, :], ALU.pow).then_inc(done, 1)

        def count_up(dst, pattern, channel):
            nc.gpsimd.iota(dst, pattern=pattern, base=0, channel_multiplier=channel,
                           allow_small_or_imprecise_dtypes=True).then_inc(consts_set, 1)

        pool.wait_ge(consts_set, 4)
        ln_rstd(0, 0, ln1_ops, ln1_rstd)
        for t in (vb_h, vb_l):
            nc.gpsimd.memset(t[:].rearrange("p b n h w -> p (b n h w)").bitcast(U32), 0).then_inc(v_zeroed, 1)
        nc.gpsimd.iota(pad_rec[:, D:D + 1].bitcast(U32), pattern=[[0, 1]], base=T, channel_multiplier=1).then_inc(consts_set, 1)
        nc.gpsimd.iota(spare_slot[:, :], pattern=[[0, 1]], base=E * REGION, channel_multiplier=1).then_inc(consts_set, 1)
        count_up(iota_e[:, :, :], [[0, TG], [1, E]], 0)
        count_up(e_off[:, :, :], [[0, TG], [REGION, E]], 0)
        count_up(tok_ids[:, :], [[1, TG]], TG)
        count_up(carry.steps_128[:, :, :], [[0, E], [P, T // P]], 0)
        count_up(carry.block_no[:, :, :], [[1, max(SAFE, NB - SAFE)], [0, E]], 0)
        nc.gpsimd.memset(wait_mark[:, :], 0.0).then_inc(consts_set, 1)

        def split_q(n, p):
            pool.wait_ge(q_hi, n + 1)
            nc.gpsimd.tensor_tensor(q_l[:, p % 2, :], q32[:, p, :], q_h[:, p % 2, :], ALU.subtract).then_inc(q_lo, 1)

        def normalize(n, p):
            pool.wait_ge(e_inv, n + 1)
            after(pool, pt_mm, n - 1)
            nc.gpsimd.tensor_tensor(pn[:, p % 2].rearrange("p t (h m) -> p t h m", h=2), ex[:, p % 2].rearrange("p t (h m) -> p t h m", h=2),
                                    rinv[:, p % 2].unsqueeze(3).broadcast_to([P, TG, 2, M]), ALU.mult).then_inc(p_nrm, 1)

        def product_lo(n, p):
            pool.wait_ge(r_hi, n + 1)
            nc.gpsimd.tensor_tensor(r_l[:, p % 2, :], r32[:, p % 2, :], r_h[:, p % 2, :], ALU.subtract).then_inc(r_lo, 1)

        def scatter(g, par, i):
            if i == 0:
                pool.wait_ge(routed.slots_done, g + 1)
                pool.wait_ge(rec_done, g + 1)
                nc.gpsimd.tensor_tensor(wait_mark[:, 1:2], wait_mark[:, 0:1], wait_mark[:, 0:1], ALU.add)
            c, t = i // TG, i % TG
            pool.indirect_dma_start(records, bass.IndirectOffsetOnAxis(slot[par][:, c, t:t + 1], 0),
                                    rec[par][:, c, t, :], None).then_inc(records_in[par], 16)

        def step(g, k, p, pairs_back=LAST):
            n = pair_no(g, p)
            if pairs_back >= 3:
                normalize(n - 3, (p - 3) % NP)
            split_q(n, p)
            if p == 3 and has_next(g):
                ln_rstd(0, g + 1, ln1_ops, ln1_rstd)
            if p == 7 and known(g, 1) and has_next(g):
                ln_rstd(1, g - 1, ln2_ops, ln2_rstd)
            if p >= 5 and known(g, 2):
                scatter(g - 2, k, p - 5)
            if p < 5 and known(g, 3):
                scatter(g - 3, 1 - k, p + 3)
            if pairs_back >= 5:
                product_lo(n - 5, (p - 5) % NP)

        for g in range(GB + 1):
            for p in range(NP):
                step(g, g % 2, p, pairs_back=min(LAST, g * NP + p))
                if g == 0 and p == 2:
                    pool.wait_ge(consts_set, CONSTS)
                    pool.indirect_dma_start(dram["out"], bass.IndirectOffsetOnAxis(pad_rec[:, D:D + 1].bitcast(U32), 0), pad_rec[:, 0:D],
                                            None).then_inc(records_in[0], 16)
                    pool.indirect_dma_start(records, bass.IndirectOffsetOnAxis(spare_slot[:, :], 0), pad_rec[:, :],
                                            None).then_inc(records_in[1], 16)
        with pool.Fori(1, B - 1) as b:
            for k in range(GB):
                for p in range(NP):
                    step(b * GB + 1 + k, (1 + k) % 2, p)
        for p in range(NP):
            step(NG - 1, 1, p)
        for p in range(LAST - 1):
            if p < 3:
                normalize(NS + p - 3, NP + p - 3)
            product_lo(NS + p - 5, NP + p - 5)
        pool.wait_ge(records_in[0], 16 + 32 * TG * (B - 1))
        pool.wait_ge(records_in[1], 16 + 32 * TG * (B - 2) + 16 * (2 * TG - LEFT))


def experts(nc, ctx, dram, carry, loads_base, weights):
    records, out = dram["records"], dram["out"]
    ident, table, rows, rows_in = carry.ident, carry.table, carry.rows, carry.rows_in
    x1_last_rows = dram["out"][0:T, :].rearrange("(g p t) d -> g p t d", p=P, t=TG)[NG - 1]

    def sb(name, shape, dt):
        return ctx.enter_context(nc.sbuf_tensor(name, shape, dt))

    def psum(name, shape):
        return ctx.enter_context(nc.psum_tensor(name, shape, F32))

    def sem(name):
        return ctx.enter_context(nc.semaphore(name))

    sb("weights_rest", [P, E - HELD, 2, WN], F16)
    meta = sb("meta", [P, RB, 2], F32)
    xt_h, xt_l = (sb(f"bx_{s}", [P, 2, KD, P], F16) for s in "hl")
    w1_now = sb("w1_now", [P, 2, 2, KD * F], F16)
    hid = sb("hid", [P, 2, FC, P], F32)
    ht_h, ht_l = (sb(f"ht_{s}", [P, 2, FC, P], F16) for s in "hl")
    y = sb("y", [P, 2, D], F32)
    wait_mark = carry.wait_mark

    stats = sb("last_stats", [P, TG, 6], F32)
    mv = sb("last_mv", [P, TG, 2], F32)
    vare, rstd, shift = (sb(f"last_{n}", [P, 2, TG], F32) for n in ("vare", "rstd", "shift"))
    x2t = sb("last_x2t", [P, KD, G], F32)
    route = routing_buffers(lambda name, shape, dt: sb(f"last_{name}", shape, dt))
    rec = [sb("last_rec", [P, 2, TG, ROW], F32), carry.rec]
    slot = [sb("last_slot", [P, 2, TG], U32), carry.slot]
    pad_first = sb("pad_first", [1, E], I32)
    LATE = NB - SAFE
    under = sb("late_under", [1, E, T // P], F32)
    cum = sb("late_cum", [1, E, E], F32)
    past, weighed = (sb(f"late_{n}", [1, LATE, E], F32) for n in ("past", "weighed"))
    count1, blocks, taken, left, ends, jump = (sb(f"late_{n}", [1, E], F32) for n in ("count", "blocks", "taken", "left", "ends", "jump"))
    blk_e, blk_s = (sb(f"late_blk_{n}", [1, LATE], F32) for n in "es")

    xt_ps = psum("bxt_ps", [P, 4, P])
    h_ps = [psum(f"h_ps{i}", [P, FC, P]) for i in range(2)]
    y_ps = [carry.pair_ps[:, 2 * i, :] for i in range(2)]
    job_ps = psum("last_job_ps", [P, G])

    mark_set = sem("mark_set")
    routed = routing_semaphores(lambda name: sem(f"last_{name}"))
    ln2_ops, ln2_rstd, ln2_shift, ln2_done, rec_done, x2_tp, x2_copied, pad_slots, table_ops = (sem(f"last_{n}") for n in (
        "ln2_ops", "ln2_rstd", "ln2_shift", "ln2_done", "rec_done", "x2_tp", "x2_copied", "pad_slots", "table_ops"))
    x1_done = sem("last_x1_done")
    x1_stored, carried_in, records_in, pads_in = (sem(f"last_{n}") for n in ("x1_stored", "carried_in", "records_in", "pads_in"))
    TABLE = 19
    loads = sem("weight_loads")
    xt_mm, x_hi, x_lo, meta_done, w1_ready, h_mm, h_act, h_hi, h_lo, y_mm, y_out, added = (sem(n) for n in (
        "xt_mm", "x_hi", "x_lo", "meta_done", "w1_ready", "h_mm", "h_act", "h_hi", "h_lo", "y_mm", "y_out", "added"))

    HEAD = 5 * RB
    BEHIND = 6
    TRIPS = (NB - HEAD - RB) // RB
    TAIL = HEAD + TRIPS * RB

    def run(eng, step, routing, everything_there):
        for i in range(HEAD):
            step(i, i % RB)
            for j in range(2):
                routing(j, i - 1 - j * BEHIND)
        everything_there()
        with eng.Fori(HEAD // RB, HEAD // RB + TRIPS) as trip:
            for r in range(RB):
                step(trip * RB + r, r)
        for i in range(TAIL, NB):
            step(i, i % RB)

    def there(i):
        return not isinstance(i, int) or i < NB

    def before_now(i):
        return not isinstance(i, int) or i >= 0

    def expert_of(eng, i):
        return eng.value_load(table[0:1, i:i + 1] if isinstance(i, int) else table[0:1, bass.ds(i, 1)], min_val=0, max_val=E - 1)

    def weights_at(e, s, start, n):
        return weights[:, bass.ds(e, 1), s, start:start + n]

    def block_loads(i, r):
        if isinstance(i, int):
            return 16 * (i // RB + 1)
        return (i - r) * (16 // RB) + 16

    block = ctx.enter_context(nc.Block())

    @block.sync
    def _(sp):
        sp.wait_ge(loads, 1)
        for e in range(HELD, E):
            sp.dma_start(weights[:, e], dram["w_split"][e]).then_inc(loads, 16)
            if e == HELD:
                sp.wait_ge(x1_done, 1)
                sp.dma_start(x1_last_rows, carry.x1[1][:, :, :]).then_inc(x1_stored, 16)
            sp.wait_ge(loads, 1 + 16 * (e - HELD + 1))
            if e == E - 3:
                sp.wait_ge(pad_slots, 1)
                for f in range(E):
                    first = sp.value_load(pad_first[0:1, f:f + 1], min_val=0, max_val=E * REGION)
                    sp.dma_start(records[bass.ds(first, P), :], carry.pad_rec[:, :]).then_inc(pads_in, 16)
        sp.wait_ge(x1_stored, 16)
        sp.wait_ge(pads_in, 16 * E)

    @block.tensor
    def _(pe):
        def transpose_x(i, r):
            pe.wait_ge(rows_in[r], block_loads(i, r))
            after(pe, x_lo, i)
            for k in range(KD):
                last = nc.tensor.transpose(xt_ps[:, k, :], rows[:, r, k * P:(k + 1) * P], ident[:, :])
            last.then_inc(xt_mm, 1)

        def hidden(i, r):
            pe.wait_ge(x_lo, i + 1)
            after(pe, h_act, i - 1)
            pe.wait_ge(w1_ready, i + 1)
            for c in range(FC):
                for j, (xt, s) in enumerate(((xt_h, 0), (xt_h, 1), (xt_l, 0))):
                    for k in range(KD):
                        last = nc.tensor.matmul(h_ps[r % 2][:, c, :], w1_now[:, r % 2, s, k * F + c * P:k * F + c * P + P],
                                                xt[:, r % 2, k, :],
                                                start=(j == 0 and k == 0), stop=(j == 2 and k == KD - 1))
            last.then_inc(h_mm, 1)

        def down(i, r, e):
            pe.wait_ge(h_lo, i + 1)
            after(pe, y_out, i - 1)
            if isinstance(i, int) and i == 0:
                pe.wait_ge(x1_done, 1)
            for c in range(FC):
                for j, (ht, s) in enumerate(((ht_h, 0), (ht_h, 1), (ht_l, 0))):
                    last = nc.tensor.matmul(y_ps[r % 2], ht[:, r % 2, c, :], weights_at(e, s, WN // 2 + c * D, D).rearrange("p o n -> p (o n)"),
                                            start=(c == 0 and j == 0), stop=(c == FC - 1 and j == 2))
            last.then_inc(y_mm, 1)

        def step(i, r):
            if there(i + 1):
                transpose_x(i + 1, (r + 1) % RB)
            hidden(i, r)
            if before_now(i - 1):
                down(i - 1, (r - 1) % RB, expert_of(pe, i - 1))

        def routing(j, i):
            if i in (2, 3):
                k = i - 2
                if k == 0:
                    pe.wait_ge(ln2_done, j + 1)
                    after(pe, routed.pos_read, j)
                else:
                    pe.wait_ge(x2_copied, 2 * j + 1)
                for t in range(TG):
                    last = nc.tensor.transpose(job_ps[:, t * P:(t + 1) * P], rec[j][:, 0, t, k * P:(k + 1) * P], ident[:, :])
                last.then_inc(x2_tp, 1)
            if i == 4:
                pe.wait_ge(x2_copied, KD * (j + 1))
                logits_products(nc, job_ps, x2t, carry.gate_t).then_inc(routed.lg_mm, 1)
            if i == 6:
                pe.wait_ge(routed.m_done, j + 1)
                if j == 1:
                    o = job_ps[:, TG * E:(TG + 1) * E]
                    nc.tensor.matmul(o, carry.ones[:, :], carry.seen_h[:, :], start=True, stop=False)
                    for t in range(TG):
                        nc.tensor.matmul(o, carry.ones[:, :], route.mboth[:, t, :], start=False, stop=(t == TG - 1))
                position_products(nc, job_ps, route, carry).then_inc(routed.pos_mm, 1)

        def everything_there():
            pe.wait_ge(table_ops, TABLE)

        transpose_x(0, 0)
        run(pe, step, routing, everything_there)
        down(NB - 1, (NB - 1) % RB, expert_of(pe, NB - 1))

    @block.scalar
    def _(act):
        def load_rows(i, r):
            first = act.value_load(table[0:1, NB + i:NB + i + 1] if isinstance(i, int) else table[0:1, bass.ds(i + NB, 1)],
                                   min_val=0, max_val=E * REGION)
            act.wait_ge(x_lo, i - RB + 1)
            act.wait_ge(meta_done, i - RB + 1)
            act.dma_start(rows[:, r, :], records[bass.ds(first, P), :]).then_inc(rows_in[r], 16)

        def x_high(i, r):
            act.wait_ge(xt_mm, i + 1)
            after(act, h_mm, i - 1)
            nc.scalar.copy(xt_h[:, r % 2], xt_ps[:, 0:KD, :]).then_inc(x_hi, 1)

        def silu(i, r):
            act.wait_ge(h_mm, i + 1)
            after(act, h_lo, i - 1)
            nc.scalar.activation(hid[:, r % 2], h_ps[r % 2][:, :, :], ACT.Silu, scale=1.0 / WS).then_inc(h_act, 1)

        def weigh(i, r):
            act.wait_ge(y_mm, i + 1)
            act.wait_ge(meta_done, i + 1)
            after(act, added, (i - 1) * 16)
            nc.scalar.mul(y[:, r % 2, :], y_ps[r % 2], meta[:, r, 1:2]).then_inc(y_out, 1)

        def step(i, r):
            if there(i + 1):
                x_high(i + 1, (r + 1) % RB)
            if there(i + RB):
                load_rows(i + RB, r)
            silu(i, r)
            if before_now(i - 1):
                weigh(i - 1, (r - 1) % RB)

        x_high(0, 0)
        nc.scalar.activation(route.edelta[:, 0:1], ident[:, 0:1], ACT.Silu)

        def routing(j, i):
            if i == 1:
                act.wait_ge(ln2_shift, j + 1)
                if j == 1:
                    act.wait_ge(carried_in, 16 * LEFT)
                for t in range(TG):
                    last = nc.scalar.activation(rec[j][:, 0, t, 0:D], carry.x1[j][:, t, :], ACT.Identity,
                                                bias=shift[:, j, t:t + 1], scale=rstd[:, j, t:t + 1])
                last.then_inc(ln2_done, 1)
            if i in (2, 3):
                act.wait_ge(x2_tp, KD * j + i - 1)
                if i == 2:
                    after(act, routed.lg_mm, j)
                nc.scalar.copy(x2t[:, i - 2, :], job_ps[:, :]).then_inc(x2_copied, 1)
            if i == 4:
                nc.scalar.copy(rec[j][:, 1, :, 0:D], rec[j][:, 0, :, 0:D]).then_inc(rec_done, 1)
            if i == 6:
                act.wait_ge(routed.top_done, j + 1)
                nc.scalar.activation(route.edelta[:, :], route.delta[:, :], ACT.Exp).then_inc(routed.ed_done, 1)

        def everything_there():
            act.wait_ge(table_ops, TABLE)
            act.wait_ge(carried_in, 16 * LEFT)
            act.wait_ge(records_in, 2 * 2 * TG * 16)
            act.wait_ge(pads_in, 16 * E)

        run(act, step, routing, everything_there)
        weigh(NB - 1, (NB - 1) % RB)

    @block.vector
    def _(dve):
        def x_low(i, r):
            dve.wait_ge(rows_in[r], block_loads(i, r))
            after(dve, added, (i - RB + 1) * 16)
            nc.vector.tensor_copy(meta[:, r, :], rows[:, r, D:D + 2]).then_inc(meta_done, 1)
            dve.wait_ge(x_hi, i + 1)
            nc.vector.tensor_tensor(xt_l[:, r % 2], xt_ps[:, 0:KD, :], xt_h[:, r % 2], ALU.subtract).then_inc(x_lo, 1)

        def take_w1(i, r, e=None):
            e = expert_of(dve, i) if e is None else e
            dve.wait_ge(loads, e * 16 + 1)
            after(dve, h_mm, i - 1)
            nc.vector.tensor_copy(w1_now[:, r % 2], weights[:, bass.ds(e, 1), :, 0:KD * F].rearrange("p o s n -> p (o s) n")).then_inc(w1_ready, 1)

        def split_h(i, r):
            dve.wait_ge(h_act, i + 1)
            after(dve, y_mm, i - 1)
            nc.vector.tensor_copy(ht_h[:, r % 2], hid[:, r % 2]).then_inc(h_hi, 1)
            dve.wait_ge(h_hi, i + 1)
            nc.vector.tensor_tensor(ht_l[:, r % 2], hid[:, r % 2], ht_h[:, r % 2], ALU.subtract).then_inc(h_lo, 1)

        def step(i, r):
            if there(i + 1):
                take_w1(i + 1, (r + 1) % RB)
                x_low(i + 1, (r + 1) % RB)
            split_h(i, r)

        nc.vector.memset(loads_base[:, :], 0.0).then_inc(loads, 1)
        first_expert = expert_of(dve, 0)
        x_low(0, 0)
        take_w1(0, 0, first_expert)
        nc.vector.scalar_tensor_tensor(carry.x1[1][:, :, :], carry.pair_ps[:, :, :], carry.gains[:, 0:1], carry.x1[1][:, :, :],
                                       ALU.mult, ALU.add).then_inc(x1_done, 1)

        def link(ins, i):
            ins.then_inc(table_ops, 1)
            dve.wait_ge(table_ops, i)

        def routing(j, i):
            if i == 0:
                if j == 1:
                    dve.wait_ge(x1_done, 1)
                for t in range(TG):
                    last = nc.vector.bn_stats(stats[:, t, :], carry.x1[j][:, t, :])
                last.then_inc(ln2_ops, 1)
                dve.wait_ge(ln2_ops, 3 * j + 1)
                nc.vector.memset(vare[:, j, :], EPS)
                for t in range(TG):
                    last = nc.vector.bn_aggr(mv[:, t, :], stats[:, t, :])
                last.then_inc(ln2_ops, 1)
                dve.wait_ge(ln2_ops, 3 * j + 2)
                nc.vector.tensor_tensor(vare[:, j, :], vare[:, j, :], mv[:, :, 1], ALU.add).then_inc(ln2_ops, 1)
            if i == 1:
                dve.wait_ge(ln2_rstd, j + 1)
                nc.vector.scalar_tensor_tensor(shift[:, j, :], mv[:, :, 0], -1.0, rstd[:, j, :], ALU.mult, ALU.mult).then_inc(ln2_shift, 1)
            if i in (4, 5):
                choose(nc, dve, job_ps, route, routed, carry, j, i - 4)
            if i == 7:
                if j == 1:
                    dve.wait_ge(routed.pos_mm, 2)
                    counts = job_ps[0:1, TG * E:(TG + 1) * E]
                    nc.vector.tensor_copy(count1[:, :], counts).then_inc(table_ops, 1)
                    nc.vector.tensor_tensor(pad_first[:, :], counts, carry.e_off[0:1, 0, :], ALU.add).then_inc(pad_slots, 1)
                    dve.wait_ge(carried_in, 16 * LEFT)
                place(nc, dve, job_ps, route, routed, carry, j, slot[j], rec[j])
            if j == 1 and i >= 8:
                late_table(i)

        def late_table(i):
            if i == 8:
                dve.wait_ge(table_ops, 1)
                link(nc.vector.tensor_tensor(under[:, :, :], carry.steps_128[:, :, :], count1[:, :].unsqueeze(2).broadcast_to([1, E, T // P]), ALU.is_lt), 2)
                link(nc.vector.tensor_reduce(blocks[:, :], under[:, :, :], AX.X, ALU.add), 3)
                link(nc.vector.tensor_tensor(taken[:, :], carry.full[:, :], carry.full_ends[:, :], ALU.subtract), 4)
                link(nc.vector.tensor_scalar(taken[:, :], taken[:, :], float(SAFE), 0.0, ALU.add, ALU.max), 5)
                link(nc.vector.tensor_tensor(taken[:, :], taken[:, :], carry.full[:, :], ALU.min), 6)
                link(nc.vector.tensor_tensor(left[:, :], blocks[:, :], taken[:, :], ALU.subtract), 7)
            if i == 9:
                link(nc.vector.tensor_tensor(cum[:, :, :], carry.upto[:, :, :], left[:, :].unsqueeze(1).broadcast_to([1, E, E]), ALU.mult), 8)
                link(nc.vector.tensor_reduce(ends[:, :], cum[:, :, :], AX.X, ALU.add), 9)
                link(nc.vector.tensor_copy(jump[:, :], blocks[:, :]), 10)
                link(nc.vector.tensor_tensor(jump[:, 0:E - 1], blocks[:, 0:E - 1], taken[:, 1:E], ALU.subtract), 11)
                link(nc.vector.tensor_tensor(past[:, :, :], carry.block_no[:, 0:LATE, :], ends[:, :].unsqueeze(1).broadcast_to([1, LATE, E]), ALU.is_ge), 12)
                link(nc.vector.tensor_reduce(blk_e[:, :], past[:, :, :], AX.X, ALU.add), 13)
            if i == 10:
                link(nc.vector.tensor_tensor(weighed[:, :, :], past[:, :, :], jump[:, :].unsqueeze(1).broadcast_to([1, LATE, E]), ALU.mult), 14)
                link(nc.vector.tensor_reduce(blk_s[:, :], weighed[:, :, :], AX.X, ALU.add), 15)
                link(nc.vector.scalar_tensor_tensor(blk_s[:, :], carry.block_no[:, 0:LATE, 0], taken[:, 0:1], blk_s[:, :], ALU.add, ALU.subtract), 16)
                link(nc.vector.tensor_scalar(blk_s[:, :], blk_s[:, :], float(P), None, ALU.mult), 17)
                link(nc.vector.scalar_tensor_tensor(blk_s[:, :], blk_e[:, :], float(REGION), blk_s[:, :], ALU.mult, ALU.add), 18)
                nc.vector.tensor_scalar(table[:, NB + SAFE:2 * NB], blk_s[:, :], float(E * REGION), None, ALU.min)
                nc.vector.tensor_scalar(table[:, SAFE:NB], blk_e[:, :], float(E - 1), None, ALU.min).then_inc(table_ops, 1)

        def everything_there():
            dve.wait_ge(table_ops, TABLE)

        run(dve, step, routing, everything_there)

    @block.gpsimd
    def _(pool):
        def step(i, r):
            pool.wait_ge(y_out, i + 1)
            after(pool, added, i * 16)
            pool.wait_ge(mark_set, i + 1)
            nc.gpsimd.tensor_tensor(wait_mark[:, 1:2], wait_mark[:, 0:1], wait_mark[:, 0:1], ALU.add).then_inc(mark_set, 1)
            pool.indirect_dma_start(out, bass.IndirectOffsetOnAxis(meta[:, r, 0:1].bitcast(U32), 0), y[:, r % 2, :], None,
                                    compute_op=ALU.add).then_inc(added, 16)

        def scatter(records_of, slots_of, n, landed):
            c, t = n // TG, n % TG
            pool.indirect_dma_start(records, bass.IndirectOffsetOnAxis(slots_of[:, c, t:t + 1], 0), records_of[:, c, t, :],
                                    None).then_inc(landed, 16)

        def ln2_rstd_of(j):
            pool.wait_ge(ln2_ops, 3 * j + 3)
            nc.gpsimd.tensor_tensor(rstd[:, j, :], vare[:, j, :], carry.minus_half[:, :], ALU.pow).then_inc(ln2_rstd, 1)

        def routing(j, i):
            if j == 1 and i == -2:
                ln2_rstd_of(1)
            if i in (7, 8, 9):
                if i == 7:
                    pool.wait_ge(routed.slots_done, j + 1)
                    pool.wait_ge(rec_done, j + 1)
                for n in range(3 * (i - 7), min(3 * (i - 6), 2 * TG)):
                    scatter(rec[j], slot[j], n, records_in)

        def everything_there():
            pool.wait_ge(x1_stored, 16)

        nc.gpsimd.memset(wait_mark[:, :], 0.0).then_inc(mark_set, 1)
        for n in range(2 * TG - LEFT, 2 * TG):
            scatter(carry.rec, carry.slot, n, carried_in)
        ln2_rstd_of(0)
        run(pool, step, routing, everything_there)
        pool.wait_ge(carried_in, 16 * LEFT)
        pool.wait_ge(records_in, 2 * 2 * TG * 16)
        pool.wait_ge(added, 16 * NB)


def kernel(x, ctx_1024, g_xattn, g_ffn, L0_xattn_w_qs, L0_xattn_w_ks, L0_xattn_w_vs, L0_xattn_w_proj, L0_xattn_b_proj,
           L0_ffn_gate_w, L0_ffn_w1, L0_ffn_w2):
    import concourse.bacc as bacc
    from concourse.bass_utils import run_bass_kernel_spmd

    nc = bacc.Bacc("TRN2", target_bir_lowering=False, num_devices=1)
    given = dict(x=x, ctxt=ctx_1024, g_xattn=g_xattn, g_ffn=g_ffn, wq=L0_xattn_w_qs, wk=L0_xattn_w_ks, wv=L0_xattn_w_vs,
                 wproj=L0_xattn_w_proj, bproj=L0_xattn_b_proj, gate=L0_ffn_gate_w, w1=L0_ffn_w1, w2=L0_ffn_w2)
    arrays = {f"in_{n}": np.ascontiguousarray(a) for n, a in given.items()}
    inputs = {n: nc.dram_tensor(f"in_{n}", given[n].shape, F32, kind="ExternalInput").ap() for n in given}
    out = nc.dram_tensor("out", (T + P, D), F32, kind="ExternalOutput").ap()
    build(nc, out=out, **inputs)
    got = run_bass_kernel_spmd(nc, [arrays], core_ids=[0])
    return got.results[0]["out"][0:T].reshape(B, L, D)
```
